# Optimizing a Trainium2 kernel written in Bass

```python
import numpy as np
import jax
import jax.numpy as jnp

def _softmax(x, axis=-1):
    return jax.nn.softmax(x, axis=axis)

def _gelu(x):
    return jax.nn.gelu(x, approximate=True)

def _silu(x):
    return jax.nn.silu(x)

def _sigmoid(x):
    return jax.nn.sigmoid(x)

def _layernorm(x, axis=-1, eps=1e-05):
    m = jnp.mean(x, axis=axis, keepdims=True)
    v = jnp.var(x, axis=axis, keepdims=True)
    return (x - m) / jnp.sqrt(v + eps)

def _scatter_add(tgt, idx, src, axis=0):
    return tgt.at[idx].add(src)

def _segment_sum(src, seg, n):
    return jax.ops.segment_sum(src, seg, n)
kernel_name = 'mk_gnn_preln_d2_gnn_r8_ed44cb'

def setup_inputs(seed: int=0):
    np.random.seed(seed)
    _w = jnp.asarray

    def _rec_inputs():
        import jax
        import jax.numpy as jnp
        _gk = jax.random.key(seed)
        x = -0.0001538 + 1 * jax.random.normal(jax.random.fold_in(_gk, 1), (1024, 768), jnp.float32)
        src = jax.random.randint(jax.random.fold_in(_gk, 2), (16384,), 0, 1024, jnp.int32)
        dst = jax.random.randint(jax.random.fold_in(_gk, 3), (16384,), 0, 1024, jnp.int32)
        _o = jnp.argsort(dst, stable=True)
        src = src[_o]
        dst = dst[_o]
        return (x, src, dst)
    x, src, dst = _rec_inputs()

    def _L0_gnn_setup():
        import jax, jax.numpy as jnp
        import numpy as np
        NEG_SLOPE = 0.2
        EPS = 1e-16
        N_NODES = 1024
        N_EDGES = 8192
        D_IN = 768
        D_HID = 768
        H1 = 8
        H2 = 1

        def gat_layer(x, W, a_s, a_d, b, edge_index, concat):
            n = x.shape[0]
            H, C = a_s.shape
            h = (x @ W).reshape(n, H, C)
            src, dst = (edge_index[0], edge_index[1])
            alpha_s = jnp.einsum('nhc,hc->nh', h, a_s)
            alpha_d = jnp.einsum('nhc,hc->nh', h, a_d)
            e = jax.nn.leaky_relu(alpha_s[src] + alpha_d[dst], NEG_SLOPE)
            m = jax.ops.segment_max(e, dst, num_segments=n)
            e = jnp.exp(e - m[dst])
            denom = jax.ops.segment_sum(e, dst, num_segments=n)
            alpha = e / (denom[dst] + EPS)
            msg = h[src] * alpha[:, :, None]
            out = jax.ops.segment_sum(msg, dst, num_segments=n)
            out = out.reshape(n, H * C) if concat else out.mean(axis=1)
            return out + b
        key = jax.random.key(seed)
        ks = jax.random.split(key, 10)
        x = jax.random.normal(ks[0], (N_NODES, D_IN), dtype=jnp.float32)
        edge_list = jax.random.randint(ks[1], (2, N_EDGES), 0, N_NODES, dtype=jnp.int32)
        s = 0.05
        W1 = jax.random.normal(ks[2], (D_IN, H1 * D_HID), dtype=jnp.float32) * s
        a_src1 = jax.random.normal(ks[3], (H1, D_HID), dtype=jnp.float32) * s
        a_dst1 = jax.random.normal(ks[4], (H1, D_HID), dtype=jnp.float32) * s
        b1 = jnp.zeros((H1 * D_HID,), dtype=jnp.float32)
        W2 = jax.random.normal(ks[5], (H1 * D_HID, H2 * D_HID), dtype=jnp.float32) * s
        a_src2 = jax.random.normal(ks[6], (H2, D_HID), dtype=jnp.float32) * s
        a_dst2 = jax.random.normal(ks[7], (H2, D_HID), dtype=jnp.float32) * s
        b2 = jnp.zeros((H2 * D_HID,), dtype=jnp.float32)
        return {'x': x, 'W1': W1, 'a_src1': a_src1, 'a_dst1': a_dst1, 'b1': b1, 'W2': W2, 'a_src2': a_src2, 'a_dst2': a_dst2, 'b2': b2, 'edge_list': edge_list}
    _L0_gnn_all = _L0_gnn_setup()
    _L0_gnn_in = {k: v for k, v in _L0_gnn_all.items() if k in ('W1', 'a_src1', 'a_dst1', 'b1', 'W2', 'a_src2', 'a_dst2', 'b2')}
    del _L0_gnn_all

    def _L1_gnn_setup():
        import jax, jax.numpy as jnp
        import numpy as np
        N_NODES = 1250
        key = jax.random.key(seed)
        k1, k2, k3 = jax.random.split(key, 3)
        x = jax.random.normal(k1, (N_NODES, 768), dtype=jnp.float32)
        edge_index = jax.random.randint(k2, (2, 12500), 0, N_NODES, dtype=jnp.int32)
        W = jax.random.normal(k3, (768, 768), dtype=jnp.float32) * (1.0 / np.sqrt(768))
        b = jnp.zeros((768,), dtype=jnp.float32)
        return {'x': x, 'edge_index': edge_index, 'W': W, 'b': b}
    _L1_gnn_all = _L1_gnn_setup()
    _L1_gnn_in = {k: v for k, v in _L1_gnn_all.items() if k in ('W', 'b')}
    del _L1_gnn_all
    return {'x': x, 'src': src, 'dst': dst, 'L0_gnn_W1': _L0_gnn_in['W1'], 'L0_gnn_a_src1': _L0_gnn_in['a_src1'], 'L0_gnn_a_dst1': _L0_gnn_in['a_dst1'], 'L0_gnn_b1': _L0_gnn_in['b1'], 'L0_gnn_W2': _L0_gnn_in['W2'], 'L0_gnn_a_src2': _L0_gnn_in['a_src2'], 'L0_gnn_a_dst2': _L0_gnn_in['a_dst2'], 'L0_gnn_b2': _L0_gnn_in['b2'], 'L1_gnn_W': _L1_gnn_in['W'], 'L1_gnn_b': _L1_gnn_in['b']}

def reference(x, src, dst, L0_gnn_W1, L0_gnn_a_src1, L0_gnn_a_dst1, L0_gnn_b1, L0_gnn_W2, L0_gnn_a_src2, L0_gnn_a_dst2, L0_gnn_b2, L1_gnn_W, L1_gnn_b):
    import jax
    import jax.numpy as jnp

    def _L0_gnn_ref(x, W1, a_src1, a_dst1, b1, W2, a_src2, a_dst2, b2, edge_list):
        import jax, jax.numpy as jnp
        import numpy as np
        NEG_SLOPE = 0.2
        EPS = 1e-16
        N_NODES = 1024
        N_EDGES = 8192
        D_IN = 768
        D_HID = 768
        H1 = 8
        H2 = 1

        def gat_layer(x, W, a_s, a_d, b, edge_index, concat):
            n = x.shape[0]
            H, C = a_s.shape
            h = (x @ W).reshape(n, H, C)
            src, dst = (edge_index[0], edge_index[1])
            alpha_s = jnp.einsum('nhc,hc->nh', h, a_s)
            alpha_d = jnp.einsum('nhc,hc->nh', h, a_d)
            e = jax.nn.leaky_relu(alpha_s[src] + alpha_d[dst], NEG_SLOPE)
            m = jax.ops.segment_max(e, dst, num_segments=n)
            e = jnp.exp(e - m[dst])
            denom = jax.ops.segment_sum(e, dst, num_segments=n)
            alpha = e / (denom[dst] + EPS)
            msg = h[src] * alpha[:, :, None]
            out = jax.ops.segment_sum(msg, dst, num_segments=n)
            out = out.reshape(n, H * C) if concat else out.mean(axis=1)
            return out + b
        h = gat_layer(x, W1, a_src1, a_dst1, b1, edge_list, concat=True)
        h = jax.nn.elu(h)
        out = gat_layer(h, W2, a_src2, a_dst2, b2, edge_list, concat=True)
        return out

    def _L1_gnn_ref(x, edge_index, W, b):
        import jax, jax.numpy as jnp
        import numpy as np
        N_NODES = 1250
        n = x.shape[0]
        loops = jnp.arange(n, dtype=edge_index.dtype)
        row = jnp.concatenate([edge_index[0], loops])
        col = jnp.concatenate([edge_index[1], loops])
        ones = jnp.ones(row.shape[0], dtype=x.dtype)
        deg = jax.ops.segment_sum(ones, col, num_segments=n)
        dinv = jnp.where(deg > 0, jax.lax.rsqrt(deg), 0.0)
        norm = dinv[row] * dinv[col]
        h = x @ W
        msg = h[row] * norm[:, None]
        out = jax.ops.segment_sum(msg, col, num_segments=n) + b
        return out
    edge_index = jnp.stack([src, dst])
    h = jnp.maximum(_layernorm(x, axis=-1), 0.0)
    x = x + _L0_gnn_ref(h, L0_gnn_W1, L0_gnn_a_src1, L0_gnn_a_dst1, L0_gnn_b1, L0_gnn_W2, L0_gnn_a_src2, L0_gnn_a_dst2, L0_gnn_b2, edge_index)
    h = jnp.maximum(_layernorm(x, axis=-1), 0.0)
    x = x + _L1_gnn_ref(h, edge_index, L1_gnn_W, L1_gnn_b)
    return x

_drawn_inputs = setup_inputs


def setup_inputs(seed=0):
    import zlib

    import numpy as np

    out = dict(_drawn_inputs(seed))
    spreads = {'L0_gnn_b1': (0.0, 0.1), 'L0_gnn_b2': (0.0, 0.1), 'L1_gnn_b': (0.0, 0.1)}
    factors = {'L0_gnn_a_dst2': 2.802}
    for name, (base, spread) in spreads.items():
        noise = np.random.default_rng([zlib.crc32(name.encode()), seed]).standard_normal(out[name].shape)
        drawn = base * np.exp(spread * noise) if base else spread * noise
        out[name] = jnp.asarray(drawn.astype(out[name].dtype))
    for name, factor in factors.items():
        out[name] = (out[name] * factor).astype(out[name].dtype)
    return out
```

```python
from contextlib import ExitStack

import concourse.bass as bass
from concourse import mybir

P = 128
F32 = mybir.dt.float32
F32R = mybir.dt.float32r
F16 = mybir.dt.float16
BF16 = mybir.dt.bfloat16
I32 = mybir.dt.int32
U16 = mybir.dt.uint16
ALU = mybir.AluOpType
ACT = mybir.ActivationFunctionType

SLOPE = 0.2
EPS_DEN = 1e-16
EPS_LN = 1e-5
FAR = -1e38
XS = 1024.0
DIGIT = 4096
START = 8


def f32(ap):
    return ap.bitcast(F32)


class Sems:

    def __init__(self, nc, ctx):
        self.nc, self.ctx = nc, ctx

    def __call__(self, name):
        return self.ctx.enter_context(self.nc.semaphore(name))


def startup(nc, env):
    x, src, dst, W1, a_s1, a_d1 = (env[k] for k in ("x", "src", "dst", "W1", "a_s1", "a_d1"))
    N, D = x.shape
    E = src.shape[0]
    H = a_s1.shape[0]
    NT, KT = N // P, D // P
    HALF = N // 2
    CH = E // P
    CG = CH // H
    RING = 4
    assert CG * P < DIGIT and H == NT and CG >= 2 * KT
    xh, xl, ct, lc, lc02, b1c = (env[k] for k in ("xh", "xl", "ct", "lc", "lc02", "b1c"))
    logit_rows, mask_dram = env["logit_rows"], env["mask_dram"]

    with ExitStack() as ctx:
        def sb(name, shape, dt):
            return ctx.enter_context(nc.sbuf_tensor(name, shape, dt))

        sem = Sems(nc, ctx)
        psum = ctx.enter_context(nc.psum_tensor("count_ps", [P, 8, 512], F32))
        edge_i = sb("edge_i", [P, 2, CH], I32)
        dst_low = sb("dst_low", [P, CH], I32)
        edge_f = sb("edge_f", [P, 3, CH], F32)
        iota = sb("iota", [P, N], F16)
        src_hot = sb("src_hot", [P, RING, N], F16)
        dst_hot = sb("dst_hot", [P, RING, HALF], F16)
        xt = sb("xt", [P, NT, D], F32)
        stats = sb("stats", [P, NT, 2, 6], F32)
        mv = sb("mv", [P, NT, 2], F32)
        root = sb("root", [P, 6, NT], F32)
        xT = sb("xT", [P, KT, N], F32)
        wv = sb("wv", [P, KT, D], F32)
        arow = sb("arow", [P, 2, D], F32)
        junk = sb("junk", [P, 2, D], BF16)
        vsum = sb("vsum", [P, 2 * KT], F32)
        V = sb("V", [P, KT, 2 * H], F32)
        packed = sb("packed", [P, 2, 512], F32)
        all_i = sb("all_i", [P, 2, 512], I32)
        high_i = sb("high_i", [P, 2, 512], I32)
        all_acc = sb("all_acc", [P, NT, 512], I32)
        high_acc = sb("high_acc", [P, NT, 512], I32)
        shifted = sb("shifted", [P, 2, 512], I32)
        near = sb("near", [P, NT, N], BF16)
        mask = sb("mask", [P, 2, N], BF16)
        ident = sb("ident", [P, P], F32)
        ident_b = sb("ident_b", [P, P], BF16)
        lg = sb("lg", [2 * H, N], F32)
        b1r = sb("b1_rows", [H * KT, P], F32)

        s_edges = sem("edges_loaded")
        s_x = sem("x_loaded")
        s_b1 = sem("b1_loaded")
        s_w = [sem(f"w_tile_loaded{k}") for k in range(KT)]
        s_a = sem("a_rows_loaded")
        s_turn = sem("loads_begun")
        s_iota = sem("iota_made")
        s_ident = sem("ident_made")
        s_prep = sem("edge_prep")
        s_ln = sem("ln_steps")
        s_root = sem("root_taken")
        s_hot = sem("one_hots_made")
        s_used = sem("one_hots_used")
        s_bank = sem("bank_filled")
        s_bfree = sem("bank_read")
        s_xn = sem("x_normed")
        s_xr = sem("x_scaled")
        s_xhi = sem("x_high")
        s_xlo = sem("x_low")
        s_v = sem("w_a_summed")
        s_vc = sem("w_a_kept")
        s_int = sem("counts_as_ints")
        s_aall = sem("all_added")
        s_ahigh = sem("high_added")
        s_acc0 = sem("acc_zeroed")
        s_shift = sem("high_shifted")
        s_low = sem("low_made")
        s_ct = sem("counts_kept")
        s_near = sem("near_made")
        s_xTp = sem("x_turned")
        s_xT = sem("xT_kept")
        s_lgp = sem("logits_ready")
        s_lg = sem("logits_kept")
        s_lcp = sem("logit_columns_ready")
        s_lc = sem("logit_columns_kept")
        s_mp = sem("mask_turned")
        s_mk = sem("mask_kept")
        s_mout = [sem(f"mask_tile_stored{n}") for n in range(2)]
        s_out = sem("logit_rows_stored")
        block = ctx.enter_context(nc.Block())

        W1v = W1.rearrange("(k p) (h c) -> p k h c", p=P, h=H)

        def keep_counts(b):
            dve = nc.vector
            dve.wait_ge(s_low, b + 1)
            dve.tensor_copy(ct[:, b, 0:HALF], shifted[:, b % 2, :]).then_inc(s_ct, 1)
            dve.tensor_copy(ct[:, b, HALF:N], high_acc[:, b, :]).then_inc(s_ct, 1)
            dve.wait_ge(s_ct, 2 * b + 2)
            dve.tensor_scalar(near[:, b, :], ct[:, b, :], 1.0, None, ALU.min).then_inc(s_near, 1)

        def to_ints(act, g, b):
            act.wait_ge(s_bfree, g * NT + (b + 1 + START))
            act.wait_ge(s_aall, g * NT + (b - 1 + START))
            act.activation(all_i[:, b % 2, :], packed[:, b % 2, :], ACT.Copy).then_inc(s_int, 1)
            act.wait_ge(s_ahigh, g * NT + (b - 1 + START))
            act.activation(high_i[:, b % 2, :], packed[:, b % 2, :], ACT.Copy, scale=1.0 / DIGIT,
                           bias=-(0.5 - 0.5 / DIGIT)).then_inc(s_int, 1)

        @block.sync
        def _(sp):
            sp.dma_start(edge_i[:, 0, :], src.rearrange("(p c) -> p c", p=P)).then_inc(s_edges, 16)
            sp.dma_start(edge_i[:, 1, :], dst.rearrange("(p c) -> p c", p=P)).then_inc(s_edges, 16)
            sp.dma_start(xt[:], x.rearrange("(t p) d -> p t d", p=P)).then_inc(s_x, 16)
            sp.dma_start(b1r[:], env["b1"].rearrange("(c p) -> c p", p=P)).then_inc(s_b1, 16)
            sp.sem_inc(s_a, START)
            for k in range(KT):
                sp.sem_inc(s_w[k], START)
            with sp.Fori(0, H) as g:
                sp.wait_ge(s_v, g * (2 * KT) + START)
                sp.sem_inc(s_turn, 1)
                sp.dma_start(arow[:, 0, :], a_s1[bass.ds(g, 1), :].to_broadcast([P, D])).then_inc(s_a, 16)
                sp.dma_start(arow[:, 1, :], a_d1[bass.ds(g, 1), :].to_broadcast([P, D])).then_inc(s_a, 16)
                for k in range(KT):
                    sp.dma_start(wv[:, k, :], W1v[:, k, bass.ds(g, 1), :]).then_inc(s_w[k], 16)
            sp.wait_ge(s_lg, 2)
            sp.dma_start(logit_rows, lg[0:H, :]).then_inc(s_out, 16)
            for t in range(NT):
                sp.wait_ge(s_mk, t + 1)
                sp.dma_start(mask_dram[t // 4, :, t % 4, :], mask[:, t % 2, :]).then_inc(s_mout[t % 2], 16)
            sp.wait_ge(s_out, 16)
            for n in range(2):
                sp.wait_ge(s_mout[n], 16 * len(range(n, NT, 2)))

        @block.gpsimd
        def _(pool):
            pool.iota(iota[:], pattern=[[1, N]], base=0, channel_multiplier=0,
                      allow_small_or_imprecise_dtypes=True).then_inc(s_iota, 1)
            pool.memset(ident[:], 0.0).then_inc(s_ident, 1)
            pool.wait_ge(s_ident, 1)
            pool.affine_select(out=ident[:], in_=ident[:], compare_op=ALU.not_equal, fill=1.0, base=0,
                               pattern=[[-1, P]], channel_multiplier=1).then_inc(s_ident, 1)
            pool.wait_ge(s_ident, 2)
            pool.tensor_copy(ident_b[:], ident[:]).then_inc(s_ident, 1)
            pool.memset(all_acc[:], 0).then_inc(s_acc0, 1)
            pool.memset(high_acc[:], 0).then_inc(s_acc0, 1)
            pool.wait_ge(s_acc0, 2)
            pool.sem_inc(s_aall, START)
            pool.sem_inc(s_ahigh, START)
            with pool.Fori(0, H) as g:
                for b in range(NT):
                    pool.wait_ge(s_int, g * (2 * NT) + (2 * b + 1 + START))
                    pool.wait_ge(s_aall, g * NT + (b + 1 - NT + START))
                    pool.tensor_tensor(all_acc[:, b, :], all_acc[:, b, :], all_i[:, b % 2, :],
                                       ALU.add).then_inc(s_aall, 1)
                    pool.wait_ge(s_int, g * (2 * NT) + (2 * b + 2 + START))
                    pool.wait_ge(s_ahigh, g * NT + (b + 1 - NT + START))
                    pool.tensor_tensor(high_acc[:, b, :], high_acc[:, b, :], high_i[:, b % 2, :],
                                       ALU.add).then_inc(s_ahigh, 1)
            for b in range(NT):
                pool.wait_ge(s_shift, b + 1)
                pool.tensor_tensor(shifted[:, b % 2, :], all_acc[:, b, :], shifted[:, b % 2, :],
                                   ALU.subtract).then_inc(s_low, 1)

        @block.vector
        def _(dve):
            dve.wait_ge(s_edges, 32)
            dve.tensor_copy(edge_f[:, 0, :], edge_i[:, 0, :]).then_inc(s_prep, 1)
            dve.tensor_scalar(dst_low[:], edge_i[:, 1, :], HALF - 1, None, ALU.bitwise_and).then_inc(s_prep, 1)
            dve.wait_ge(s_prep, 1)
            dve.tensor_scalar(edge_i[:, 0, :], edge_i[:, 1, :], HALF.bit_length() - 1, None,
                              ALU.logical_shift_right).then_inc(s_prep, 1)
            dve.wait_ge(s_prep, 3)
            dve.tensor_copy(edge_f[:, 1, :], dst_low[:]).then_inc(s_prep, 1)
            dve.tensor_scalar(edge_f[:, 2, :], edge_i[:, 0, :], float(DIGIT - 1), 1.0, ALU.mult,
                              ALU.add).then_inc(s_prep, 1)
            dve.wait_ge(s_x, 16)
            for t in range(NT):
                for c in range(2):
                    dve.bn_stats(stats[:, t, c, :], xt[:, t, c * (D // 2):(c + 1) * (D // 2)]).then_inc(s_ln, 1)
            for t in range(NT):
                dve.wait_ge(s_ln, 2 * t + 2)
                dve.bn_aggr(mv[:, t, :], stats[:, t, :, :].rearrange("p a b -> p (a b)")).then_inc(s_ln, 1)
            done = rstd_steps(dve, mv, root, s_ln, 3 * NT, s_root)
            dve.wait_ge(s_ln, done)

            dve.wait_ge(s_iota, 1)
            dve.wait_ge(s_prep, 5)
            for s in (s_hot, s_v, s_vc, s_xn, s_xr, s_xlo):
                dve.sem_inc(s, START)
            with dve.Fori(0, H) as g:
                c0 = dve.snap(g * CG)
                for j in range(CG):
                    if j == RING - 1:
                        dve.wait_ge(s_bank, g * NT + START)
                    else:
                        n = j + 1 - RING if j >= RING else j + 2 - RING
                        dve.wait_ge(s_used, g * (CG - 1) + (n + START))
                    dve.tensor_scalar(src_hot[:, j % RING, :], iota[:], edge_f[:, 0, bass.ds(c0 + j, 1)], None,
                                      ALU.is_equal).then_inc(s_hot, 1)
                    dve.tensor_scalar(dst_hot[:, j % RING, :], iota[:, 0:HALF], edge_f[:, 1, bass.ds(c0 + j, 1)],
                                      edge_f[:, 2, bass.ds(c0 + j, 1)], ALU.is_equal, ALU.mult).then_inc(s_hot, 1)
                    q = j - (CG - 2 * KT)
                    if q < 0:
                        continue
                    k, sd = q // 2, q % 2
                    if q == 0:
                        dve.wait_ge(s_a, g * 32 + (32 + START))
                        dve.wait_ge(s_vc, g + START)
                    dve.wait_ge(s_w[k], g * 16 + (16 + START))
                    dve.wait_ge(s_v, g * (2 * KT) + (q - 1 + START))
                    dve.tensor_tensor_reduce(junk[:, q % 2, :], wv[:, k, :], arow[:, sd, :], 1.0, 0.0,
                                             ALU.mult, ALU.add, vsum[:, q:q + 1]).then_inc(s_v, 1)
                dve.tensor_scalar(xt[:, bass.ds(g, 1), :], xt[:, bass.ds(g, 1), :], mv[:, bass.ds(g, 1), 0:1],
                                  root[:, 5, bass.ds(g, 1)], ALU.subtract, ALU.mult).then_inc(s_xn, 1)
                dve.wait_ge(s_v, g * (2 * KT) + (2 * KT + START))
                dve.tensor_copy(V[:, :, bass.ds(g, 1)], vsum[:].rearrange("p (k s) -> p k s", s=2)[:, :, 0:1])
                dve.tensor_copy(V[:, :, bass.ds(g + H, 1)],
                                vsum[:].rearrange("p (k s) -> p k s", s=2)[:, :, 1:2]).then_inc(s_vc, 1)
                dve.wait_ge(s_xn, g + (1 + START))
                dve.tensor_scalar(xt[:, bass.ds(g, 1), :], xt[:, bass.ds(g, 1), :], 0.0, XS, ALU.max,
                                  ALU.mult).then_inc(s_xr, 1)
                dve.wait_ge(s_xr, g + (1 + START))
                dve.wait_ge(s_xhi, g + (1 + START))
                dve.tensor_tensor(xl[:, bass.ds(g, 1), :], xt[:, bass.ds(g, 1), :], xh[:, bass.ds(g, 1), :],
                                  ALU.subtract).then_inc(s_xlo, 1)
            for b in range(NT):
                dve.wait_ge(s_ahigh, START + NT * (H - 1) + b + 1)
                if b >= 2:
                    dve.wait_ge(s_ct, 2 * (b - 2) + 1)
                dve.tensor_scalar(shifted[:, b % 2, :], high_acc[:, b, :], DIGIT.bit_length() - 1, None,
                                  ALU.logical_shift_left).then_inc(s_shift, 1)
                if b >= 1:
                    keep_counts(b - 1)
            keep_counts(NT - 1)

            for nh in range(2):
                dve.wait_ge(s_lgp, nh + 1)
                dve.tensor_scalar(lg[:, nh * 512:(nh + 1) * 512], psum[0:2 * H, 6 + nh, :], 1.0 / XS, None,
                                  ALU.mult).then_inc(s_lg, 1)
            dve.wait_ge(s_lcp, 1)
            dve.tensor_copy(b1c[:], psum[:, 6, P:P + H * KT])
            dve.tensor_copy(lc[:].rearrange("p t c -> p (t c)"), psum[:, 6, 0:NT * 2 * H]).then_inc(s_lc, 1)
            dve.wait_ge(s_lc, 1)
            dve.tensor_scalar(lc02[:].rearrange("p t c -> p (t c)"), lc[:].rearrange("p t c -> p (t c)"),
                              SLOPE, None, ALU.mult).then_inc(s_lc, 1)
            dve.wait_ge(s_lc, 2)

        @block.scalar
        def _(act):
            act.wait_ge(s_ln, 3 * NT + 1)
            act.activation(root[:, 1, :], root[:, 0, :], ACT.Sqrt).then_inc(s_root, 1)
            for s in (s_bfree, s_int, s_xhi):
                act.sem_inc(s, START)
            with act.Fori(0, H) as g:
                for b in range(NT):
                    act.wait_ge(s_bank, g * NT + (b + 1 + START))
                    act.wait_ge(s_int, g * (2 * NT) + (2 * b - 2 + START))
                    act.activation(packed[:, b % 2, :], psum[:, b, :], ACT.Copy).then_inc(s_bfree, 1)
                    if b >= 1:
                        to_ints(act, g, b - 1)
                to_ints(act, g, NT - 1)
                act.wait_ge(s_xn, g + (1 + START))
                act.wait_ge(s_xr, g + (1 + START))
                act.activation(xh[:, bass.ds(g, 1), :], xt[:, bass.ds(g, 1), :], ACT.Copy).then_inc(s_xhi, 1)
            for i in range(2 * KT):
                k, nh = i // 2, i % 2
                act.wait_ge(s_xTp, i + 1)
                act.activation(xT[:, k, nh * 512:(nh + 1) * 512], psum[:, i % 6, :], ACT.Copy).then_inc(s_xT, 1)
            for t in range(NT):
                act.wait_ge(s_mp, t + 1)
                if t >= 2:
                    act.wait_ge(s_mout[t % 2], 16 * (t // 2))
                act.activation(mask[:, t % 2, :], psum[:, t % 6, :].bitcast(BF16), ACT.Copy, scale=-FAR,
                               bias=FAR).then_inc(s_mk, 1)

        @block.tensor
        def _(pe):
            pe.sem_inc(s_used, START)
            pe.sem_inc(s_bank, START)
            with pe.Fori(0, H) as g:
                for j in range(CG):
                    pe.wait_ge(s_hot, g * (2 * CG) + (2 * j + 2 + START))
                    for b in range(NT):
                        if j == 0:
                            pe.wait_ge(s_bfree, g * NT + (b + 1 - NT + START))
                        mm = pe.matmul(psum[:, b, :], src_hot[:, j % RING, b * P:(b + 1) * P],
                                       dst_hot[:, j % RING, :], start=(j == 0), stop=(j == CG - 1))
                        if j == CG - 1:
                            mm.then_inc(s_bank, 1)
                    if j < CG - 1:
                        mm.then_inc(s_used, 1)
            pe.wait_ge(s_ident, 3)
            pe.wait_ge(s_xlo, H + START)
            pe.wait_ge(s_bfree, NT * H + START)
            for i in range(2 * KT):
                k, nh = i // 2, i % 2
                if i >= 6:
                    pe.wait_ge(s_xT, i - 5)
                for q in range(4):
                    mm = pe.transpose(psum[:, i % 6, q * P:(q + 1) * P], xt[:, 4 * nh + q, k * P:(k + 1) * P],
                                      ident[:])
                mm.then_inc(s_xTp, 1)
            pe.wait_ge(s_vc, H + START)
            for nh in range(2):
                for k in range(KT):
                    pe.wait_ge(s_xT, 2 * k + nh + 1)
                    mm = pe.matmul(psum[0:2 * H, 6 + nh, :], V[:, k, :], xT[:, k, nh * 512:(nh + 1) * 512],
                                   start=(k == 0), stop=(k == KT - 1))
                mm.then_inc(s_lgp, 1)
            pe.wait_ge(s_lg, 2)
            for t in range(NT):
                mm = pe.transpose(psum[:, 6, t * 2 * H:(t + 1) * 2 * H], lg[:, t * P:(t + 1) * P],
                                  ident[0:2 * H, 0:2 * H])
            pe.wait_ge(s_b1, 16)
            pe.transpose(psum[:, 6, P:P + H * KT], b1r[:], ident[0:H * KT, 0:H * KT]).then_inc(s_lcp, 1)
            pe.wait_ge(s_near, NT)
            pe.wait_ge(s_xT, 2 * KT)
            for t in range(NT):
                if t >= 6:
                    pe.wait_ge(s_mk, t - 5)
                turned = psum[:, t % 6, :].bitcast(BF16)
                for s in range(NT):
                    mm = pe.transpose(turned[:, s * P:(s + 1) * P], near[:, s, t * P:(t + 1) * P], ident_b[:])
                mm.then_inc(s_mp, 1)


def rstd_steps(dve, mv, root, s_ln, done, s_root, roots=1, cols=slice(None)):
    r = [root[:, i, cols] for i in range(6)]
    dve.wait_ge(s_ln, done)
    dve.tensor_scalar(r[0], mv[:, cols, 1:2].rearrange("p t o -> p (t o)"), EPS_LN, None, ALU.add).then_inc(s_ln, 1)
    dve.wait_ge(s_root, roots)
    dve.reciprocal(r[2], r[1]).then_inc(s_ln, 1)
    dve.wait_ge(s_ln, done + 2)
    dve.tensor_tensor(r[3], r[0], r[2], ALU.mult).then_inc(s_ln, 1)
    dve.wait_ge(s_ln, done + 3)
    dve.scalar_tensor_tensor(out=r[4], in0=r[1], scalar=1.0, in1=r[3], op0=ALU.mult, op1=ALU.add).then_inc(s_ln, 1)
    dve.wait_ge(s_ln, done + 4)
    dve.tensor_scalar(r[3], r[4], 0.5, None, ALU.mult).then_inc(s_ln, 1)
    dve.wait_ge(s_ln, done + 5)
    dve.reciprocal(r[5], r[3]).then_inc(s_ln, 1)
    return done + 6


def heads(nc, env):
    W1, W2, b1c = env["W1"], env["W2"], env["b1c"]
    xh, xl, ct, lc, lc02 = (env[k] for k in ("xh", "xl", "ct", "lc", "lc02"))
    logit_rows, mask_dram, ab_dram, h2_dram = (env[k] for k in ("logit_rows", "mask_dram", "ab_dram", "h2_dram"))
    D = W2.shape[1]
    H = W1.shape[1] // D
    N = ct.shape[2]
    NT, KT = N // P, D // P
    HALF = N // 2
    DT = HALF // P
    S = START

    with ExitStack() as ctx:
        def sb(name, shape, dt):
            return ctx.enter_context(nc.sbuf_tensor(name, shape, dt))

        sem = Sems(nc, ctx)
        h2ps = ctx.enter_context(nc.psum_tensor("h2ps", [P, 6, 512], F32))
        bank = [ctx.enter_context(nc.psum_tensor(f"bank{i}", [P, 512], F32)) for i in range(2)]
        ph = [sb(f"p_high{i}", [P, NT, HALF], F16) for i in range(2)]
        pl = [sb(f"p_low{i}", [P, NT, HALF], F16) for i in range(2)]
        zh = sb("z_high", [P, KT, HALF], F32R)
        zl = sb("z_low", [P, KT, HALF], F32R)
        w1r = sb("w1_raw", [P, 2, KT, P], F32)
        w1h = sb("w1_high", [P, 2, KT, P], F32R)
        w1l = sb("w1_low", [P, 2, KT, P], F32R)
        w2r = sb("w2_raw", [P, 2, D], F32)
        w2h = sb("w2_high", [P, 2, D], F32R)
        w2l = sb("w2_low", [P, 2, D], F32R)
        hh = sb("h_high", [P, 3, HALF], F32R)
        hl = sb("h_low", [P, 3, HALF], F32R)
        work = sb("work", [P, 6, HALF], F32)
        zt, ut, et = (work[:, 2 * i:2 * i + 2, :] for i in range(3))
        ab_rows = [sb(f"ab_rows{i}", [P, 2, HALF], F32) for i in range(2)]
        as_row = sb("as_row", [P, N], F32)
        mask = sb("mask_half", [P, DT, N], BF16)
        ta = sb("ta", [P, 2, HALF], F32)
        tb = sb("tb", [P, 2, HALF], F32)
        psums = sb("p_sums", [P, 2, HALF], F32)
        rden = sb("rden", [P, HALF], F32)
        den = sb("den", [P, HALF], F32)
        junk = sb("junk_m", [P, 2, N], BF16)
        top = sb("top", [P, 4, DT], F32)
        ab = [sb(f"ab{i}", [P, 2, DT], F32) for i in range(2)]
        b1u = [sb(f"b1u{i}", [P, KT], F32) for i in range(2)]
        ones = sb("ones", [P, P], F32)

        m_ones = sem("ones_made")
        m_mask = sem("mask_half_loaded")
        m_as = sem("as_row_loaded")
        m_top = sem("maxima_taken")
        m_sp = sem("sp_waits_over")
        m_small = sem("maxima_steps")
        m_turn = sem("maximum_begun")
        m_ab = sem("ab_columns_made")
        m_abs = sem("ab_columns_stored")
        m_abr = [sem(f"ab_rows_loaded{i}") for i in range(2)]
        m_b1 = sem("b1_columns_taken")
        m_terms = sem("exponent_terms_made")
        m_expo = sem("exponents_made")
        m_exp = sem("exponentials_made")
        m_p = sem("weights_made")
        m_ph = sem("weights_high")
        m_pl = sem("weights_low")
        m_sum = sem("weights_summed")
        m_den = sem("denominator_ready")
        m_deneps = sem("denominator_kept")
        m_rden = sem("denominator_inverted")
        m_z = sem("z_ready")
        m_zt = sem("z_scaled")
        m_zh = sem("z_high_done")
        m_zl = sem("z_low_done")
        m_w1 = [sem(f"w1_loaded{i}") for i in range(2)]
        m_w2 = [sem(f"w2_loaded{i}") for i in range(2)]
        m_w1h, m_w1l = sem("w1_high_done"), sem("w1_low_done")
        m_w2h, m_w2l = sem("w2_high_done"), sem("w2_low_done")
        m_h = sem("h_ready")
        m_u = sem("h_biased")
        m_neg = sem("h_negative_part")
        m_eexp = sem("h_exp")
        m_elu = sem("h_elu")
        m_hh = sem("h_high_done")
        m_hl = sem("h_low_done")
        m_o = sem("h2_added")
        m_keep = sem("h2_half_copied")
        m_zero = sem("h2_zeroed")
        m_store = sem("h2_half_stored")
        block = ctx.enter_context(nc.Block())

        W1v = W1.rearrange("(k p) (c j) -> p k c j", p=P, j=P)
        W2v = W2.rearrange("(c p) d -> p c d", p=P)


        def counter(eng, u0):
            cache = {}

            def at(j, per, n):
                if isinstance(u0, int):
                    return (u0 + j) * per + n + S
                if per not in cache:
                    cache[per] = eng.snap(u0 * per)
                return cache[per] + (j * per + n + S)
            return at

        def load_stats(sp, v):
            hv, fv = (sp.snap(n) if not isinstance(v, int) else n for n in (v % H, (v // H) % 2))
            sp.wait_ge(m_top, v * DT + S)
            sp.sem_inc(m_sp, 1)
            sp.dma_start(as_row[:], logit_rows[bass.ds(hv, 1), :].to_broadcast([P, N])).then_inc(m_as, 16)
            sp.dma_start(mask[:], mask_dram[bass.ds(fv, 1), :, :, :]).then_inc(m_mask, 16)

        def spread(sp, v, par):
            sp.wait_ge(m_ab, v + (1 + S))
            sp.sem_inc(m_sp, 1)
            sp.wait_ge(m_terms, v * NT + (S - NT))
            sp.sem_inc(m_sp, 1)
            sp.dma_start(ab_dram[par].rearrange("a (t p) -> p a t", p=P), ab[par][:],
                         allow_slow_non_contiguous=True).then_inc(m_abs, 16)
            sp.wait_ge(m_abs, v * 16 + (16 + S))
            sp.sem_inc(m_sp, 1)
            sp.dma_start(ab_rows[par][:], ab_dram[par].partition_broadcast(P)).then_inc(m_abr[par], 16)

        def maxima(dve, v, par):
            hv, tv = (dve.snap(n) if not isinstance(v, int) else n for n in (v % H, ((v // H) % 2) * DT))
            dve.wait_ge(m_as, v * 16 + (16 + S))
            dve.wait_ge(m_mask, v * 16 + (16 + S))
            dve.wait_ge(m_ab, v + S)
            for t in range(DT):
                dve.wait_ge(m_top, v * DT + (t - 1 + S))
                dve.sem_inc(m_turn, 1)
                dve.tensor_tensor_reduce(junk[:, t % 2, :], mask[:, t, :], as_row[:], 1.0, FAR, ALU.add,
                                         ALU.max, top[:, 0, t:t + 1]).then_inc(m_top, 1)
            ad = lc[:, bass.ds(tv, DT), bass.ds(hv + H, 1)].rearrange("p t o -> p (t o)")
            dve.wait_ge(m_top, v * DT + (DT + S))
            dve.tensor_tensor(top[:, 1, :], top[:, 0, :], ad, ALU.add).then_inc(m_small, 1)
            dve.wait_ge(m_small, v * 2 + (1 + S))
            dve.scalar_tensor_tensor(out=top[:, 2, :], in0=top[:, 1, :], scalar=SLOPE, in1=top[:, 1, :],
                                     op0=ALU.mult, op1=ALU.max).then_inc(m_small, 1)
            dve.wait_ge(m_small, v * 2 + (2 + S))
            dve.wait_ge(m_abs, v * 16 + S)
            dve.tensor_tensor(ab[par][:, 0, :], ad, top[:, 2, :], ALU.subtract)
            dve.scalar_tensor_tensor(out=ab[par][:, 1, :], in0=ad, scalar=SLOPE, in1=top[:, 2, :],
                                     op0=ALU.mult, op1=ALU.subtract).then_inc(m_ab, 1)

        def exponent_terms(dve, at, j, s, par, hv):
            if s == 0:
                dve.wait_ge(m_abr[par], at(j, 8, 8 if par else 16))
            dve.wait_ge(m_p, at(j, NT, s - 1))
            dve.tensor_scalar(ta[:, s % 2, :], ab_rows[par][:, 0, :], lc[:, s, bass.ds(hv, 1)], 0.0, ALU.add,
                              ALU.min)
            dve.wait_ge(m_pl, at(j, NT, s - 1))
            dve.wait_ge(m_sum, at(j, NT, s - 1))
            dve.tensor_scalar(tb[:, s % 2, :], ab_rows[par][:, 1, :], lc02[:, s, bass.ds(hv, 1)], 0.0, ALU.add,
                              ALU.min).then_inc(m_terms, 1)

        def exponent(dve, at, j, s):
            dve.wait_ge(m_terms, at(j, NT, s + 1))
            dve.tensor_tensor(ta[:, s % 2, :], ta[:, s % 2, :], tb[:, s % 2, :], ALU.max).then_inc(m_expo, 1)

        def weights(dve, at, j, s, tv):
            dve.wait_ge(m_exp, at(j, NT, s + 1))
            dve.tensor_tensor(tb[:, s % 2, :], ta[:, s % 2, :], ct[:, s, bass.ds(tv, HALF)],
                              ALU.mult).then_inc(m_p, 1)

        def weights_low(dve, at, j, s, par):
            dve.wait_ge(m_ph, at(j, NT, s + 1))
            dve.tensor_tensor(pl[par][:, s, :], tb[:, s % 2, :], ph[par][:, s, :], ALU.subtract).then_inc(m_pl, 1)

        def z_scaled(dve, at, j, k):
            dve.wait_ge(m_z, at(j, KT, k + 1))
            if k < 2:
                dve.wait_ge(m_zl, at(j, KT, 0))
                dve.wait_ge(m_rden, at(j, 1, 1))
            else:
                dve.wait_ge(m_zl, at(j, KT, k - 1))
            dve.tensor_tensor(zt[:, k % 2, :], bank[(k + 1) % 2][:], rden[:], ALU.mult).then_inc(m_zt, 1)

        def z_low(dve, at, j, k):
            dve.wait_ge(m_zh, at(j, KT, k + 1))
            dve.tensor_tensor(zl[:, k, :], zt[:, k % 2, :], f32(zh[:, k, :]), ALU.subtract).then_inc(m_zl, 1)

        def w1_low(dve, at, j, i):
            dve.wait_ge(m_w1h, at(j, KT, i + 1))
            dve.tensor_tensor(w1l[:, i % 2, :, :], w1r[:, i % 2, :, :], f32(w1h[:, i % 2, :, :]),
                              ALU.subtract).then_inc(m_w1l, 1)

        def w2_low(dve, at, j, i):
            dve.wait_ge(m_w2h, at(j, KT, i + 1))
            dve.tensor_tensor(w2l[:, i % 2, :], w2r[:, i % 2, :], f32(w2h[:, i % 2, :]),
                              ALU.subtract).then_inc(m_w2l, 1)

        def h_negative(dve, at, j, i):
            dve.wait_ge(m_u, at(j, KT, i + 1))
            dve.wait_ge(m_hl, at(j, KT, i - 1))
            dve.tensor_scalar(et[:, i % 2, :], ut[:, i % 2, :], 0.0, None, ALU.min).then_inc(m_neg, 1)

        def h_elu(dve, at, j, i):
            dve.wait_ge(m_eexp, at(j, KT, i + 1))
            dve.scalar_tensor_tensor(out=et[:, i % 2, :], in0=et[:, i % 2, :], scalar=-1.0, in1=ut[:, i % 2, :],
                                     op0=ALU.add, op1=ALU.max).then_inc(m_elu, 1)

        def h_low(dve, at, j, i):
            dve.wait_ge(m_hh, at(j, KT, i + 1))
            dve.tensor_tensor(hl[:, i % 3, :], et[:, i % 2, :], f32(hh[:, i % 3, :]), ALU.subtract).then_inc(m_hl, 1)

        def exponential(act, at, j, s):
            act.wait_ge(m_expo, at(j, NT, s + 1))
            act.activation(ta[:, s % 2, :], ta[:, s % 2, :], ACT.Exp).then_inc(m_exp, 1)

        def weights_high(act, at, j, s, par):
            act.wait_ge(m_p, at(j, NT, s + 1))
            if s == 0:
                act.wait_ge(m_z, at(j, KT, -KT))
            act.activation(ph[par][:, s, :], tb[:, s % 2, :], ACT.Copy).then_inc(m_ph, 1)

        def z_high(act, at, j, k):
            act.wait_ge(m_zt, at(j, KT, k + 1))
            if k == 0:
                act.wait_ge(m_h, at(j, KT, 0))
            act.activation(zh[:, k, :], zt[:, k % 2, :], ACT.Copy).then_inc(m_zh, 1)

        def w1_high(act, at, j, i):
            act.wait_ge(m_w1[i % 2], at(j, 8 * KT, 16 * (i // 2 + 1)))
            act.wait_ge(m_h, at(j, KT, i - 1))
            act.activation(w1h[:, i % 2, :, :], w1r[:, i % 2, :, :], ACT.Copy).then_inc(m_w1h, 1)

        def w2_high(act, at, j, i):
            act.wait_ge(m_w2[i % 2], at(j, 8 * KT, 16 * (i // 2 + 1)))
            act.wait_ge(m_o, at(j, KT, i - 1))
            act.activation(w2h[:, i % 2, :], w2r[:, i % 2, :], ACT.Copy).then_inc(m_w2h, 1)

        def h_biased(act, at, j, i):
            act.wait_ge(m_h, at(j, KT, i + 1))
            if i == 0:
                act.wait_ge(m_b1, at(j, 1, 1))
            act.wait_ge(m_elu, at(j, KT, i - 1))
            act.activation(ut[:, i % 2, :], bank[(i + 1) % 2][:], ACT.Identity, bias=b1u[j][:, i:i + 1]).then_inc(m_u, 1)

        def h_exp(act, at, j, i):
            act.wait_ge(m_neg, at(j, KT, i + 1))
            act.activation(et[:, i % 2, :], et[:, i % 2, :], ACT.Exp).then_inc(m_eexp, 1)

        def h_high(act, at, j, i):
            act.wait_ge(m_elu, at(j, KT, i + 1))
            act.wait_ge(m_o, at(j, KT, i - 2))
            act.activation(hh[:, i % 3, :], et[:, i % 2, :], ACT.Copy).then_inc(m_hh, 1)

        W1_AT = {1: 0, 2: 1, 7: 2, 8: 3, 9: 4, 10: 5}
        W2_AT = {3: 0, 4: 1, 9: 2, 10: 3, 11: 4, 12: 5}
        P_AT = {3: 0, 4: 1, 5: 2, 6: 3, 8: 4, 9: 5, 10: 6, 11: 7}
        STEPS = range(14)

        @block.sync
        def _(sp):
            for s in (m_as, m_mask, m_abs, *m_abr, *m_w1, *m_w2, m_store):
                sp.sem_inc(s, S)
            for i in range(2):
                sp.dma_start(w1r[:, i, :, :], W1v[:, :, i, :]).then_inc(m_w1[i], 16)
                sp.dma_start(w2r[:, i, :], W2v[:, i, :]).then_inc(m_w2[i], 16)
            load_stats(sp, 0)
            spread(sp, 0, 0)
            with sp.Fori(0, 2 * H, H) as half:
                with sp.Fori(0, H, 2) as pair:
                    u0 = sp.snap(half + pair)
                    at = counter(sp, u0)
                    for j in range(2):
                        u = sp.snap(u0 + j)
                        head = sp.snap(u % H)
                        tile0 = sp.snap(head * KT)
                        next0 = sp.snap(((u + 1) % H) * KT)

                        behind = [sp.snap(tile0 + (i + 2) if i < KT - 2 else next0 + (i + 2 - KT))
                                  for i in range(KT)]

                        def tile(i):
                            return bass.ds(behind[i], 1)
                        load_stats(sp, u + 1)
                        for t in STEPS:
                            if t in W1_AT:
                                sp.wait_ge(m_w1l, at(j, KT, W1_AT[t] + 1))
                                sp.sem_inc(m_sp, 1)
                                sp.dma_start(w1r[:, W1_AT[t] % 2, :, :], W1v[:, :, tile(W1_AT[t]), :])\
                                    .then_inc(m_w1[W1_AT[t] % 2], 16)
                            if t in W2_AT:
                                sp.wait_ge(m_w2l, at(j, KT, W2_AT[t] + 1))
                                sp.sem_inc(m_sp, 1)
                                sp.dma_start(w2r[:, W2_AT[t] % 2, :], W2v[:, tile(W2_AT[t]), :])\
                                    .then_inc(m_w2[W2_AT[t] % 2], 16)
                            if t == 1:
                                spread(sp, u + 1, (j + 1) % 2)
                hn = sp.snap(half // H)
                sp.wait_ge(m_keep, hn * 6 + (6 + S))
                sp.sem_inc(m_sp, 1)
                sp.dma_start(h2_dram[bass.ds(hn, 1), :, :, :], work[:]).then_inc(m_store, 16)
            sp.wait_ge(m_store, 32 + S)
            sp.wait_ge(m_abs, 16 * (2 * H + 1) + S)
            sp.wait_ge(m_as, 16 * (2 * H + 1) + S)
            sp.wait_ge(m_mask, 16 * (2 * H + 1) + S)
            sp.wait_ge(m_abr[0], 16 * (H + 1) + S)
            for i in range(2):
                sp.wait_ge(m_w1[i], 16 * (KT * H + 1) + S)
                sp.wait_ge(m_w2[i], 16 * (KT * H + 1) + S)

        @block.gpsimd
        def _(pool):
            pool.memset(ones[:], 1.0).then_inc(m_ones, 1)
            pool.sem_inc(m_sum, S)

            def add(at, j, s, par):
                if s == 0:
                    return
                pool.wait_ge(m_p, at(j, NT, s + 1))
                if s == 1:
                    pool.wait_ge(m_den, at(j, 1, -1))
                    pool.tensor_tensor(psums[:, par, :], tb[:, 0, :], tb[:, 1, :], ALU.add).then_inc(m_sum, 2)
                else:
                    pool.wait_ge(m_sum, at(j, NT, s))
                    pool.tensor_tensor(psums[:, par, :], psums[:, par, :], tb[:, s % 2, :], ALU.add).then_inc(m_sum, 1)

            at = counter(pool, 0)
            for s in range(NT):
                add(at, 0, s, 0)
            with pool.Fori(0, 2 * H, 2) as u0:
                at = counter(pool, u0)
                for j in range(2):
                    for s in range(NT):
                        add(at, j + 1, s, (j + 1) % 2)

        @block.vector
        def _(dve):
            for s in (m_top, m_small, m_ab, m_terms, m_expo, m_p, m_pl, m_deneps, m_rden, m_zt, m_zl, m_w1l,
                      m_w2l, m_neg, m_elu, m_hl, m_keep, m_zero, m_b1):
                dve.sem_inc(s, S)
            for b in range(6):
                dve.memset(h2ps[:, b, :], 0.0).then_inc(m_zero, 1)
            maxima(dve, 0, 0)
            at = counter(dve, 0)
            for s in range(NT):
                exponent_terms(dve, at, 0, s, 0, 0)
                exponent(dve, at, 0, s)
                weights(dve, at, 0, s, 0)
                weights_low(dve, at, 0, s, 0)
            with dve.Fori(0, 2 * H, H) as half:
                with dve.Fori(0, H, 2) as pair:
                    u0 = dve.snap(half + pair)
                    at = counter(dve, u0)
                    for j in range(2):
                        v = dve.snap(u0 + (j + 1))
                        hv = dve.snap(v % H)
                        tv = dve.snap(((v // H) % 2) * HALF)
                        par = (j + 1) % 2
                        for t in STEPS:
                            k, i, s = t - 1, t - 7, P_AT.get(t)
                            if t == 0:
                                dve.wait_ge(m_den, at(j, 1, 1))
                                dve.wait_ge(m_rden, at(j, 1, 0))
                                dve.tensor_scalar(den[:], bank[0][:], EPS_DEN, XS, ALU.add, ALU.mult)\
                                    .then_inc(m_deneps, 1)
                                dve.wait_ge(m_deneps, at(j, 1, 1))
                                dve.wait_ge(m_zt, at(j, KT, 0))
                                dve.reciprocal(rden[:], den[:]).then_inc(m_rden, 1)
                                dve.wait_ge(m_u, at(j, KT, -KT))
                                dve.tensor_copy(b1u[j][:], b1c[:, bass.ds(dve.snap(((u0 + j) % H) * KT), KT)])\
                                    .then_inc(m_b1, 1)
                                maxima(dve, v, par)
                            if s is not None:
                                exponent_terms(dve, at, j + 1, s, par, hv)
                            if 0 <= k < KT:
                                if k == 0:
                                    dve.wait_ge(m_store, (half // H) * 16 + S)
                                z_scaled(dve, at, j, k)
                            if 0 <= i < KT:
                                h_negative(dve, at, j, i)
                            if s is not None:
                                exponent(dve, at, j + 1, s)
                            if 0 <= i < KT:
                                h_elu(dve, at, j, i)
                            if s is not None:
                                weights(dve, at, j + 1, s, tv)
                            if 0 <= k < KT:
                                z_low(dve, at, j, k)
                            if 0 <= i < KT:
                                h_low(dve, at, j, i)
                            if s is not None:
                                weights_low(dve, at, j + 1, s, par)
                            if t in W1_AT:
                                w1_low(dve, at, j, W1_AT[t])
                            if t in W2_AT:
                                w2_low(dve, at, j, W2_AT[t])
                hn = dve.snap(half // H)
                dve.wait_ge(m_o, half * KT + (H * KT + S))
                dve.wait_ge(m_hl, half * KT + (H * KT + S))
                for b in range(3, 6):
                    dve.tensor_copy(work[:, b, :], h2ps[:, b, :]).then_inc(m_keep, 1)
                dve.wait_ge(m_keep, hn * 6 + (6 + S))
                for b in range(6):
                    dve.memset(h2ps[:, b, :], 0.0).then_inc(m_zero, 1)

        @block.scalar
        def _(act):
            for s in (m_exp, m_ph, m_zh, m_w1h, m_w2h, m_u, m_eexp, m_hh):
                act.sem_inc(s, S)
            at = counter(act, 0)
            for s in range(NT):
                exponential(act, at, 0, s)
                weights_high(act, at, 0, s, 0)
            with act.Fori(0, 2 * H, H) as half:
                with act.Fori(0, H, 2) as pair:
                    u0 = act.snap(half + pair)
                    at = counter(act, u0)
                    for j in range(2):
                        par = (j + 1) % 2
                        for t in STEPS:
                            k, i, s = t - 1, t - 7, P_AT.get(t)
                            if 0 <= i < KT:
                                h_biased(act, at, j, i)
                            if s is not None:
                                exponential(act, at, j + 1, s)
                            if 0 <= i < KT:
                                h_exp(act, at, j, i)
                            if 0 <= k < KT:
                                z_high(act, at, j, k)
                            if s is not None:
                                weights_high(act, at, j + 1, s, par)
                            if 0 <= i < KT:
                                h_high(act, at, j, i)
                            if t in W1_AT:
                                w1_high(act, at, j, W1_AT[t])
                            if t in W2_AT:
                                w2_high(act, at, j, W2_AT[t])
                act.wait_ge(m_o, half * KT + (H * KT + S))
                act.wait_ge(m_hl, half * KT + (H * KT + S))
                for b in range(3):
                    act.activation(work[:, b, :], h2ps[:, b, :], ACT.Copy).then_inc(m_keep, 1)

        @block.tensor
        def _(pe):
            for s in (m_den, m_z, m_h, m_o):
                pe.sem_inc(s, S)
            pe.wait_ge(m_ones, 1)

            def product(out, terms, **kw):
                for n, (a, b) in enumerate(terms):
                    mm = pe.matmul(out, a, b, start=(n == 0), stop=(n == len(terms) - 1), **kw)
                return mm

            def z_tile(at, j, k):
                if k == 0:
                    pass
                elif k == 1:
                    pe.wait_ge(m_deneps, at(j, 1, 1))
                else:
                    pe.wait_ge(m_zt, at(j, KT, k - 1))
                for s in range(NT):
                    if k == 0:
                        pe.wait_ge(m_pl, at(j, NT, s + 1))
                    kk = slice(k * P, (k + 1) * P)
                    for n, (a, b) in enumerate(((xh, ph), (xh, pl), (xl, ph))):
                        mm = pe.matmul(bank[(k + 1) % 2][:], a[:, s, kk], b[j][:, s, :], start=(s == 0 and n == 0),
                                       stop=(s == NT - 1 and n == 2))
                mm.then_inc(m_z, 1)

            def h_tile(at, j, i):
                pe.wait_ge(m_w1l, at(j, KT, i + 1))
                if i < 2:
                    pe.wait_ge(m_zt, at(j, KT, KT - 1 + i))
                else:
                    pe.wait_ge(m_u, at(j, KT, i - 1))
                for k in range(KT):
                    if i == 0:
                        pe.wait_ge(m_zl, at(j, KT, k + 1))
                    for n, (a, b) in enumerate(((w1h, zh), (w1h, zl), (w1l, zh))):
                        mm = pe.matmul(bank[(i + 1) % 2][:], a[:, i % 2, k, :], b[:, k, :], start=(k == 0 and n == 0),
                                       stop=(k == KT - 1 and n == 2))
                mm.then_inc(m_h, 1)

            def h2_tile(at, j, i, hn):
                pe.wait_ge(m_hl, at(j, KT, i + 1))
                pe.wait_ge(m_w2l, at(j, KT, i + 1))
                if j == 0 and i == 0:
                    pe.wait_ge(m_zero, hn * 6 + (6 + S))
                for a, b in ((hh, w2h), (hh, w2l), (hl, w2h)):
                    for t in range(DT):
                        at0 = t * D
                        while at0 < (t + 1) * D:
                            to = min((t + 1) * D, (at0 // 512 + 1) * 512)
                            mm = pe.matmul(h2ps[:, at0 // 512, at0 % 512:at0 % 512 + to - at0],
                                           a[:, i % 3, t * P:(t + 1) * P], b[:, i % 2, at0 - t * D:to - t * D],
                                           start=False, stop=True, skip_group_check=True)
                            at0 = to
                mm.then_inc(m_o, 1)

            with pe.Fori(0, 2 * H, H) as half:
                hn = pe.snap(half // H)
                with pe.Fori(0, H, 2) as pair:
                    u0 = pe.snap(half + pair)
                    at = counter(pe, u0)
                    for j in range(2):
                        pe.wait_ge(m_sum, at(j, NT, NT))
                        pe.matmul(bank[0][:], ones[:], psums[:, j, :], start=True, stop=True).then_inc(m_den, 1)
                        for k in range(KT):
                            z_tile(at, j, k)
                        h_tile(at, j, 0)
                        h_tile(at, j, 1)
                        for i in range(2, KT):
                            h_tile(at, j, i)
                            h2_tile(at, j, i - 2, hn)
                        h2_tile(at, j, KT - 2, hn)
                        h2_tile(at, j, KT - 1, hn)


def second_logits(nc, env):
    h2_dram, mask_dram, row_dram, row2_dram = (env[k] for k in ("h2_dram", "mask_dram", "row_dram", "row2_dram"))
    a_s2, a_d2 = env["a_s2"], env["a_d2"]
    ct, hh, hl, lc2, ab2, dinv = (env[k] for k in ("ct", "h2h", "h2l", "lc2", "ab2", "dinv"))
    NT, N = ct.shape[1], ct.shape[2]
    D = a_s2.shape[1]
    HT = NT // 2

    with ExitStack() as ctx:
        def sb(name, shape, dt):
            return ctx.enter_context(nc.sbuf_tensor(name, shape, dt))

        sem = Sems(nc, ctx)
        ps = ctx.enter_context(nc.psum_tensor("l2_ps", [P, 4, 512], F32))
        hraw = sb("h2_raw", [P, NT, D], F32)
        arow = sb("a2_rows", [P, 2, D], F32)
        junk = sb("junk2", [P, 2, N], BF16)
        mask = sb("mask2", [P, 2, HT, N], BF16)
        as_row = sb("as2_row", [P, N], F32)
        small = sb("small2", [P, 3, NT], F32)
        rows = sb("rows2", [2 * NT, P], F32)
        rows1 = sb("rows1", [NT, P], F32)
        ident = sb("ident2", [P, P], F32)
        cth = sb("ct_high", [P, 2, N], F16)
        ctl = sb("ct_low", [P, 2, N], F16)
        ones = sb("ones2", [P, 2], F16)
        zeros = sb("zeros2", [P, P], F16)
        deg = sb("deg", [P, 5, NT], F32)

        t_h = [sem(f"h2_loaded{i}") for i in range(2)]
        t_a = sem("a2_rows_loaded")
        t_mask = [sem(f"mask2_loaded{i}") for i in range(2)]
        t_c = sem("constants_made")
        t_sum = sem("a2_sums")
        t_hi = sem("h2_high_done")
        t_lo = sem("h2_low_done")
        t_turn = sem("columns_turned")
        t_rows = sem("rows_kept")
        t_dram = sem("rows_stored")
        t_back = sem("rows_back")
        t_max = sem("maxima2_taken")
        t_small = sem("small2_steps")
        t_cth = sem("ct_high_done")
        t_ctl = sem("ct_low_done")
        t_deg = sem("ct_tile_counted")
        t_root = sem("degree_root")
        t_dg = sem("degree_steps")
        block = ctx.enter_context(nc.Block())

        @block.sync
        def _(sp):
            for hf in range(2):
                sp.dma_start(hraw[:, hf * HT:(hf + 1) * HT, :].rearrange("p t d -> p (t d)"),
                             h2_dram[hf].rearrange("p b c -> p (b c)")).then_inc(t_h[hf], 16)
            sp.dma_start(arow[:, 0, :], a_s2.to_broadcast([P, D])).then_inc(t_a, 16)
            sp.dma_start(arow[:, 1, :], a_d2.to_broadcast([P, D])).then_inc(t_a, 16)
            for hf in range(2):
                sp.dma_start(mask[:, hf, :, :], mask_dram[hf]).then_inc(t_mask[hf], 16)
            sp.wait_ge(t_rows, 1)
            sp.dma_start(row_dram, rows1[:]).then_inc(t_dram, 16)
            sp.wait_ge(t_dram, 16)
            sp.dma_start(as_row[:], row_dram.rearrange("t p -> (t p)").partition_broadcast(P)).then_inc(t_back, 16)
            sp.wait_ge(t_rows, 2)
            sp.dma_start(row2_dram, rows[:]).then_inc(t_dram, 16)
            sp.wait_ge(t_dram, 32)

        @block.gpsimd
        def _(pool):
            pool.memset(ident[:], 0.0).then_inc(t_c, 1)
            pool.wait_ge(t_c, 1)
            pool.affine_select(out=ident[:], in_=ident[:], compare_op=ALU.not_equal, fill=1.0, base=0,
                               pattern=[[-1, P]], channel_multiplier=1).then_inc(t_c, 1)
            pool.memset(ones[:], 1.0).then_inc(t_c, 1)
            pool.memset(zeros[:], 0.0).then_inc(t_c, 1)

        @block.vector
        def _(dve):
            dve.wait_ge(t_a, 32)
            for t in range(NT):
                if t % HT == 0:
                    dve.wait_ge(t_h[t // HT], 16)
                for sd in range(2):
                    n = 2 * t + sd
                    if n >= 2:
                        dve.wait_ge(t_sum, n - 1)
                    dve.tensor_tensor_reduce(junk[:, sd, 0:D], hraw[:, t, :], arow[:, sd, :], 1.0, 0.0, ALU.mult,
                                             ALU.add, lc2[:, sd, t:t + 1]).then_inc(t_sum, 1)
                dve.wait_ge(t_cth, t + 1)
                if t >= 2:
                    dve.wait_ge(t_deg, t - 1)
                dve.tensor_tensor(ctl[:, t % 2, :], ct[:, t, :], cth[:, t % 2, :], ALU.subtract).then_inc(t_ctl, 1)
                dve.wait_ge(t_hi, t + 1)
                dve.tensor_tensor(hl[:, t, 0:D], hraw[:, t, :], f32(hh[:, t, 0:D]), ALU.subtract).then_inc(t_lo, 1)
            dve.wait_ge(t_sum, 2 * NT)
            dve.tensor_scalar(lc2[:, 2, :], lc2[:, 0, :], SLOPE, None, ALU.mult).then_inc(t_small, 1)
            dve.wait_ge(t_turn, 1)
            dve.tensor_copy(rows1[:], ps[0:NT, 0, 0:P]).then_inc(t_rows, 1)
            dve.wait_ge(t_deg, NT)
            dve.tensor_scalar(deg[:, 0, :], ps[:, 3, 0:2 * NT].rearrange("p (t o) -> p t o", o=2)[:, :, 0:1]
                              .rearrange("p t o -> p (t o)"), 1.0, None, ALU.add).then_inc(t_dg, 1)
            dve.wait_ge(t_root, 1)
            dve.reciprocal(deg[:, 2, :], deg[:, 1, :]).then_inc(t_dg, 1)
            dve.wait_ge(t_dg, 2)
            dve.tensor_tensor(deg[:, 3, :], deg[:, 0, :], deg[:, 2, :], ALU.mult).then_inc(t_dg, 1)
            dve.wait_ge(t_dg, 3)
            dve.tensor_tensor(deg[:, 4, :], deg[:, 3, :], deg[:, 1, :], ALU.add).then_inc(t_dg, 1)
            dve.wait_ge(t_dg, 4)
            dve.tensor_scalar(deg[:, 3, :], deg[:, 4, :], 0.5, None, ALU.mult).then_inc(t_dg, 1)
            dve.wait_ge(t_dg, 5)
            dve.reciprocal(dinv[:, 0, :], deg[:, 3, :]).then_inc(t_dg, 1)
            dve.wait_ge(t_dg, 6)
            dve.tensor_scalar(dinv[:, 1, :], dinv[:, 0, :], XS, None, ALU.mult)
            dve.tensor_scalar(dinv[:, 2, :], dinv[:, 0, :], 1.0 / XS, None, ALU.mult).then_inc(t_dg, 1)
            dve.wait_ge(t_back, 16)
            for t in range(NT):
                if t % HT == 0:
                    dve.wait_ge(t_mask[t // HT], 16)
                if t >= 2:
                    dve.wait_ge(t_max, t - 1)
                else:
                    dve.wait_ge(t_sum, 2 * NT)
                dve.tensor_tensor_reduce(junk[:, t % 2, :], mask[:, t // HT, t % HT, :], as_row[:], 1.0, FAR,
                                         ALU.add, ALU.max, small[:, 0, t:t + 1]).then_inc(t_max, 1)
            dve.wait_ge(t_max, NT)
            dve.tensor_tensor(small[:, 1, :], small[:, 0, :], lc2[:, 1, :], ALU.add).then_inc(t_small, 1)
            dve.wait_ge(t_small, 2)
            dve.scalar_tensor_tensor(out=small[:, 2, :], in0=small[:, 1, :], scalar=SLOPE, in1=small[:, 1, :],
                                     op0=ALU.mult, op1=ALU.max).then_inc(t_small, 1)
            dve.wait_ge(t_small, 3)
            dve.tensor_tensor(ab2[:, 0, :], lc2[:, 1, :], small[:, 2, :], ALU.subtract)
            dve.scalar_tensor_tensor(out=ab2[:, 1, :], in0=lc2[:, 1, :], scalar=SLOPE, in1=small[:, 2, :],
                                     op0=ALU.mult, op1=ALU.subtract).then_inc(t_small, 1)
            dve.wait_ge(t_turn, 2)
            dve.tensor_copy(rows[:], ps[0:2 * NT, 1, 0:P]).then_inc(t_rows, 1)

        @block.scalar
        def _(act):
            for t in range(NT):
                if t >= 2:
                    act.wait_ge(t_deg, t - 1)
                act.activation(cth[:, t % 2, :], ct[:, t, :], ACT.Copy).then_inc(t_cth, 1)
                if t % HT == 0:
                    act.wait_ge(t_h[t // HT], 16)
                act.activation(hh[:, t, 0:D], hraw[:, t, :], ACT.Copy).then_inc(t_hi, 1)
            act.wait_ge(t_c, 4)
            act.activation(hh[:, :, D:D + 2], ones[:].unsqueeze(1).to_broadcast([P, NT, 2]), ACT.Copy)
            act.activation(hl[:, :, D:D + 2], zeros[:, 0:2].unsqueeze(1).to_broadcast([P, NT, 2]), ACT.Copy)
            act.wait_ge(t_dg, 1)
            act.activation(deg[:, 1, :], deg[:, 0, :], ACT.Sqrt).then_inc(t_root, 1)

        @block.tensor
        def _(pe):
            pe.wait_ge(t_c, 4)
            pe.matmul(ps[:, 3, 0:2 * NT], zeros[:], zeros[:, 0:2 * NT], start=True, stop=False, skip_group_check=True)
            for s in range(NT):
                pe.wait_ge(t_ctl, s + 1)
                for part in (cth, ctl):
                    for t in range(NT):
                        mm = pe.matmul(ps[:, 3, 2 * t:2 * t + 2], part[:, s % 2, t * P:(t + 1) * P], ones[:],
                                       start=False, stop=True, skip_group_check=True)
                mm.then_inc(t_deg, 1)
            pe.wait_ge(t_sum, 2 * NT)
            pe.transpose(ps[0:NT, 0, 0:P], lc2[:, 0, :], ident[:]).then_inc(t_turn, 1)
            pe.wait_ge(t_small, 4)
            pe.transpose(ps[0:2 * NT, 1, 0:P], ab2[:].rearrange("p a t -> p (a t)"), ident[:]).then_inc(t_turn, 1)


def second_attention(nc, env):
    x, b2, row2_dram = env["x"], env["b2"], env["row2_dram"]
    ct, hh, hl, lc2, dinv, xt, mv = (env[k] for k in ("ct", "h2h", "h2l", "lc2", "dinv", "xt", "mv"))
    NT, N = ct.shape[1], ct.shape[2]
    D = x.shape[1]
    HT, HALF = NT // 2, N // 2

    with ExitStack() as ctx:
        def sb(name, shape, dt):
            return ctx.enter_context(nc.sbuf_tensor(name, shape, dt))

        sem = Sems(nc, ctx)
        ps = ctx.enter_context(nc.psum_tensor("a2_ps", [P, 8, 512], F32))
        ph = [sb(f"p2_high{i}", [P, NT, HALF], F32R) for i in range(2)]
        pl = [sb(f"p2_low{i}", [P, NT, HALF], F32R) for i in range(2)]
        ab_rows = sb("ab2_rows", [P, 2, N], F32)
        b2row = sb("b2_row", [P, D], F32)
        ta = sb("ta2", [P, 2, HALF], F32)
        tb = sb("tb2", [P, 2, HALF], F32)
        rd = sb("rd2", [P, 2, NT], F32)
        stats = sb("stats2", [P, NT, 2, 6], F32)
        root = sb("root2", [P, 6, NT], F32)

        t_ab = sem("ab2_rows_loaded")
        t_x = sem("x_back")
        t_b2 = sem("b2_loaded")
        t_terms = sem("terms2_made")
        t_expo = sem("exponents2_made")
        t_exp = sem("exponentials2_made")
        t_p = sem("weights2_made")
        t_ph = sem("weights2_high")
        t_pl = sem("weights2_low")
        t_xb = sem("x_biased")
        t_o = sem("attention2_tile")
        t_rd = sem("sum2_steps")
        t_x1 = sem("x1_parts")
        t_st = sem("stats2_steps")
        t_root = sem("root2_taken")
        block = ctx.enter_context(nc.Block())

        @block.sync
        def _(sp):
            sp.dma_start(ab_rows[:], row2_dram.rearrange("(a t) p -> a (t p)", a=2).partition_broadcast(P))\
              .then_inc(t_ab, 16)
            sp.dma_start(b2row[:], b2.partition_broadcast(P)).then_inc(t_b2, 16)
            sp.dma_start(xt[:], x.rearrange("(t p) d -> p t d", p=P)).then_inc(t_x, 16)

        @block.gpsimd
        def _(pool):
            pool.wait_ge(t_x, 16)
            pool.wait_ge(t_b2, 16)
            for t in range(NT):
                pool.tensor_tensor(xt[:, t, :], xt[:, t, :], b2row[:], ALU.add).then_inc(t_xb, 1)

        def halves(hf):
            return slice(hf * HALF, (hf + 1) * HALF)

        @block.vector
        def _(dve):
            dve.wait_ge(t_ab, 16)

            def terms(n):
                hf, s = divmod(n, NT)
                if n >= 2:
                    dve.wait_ge(t_pl, n - 1)
                dve.tensor_scalar(ta[:, n % 2, :], ab_rows[:, 0, halves(hf)], lc2[:, 0, s:s + 1], 0.0, ALU.add,
                                  ALU.min)
                dve.tensor_scalar(tb[:, n % 2, :], ab_rows[:, 1, halves(hf)], lc2[:, 2, s:s + 1], 0.0, ALU.add,
                                  ALU.min).then_inc(t_terms, 1)
                dve.wait_ge(t_terms, n + 1)
                dve.tensor_tensor(ta[:, n % 2, :], ta[:, n % 2, :], tb[:, n % 2, :], ALU.max).then_inc(t_expo, 1)

            def rest(n):
                hf, s = divmod(n, NT)
                dve.wait_ge(t_exp, n + 1)
                dve.tensor_tensor(tb[:, n % 2, :], ta[:, n % 2, :], ct[:, s, halves(hf)], ALU.mult).then_inc(t_p, 1)
                dve.wait_ge(t_ph, n + 1)
                dve.tensor_tensor(pl[hf][:, s, :], tb[:, n % 2, :], f32(ph[hf][:, s, :]), ALU.subtract)\
                    .then_inc(t_pl, 1)

            def tile_out(t):
                a, b = ps[:, 2 * (t % 4), :], ps[:, 2 * (t % 4) + 1, :]
                dve.wait_ge(t_o, t + 1)
                dve.tensor_scalar(rd[:, 0, t:t + 1], b[:, D - 384:D - 383], EPS_DEN, None, ALU.add).then_inc(t_rd, 1)
                dve.wait_ge(t_rd, 2 * t + 1)
                dve.reciprocal(rd[:, 1, t:t + 1], rd[:, 0, t:t + 1]).then_inc(t_rd, 1)
                dve.wait_ge(t_rd, 2 * t + 2)
                dve.wait_ge(t_xb, t + 1)
                for c, bankc in enumerate((a, b)):
                    part = xt[:, t, c * 384:(c + 1) * 384]
                    dve.scalar_tensor_tensor(out=part, in0=bankc[:, 0:384], scalar=rd[:, 1, t:t + 1], in1=part,
                                             op0=ALU.mult, op1=ALU.add).then_inc(t_x1, 1)
                for c in range(2):
                    dve.wait_ge(t_x1, 2 * t + c + 1)
                    dve.bn_stats(stats[:, t, c, :], xt[:, t, c * 384:(c + 1) * 384]).then_inc(t_st, 1)
                dve.wait_ge(t_st, 3 * t + 2)
                dve.bn_aggr(mv[:, t, :], stats[:, t, :, :].rearrange("p a b -> p (a b)")).then_inc(t_st, 1)

            for n in range(2 * NT + 1):
                if n < 2 * NT:
                    terms(n)
                if n >= 1:
                    rest(n - 1)
            for t in range(NT):
                tile_out(t)
            done = rstd_steps(dve, mv, root, t_st, 3 * NT, t_root)
            dve.wait_ge(t_st, done)
            dve.tensor_copy(dinv[:, 3, :], root[:, 5, :])

        @block.scalar
        def _(act):
            for n in range(2 * NT):
                hf, s = divmod(n, NT)
                act.wait_ge(t_expo, n + 1)
                act.activation(ta[:, n % 2, :], ta[:, n % 2, :], ACT.Exp).then_inc(t_exp, 1)
                act.wait_ge(t_p, n + 1)
                act.activation(ph[hf][:, s, :], tb[:, n % 2, :], ACT.Copy).then_inc(t_ph, 1)
            act.wait_ge(t_st, 3 * NT + 1)
            act.activation(root[:, 1, :], root[:, 0, :], ACT.Sqrt).then_inc(t_root, 1)

        @block.tensor
        def _(pe):
            for t in range(NT):
                hf, tt = divmod(t, HT)
                if t >= 4:
                    pe.wait_ge(t_x1, 2 * (t - 3))
                for s in range(NT):
                    if tt == 0:
                        pe.wait_ge(t_pl, hf * NT + s + 1)
                    dd = slice(tt * P, (tt + 1) * P)
                    for n, (a, b) in enumerate(((ph, hh), (ph, hl), (pl, hh))):
                        for c, (lo, hi) in enumerate(((0, 384), (384, D + 2))):
                            mm = pe.matmul(ps[:, 2 * (t % 4) + c, 0:hi - lo], a[hf][:, s, dd], b[:, s, lo:hi],
                                           start=(s == 0 and n == 0), stop=(s == NT - 1 and n == 2))
                mm.then_inc(t_o, 1)


def convolution(nc, env):
    Wg, bg, out = env["Wg"], env["bg"], env["out"]
    ct, dinv, xt, mv = (env[k] for k in ("ct", "dinv", "xt", "mv"))
    NT, N = ct.shape[1], ct.shape[2]
    D = Wg.shape[1]
    KT = D // P
    HALF = N // 2
    HT = NT // 2

    with ExitStack() as ctx:
        def sb(name, shape, dt):
            return ctx.enter_context(nc.sbuf_tensor(name, shape, dt))

        sem = Sems(nc, ctx)
        ps = ctx.enter_context(nc.psum_tensor("g_ps", [P, 8, 512], F32))
        xh = sb("x2_high", [P, NT, D], F16)
        xl = sb("x2_low", [P, NT, D], F16)
        xs = sb("x2_scaled", [P, 2, D], F32)
        cf = sb("count_f", [P, 2, N], F32)
        chi = sb("count_high", [P, NT, N], F16)
        clo = sb("count_low", [P, NT, N], F16)
        ident = sb("ident3", [P, P], F32)
        wr = sb("wg_raw", [P, 2, D], F32)
        wh = sb("wg_high", [P, KT, D], F32R)
        wl = sb("wg_low", [P, KT, D], F32R)
        zt = sb("z3", [P, 2, HALF], F32)
        zh = sb("z3_high", [P, KT, N], F32R)
        zl = sb("z3_low", [P, KT, N], F32R)
        bgrow = sb("bg_row", [P, D], F32)

        g_w = [sem(f"wg_loaded{i}") for i in range(2)]
        g_b = sem("bg_loaded")
        g_c = sem("ident3_made")
        g_xs = sem("x2_scaled_steps")
        g_xh = sem("x2_high_done")
        g_xl = sem("x2_low_done")
        g_cf = sem("counts_float")
        g_ci = sem("loops_added")
        g_ch = sem("counts_high")
        g_cl = sem("counts_low")
        g_wh = sem("wg_high_done")
        g_wl = sem("wg_low_done")
        g_xb = sem("x1_biased")
        g_z = sem("z3_ready")
        g_zt = sem("z3_copied")
        g_zh = sem("z3_high_done")
        g_zl = sem("z3_low_done")
        g_o = sem("convolution_tile")
        g_y = sem("output_parts")
        g_out = sem("output_stored")
        block = ctx.enter_context(nc.Block())

        @block.sync
        def _(sp):
            sp.dma_start(bgrow[:], bg.partition_broadcast(P)).then_inc(g_b, 16)
            for k in range(KT):
                if k >= 2:
                    sp.wait_ge(g_wl, k - 1)
                sp.dma_start(wr[:, k % 2, :], Wg[k * P:(k + 1) * P, :]).then_inc(g_w[k % 2], 16)
            for t in range(NT):
                sp.wait_ge(g_y, 2 * t + 2)
                sp.dma_start(out[t * P:(t + 1) * P, :], xt[:, t, :]).then_inc(g_out, 16)
            sp.wait_ge(g_out, 16 * NT)

        @block.gpsimd
        def _(pool):
            pool.memset(ident[:], 0.0).then_inc(g_c, 1)
            pool.wait_ge(g_c, 1)
            pool.affine_select(out=ident[:], in_=ident[:], compare_op=ALU.not_equal, fill=1.0, base=0,
                               pattern=[[-1, P]], channel_multiplier=1).then_inc(g_c, 1)
            pool.wait_ge(g_b, 16)
            for t in range(NT):
                pool.wait_ge(g_xs, 2 * t + 1)
                pool.tensor_tensor(xt[:, t, :], xt[:, t, :], bgrow[:], ALU.add).then_inc(g_xb, 1)

        @block.vector
        def _(dve):
            dve.wait_ge(g_c, 2)

            def tile_in(s):
                if s >= 2:
                    dve.wait_ge(g_xl, s - 1)
                dve.tensor_scalar(xs[:, s % 2, :], xt[:, s, :], mv[:, s, 0:1], dinv[:, 3, s:s + 1], ALU.subtract,
                                  ALU.mult).then_inc(g_xs, 1)
                dve.wait_ge(g_cf, s + 1)
                diag = cf[:, s % 2, s * P:(s + 1) * P]
                dve.tensor_tensor(diag, diag, ident[:], ALU.add).then_inc(g_ci, 1)
                dve.wait_ge(g_xs, 2 * s + 1)
                dve.tensor_scalar(xs[:, s % 2, :], xs[:, s % 2, :], 0.0, dinv[:, 1, s:s + 1], ALU.max,
                                  ALU.mult).then_inc(g_xs, 1)
                dve.wait_ge(g_ch, s + 1)
                dve.tensor_tensor(clo[:, s, :], cf[:, s % 2, :], chi[:, s, :], ALU.subtract).then_inc(g_cl, 1)
                dve.wait_ge(g_xh, s + 1)
                dve.tensor_tensor(xl[:, s, :], xs[:, s % 2, :], xh[:, s, :], ALU.subtract).then_inc(g_xl, 1)

            def w_low(k):
                dve.wait_ge(g_wh, k + 1)
                dve.tensor_tensor(wl[:, k, :], wr[:, k % 2, :], f32(wh[:, k, :]), ALU.subtract).then_inc(g_wl, 1)

            for s in range(NT):
                tile_in(s)
            for n in range(2 * KT):
                hf, k = divmod(n, KT)
                dve.wait_ge(g_z, n + 1)
                if n >= 2:
                    dve.wait_ge(g_zl, n - 1)
                dve.tensor_copy(zt[:, n % 2, :], ps[:, n % 2, :]).then_inc(g_zt, 1)
                if n < KT:
                    w_low(n)
                dve.wait_ge(g_zh, n + 1)
                dve.tensor_tensor(zl[:, k, hf * HALF:(hf + 1) * HALF], zt[:, n % 2, :],
                                  f32(zh[:, k, hf * HALF:(hf + 1) * HALF]), ALU.subtract).then_inc(g_zl, 1)
            for t in range(NT):
                dve.wait_ge(g_o, t + 1)
                dve.wait_ge(g_xb, t + 1)
                for c in range(2):
                    part = xt[:, t, c * 384:(c + 1) * 384]
                    dve.scalar_tensor_tensor(out=part, in0=ps[:, 2 + 2 * (t % 3) + c, 0:384],
                                             scalar=dinv[:, 2, t:t + 1], in1=part, op0=ALU.mult,
                                             op1=ALU.add).then_inc(g_y, 1)

        @block.scalar
        def _(act):
            for s in range(NT):
                if s >= 2:
                    act.wait_ge(g_cl, s - 1)
                act.activation(cf[:, s % 2, :], ct[:, s, :], ACT.Copy).then_inc(g_cf, 1)
                act.wait_ge(g_ci, s + 1)
                act.activation(chi[:, s, :], cf[:, s % 2, :], ACT.Copy).then_inc(g_ch, 1)
                act.wait_ge(g_xs, 2 * s + 2)
                act.activation(xh[:, s, :], xs[:, s % 2, :], ACT.Copy).then_inc(g_xh, 1)
            for n in range(2 * KT):
                hf, k = divmod(n, KT)
                if n < KT:
                    act.wait_ge(g_w[n % 2], 16 * (n // 2 + 1))
                    act.activation(wh[:, n, :], wr[:, n % 2, :], ACT.Copy).then_inc(g_wh, 1)
                act.wait_ge(g_zt, n + 1)
                act.activation(zh[:, k, hf * HALF:(hf + 1) * HALF], zt[:, n % 2, :], ACT.Copy).then_inc(g_zh, 1)

        @block.tensor
        def _(pe):
            for n in range(2 * KT):
                hf, k = divmod(n, KT)
                if n >= 2:
                    pe.wait_ge(g_zt, n - 1)
                for s in range(NT):
                    if n == 0:
                        pe.wait_ge(g_xl, s + 1)
                        pe.wait_ge(g_cl, s + 1)
                    for i, (a, b) in enumerate(((xh, chi), (xh, clo), (xl, chi))):
                        mm = pe.matmul(ps[:, n % 2, :], a[:, s, k * P:(k + 1) * P],
                                       b[:, s, hf * HALF:(hf + 1) * HALF], start=(s == 0 and i == 0),
                                       stop=(s == NT - 1 and i == 2))
                mm.then_inc(g_z, 1)
            pe.wait_ge(g_wl, KT)
            for t in range(NT):
                if t >= 3:
                    pe.wait_ge(g_y, 2 * (t - 2))
                for k in range(KT):
                    if t in (0, HT):
                        pe.wait_ge(g_zl, (t // HT) * KT + k + 1)
                    for i, (a, b) in enumerate(((zh, wh), (zh, wl), (zl, wh))):
                        for c in range(2):
                            mm = pe.matmul(ps[:, 2 + 2 * (t % 3) + c, 0:384], a[:, k, t * P:(t + 1) * P],
                                           b[:, k, c * 384:(c + 1) * 384], start=(k == 0 and i == 0),
                                           stop=(k == KT - 1 and i == 2))
                mm.then_inc(g_o, 1)


def build(nc, x, src, dst, W1, a_s1, a_d1, b1, W2, a_s2, a_d2, b2, Wg, bg, out):
    N, D = x.shape
    H = a_s1.shape[0]
    NT, KT, HALF = N // P, D // P, N // 2
    env = dict(x=x, src=src, dst=dst, W1=W1, a_s1=a_s1, a_d1=a_d1, b1=b1, W2=W2, a_s2=a_s2, a_d2=a_d2,
               b2=b2, Wg=Wg, bg=bg, out=out)
    for name, shape, dt in (("logit_rows", (H, N), F32), ("mask_dram", (2, P, NT // 2, N), BF16),
                            ("ab_dram", (2, 2, HALF), F32), ("h2_dram", (2, P, 6, 512), F32),
                            ("row_dram", (NT, P), F32), ("row2_dram", (2 * NT, P), F32)):
        env[name] = nc.dram_tensor(name, shape, dt).ap()
    with ExitStack() as whole:
        env["ct"] = whole.enter_context(nc.sbuf_tensor("ct", [P, NT, N], U16))
        with ExitStack() as first:
            for name, shape, dt in (("xh", [P, NT, D], F16), ("xl", [P, NT, D], F16), ("lc", [P, NT, 2 * H], F32),
                                    ("lc02", [P, NT, 2 * H], F32), ("b1c", [P, H * KT], F32)):
                env[name] = first.enter_context(nc.sbuf_tensor(name, shape, dt))
            startup(nc, env)
            heads(nc, env)
        for name, shape, dt in (("lc2", [P, 3, NT], F32), ("ab2", [P, 2, NT], F32), ("dinv", [P, 4, NT], F32),
                                ("mv2", [P, NT, 2], F32), ("xt2", [P, NT, D], F32)):
            env[name] = whole.enter_context(nc.sbuf_tensor(name, shape, dt))
        env["xt"], env["mv"] = env["xt2"], env["mv2"]
        with ExitStack() as second:
            env["h2h"] = second.enter_context(nc.sbuf_tensor("h2h", [P, NT, D + 2], F32R))
            env["h2l"] = second.enter_context(nc.sbuf_tensor("h2l", [P, NT, D + 2], F32R))
            second_logits(nc, env)
            second_attention(nc, env)
        convolution(nc, env)


_INS = ['x', 'src', 'dst', 'L0_gnn_W1', 'L0_gnn_a_src1', 'L0_gnn_a_dst1', 'L0_gnn_b1', 'L0_gnn_W2',
        'L0_gnn_a_src2', 'L0_gnn_a_dst2', 'L0_gnn_b2', 'L1_gnn_W', 'L1_gnn_b']


def kernel(**inputs):
    import numpy as _np
    import concourse.bacc as _bacc
    from concourse import mybir as _mybir
    from concourse.bass_utils import run_bass_kernel_spmd as _run

    nc = _bacc.Bacc("TRN2", target_bir_lowering=False, num_devices=1)
    arrays, args = {}, []
    for name in _INS:
        a = _np.ascontiguousarray(inputs[name])
        arrays[f"in_{name}_dram"] = a
        args.append(nc.dram_tensor(f"in_{name}_dram", a.shape, _mybir.dt.from_np(a.dtype), kind="ExternalInput").ap())
    out = nc.dram_tensor("out_0_dram", arrays["in_x_dram"].shape, F32, kind="ExternalOutput").ap()
    build(nc, *args, out)
    r = _run(nc, [arrays], core_ids=[0])
    return r.results[0]["out_0_dram"]
```

```python
from contextlib import ExitStack

import concourse.bass as bass
from concourse import mybir

P = 128
F32 = mybir.dt.float32
F32R = mybir.dt.float32r
F16 = mybir.dt.float16
BF16 = mybir.dt.bfloat16
I32 = mybir.dt.int32
U16 = mybir.dt.uint16
ALU = mybir.AluOpType
ACT = mybir.ActivationFunctionType

SLOPE = 0.2
EPS_DEN = 1e-16
EPS_LN = 1e-5
FAR = -1e38
XS = 1024.0
DIGIT = 4096
START = 16


def f32(ap):
    return ap.bitcast(F32)


class Sems:

    def __init__(self, nc, ctx):
        self.nc, self.ctx = nc, ctx

    def __call__(self, name):
        return self.ctx.enter_context(self.nc.semaphore(name))


def startup(nc, env):
    x, src, dst, W1, a_s1, a_d1 = (env[k] for k in ("x", "src", "dst", "W1", "a_s1", "a_d1"))
    N, D = x.shape
    E = src.shape[0]
    H = a_s1.shape[0]
    NT, KT = N // P, D // P
    HALF = N // 2
    CH = E // P
    CG = DIGIT // P
    NG = CH // CG
    HG = H // NG
    RING = 8
    assert CG * P <= DIGIT and CH == CG * NG and H == NT == HG * NG and CG == NT + 2 * KT * HG
    xh, xl, ct, lc, lc02, b1c = (env[k] for k in ("xh", "xl", "ct", "lc", "lc02", "b1c"))
    logit_rows, mask_dram = env["logit_rows"], env["mask_dram"]

    with ExitStack() as ctx:
        def sb(name, shape, dt):
            return ctx.enter_context(nc.sbuf_tensor(name, shape, dt))

        sem = Sems(nc, ctx)
        psum = ctx.enter_context(nc.psum_tensor("count_ps", [P, 8, 512], F32))
        edge_i = sb("edge_i", [P, 2, CH], I32)
        dst_low = sb("dst_low", [P, CH], I32)
        edge_f = sb("edge_f", [P, 3, CH], F32)
        iota = sb("iota", [P, N], F16)
        src_hot = sb("src_hot", [P, RING, N], F16)
        dst_hot = sb("dst_hot", [P, RING, HALF], F16)
        xt = sb("xt", [P, NT, D], F32)
        stats = sb("stats", [P, HG, 2, 6], F32)
        mv = sb("mv", [P, HG, 2], F32)
        root = sb("root", [P, 7, HG], F32)
        xT = sb("xT", [P, KT, N], F32)
        wv = sb("wv", [P, KT, D], F32)
        arow = sb("arow", [P, HG, 2, D], F32)
        junk = sb("junk", [P, 2, D], BF16)
        vsum = sb("vsum", [P, 2 * KT], F32)
        V = sb("V", [P, KT, 2 * H], F32)
        packed = sb("packed", [P, NT, 512], F32)
        digits = sb("digits", [P, NT, N], U16)
        near = sb("near", [P, NT, N], BF16)
        ident = sb("ident", [P, P], F32)
        ident_b = sb("ident_b", [P, P], BF16)
        lg = sb("lg", [H, N], F32)
        half_col = sb("half_col", [P, 1], F32)
        b1r = sb("b1_rows", [H * KT, P], F32)

        s_edges = sem("edges_loaded")
        s_x = sem("x_loaded")
        s_b1 = sem("b1_loaded")
        s_w = [sem(f"w_tile_loaded{k}") for k in range(KT)]
        s_a = [sem(f"a_rows_loaded{i}") for i in range(HG)]
        s_turn = sem("loads_begun")
        s_iota = sem("iota_made")
        s_ident = sem("ident_made")
        s_prep = sem("edge_prep")
        s_ln = sem("ln_steps")
        s_root = sem("root_taken")
        s_hot = sem("one_hots_made")
        s_used = sem("one_hots_used")
        s_bank = sem("bank_filled")
        s_bfree = sem("bank_read")
        s_xturn = sem("x_turn_begun")
        s_lnturn = sem("averages_begun")
        s_xn = sem("x_centred")
        s_xr = sem("x_normed")
        s_xhi = sem("x_high")
        s_xlo = sem("x_low")
        s_v = sem("w_a_summed")
        s_vc = sem("w_a_kept")
        s_high = sem("high_digits")
        s_low = sem("low_digits")
        s_add = sem("counts_added")
        s_near = sem("near_made")
        s_xTp = sem("x_turned")
        s_xT = sem("xT_kept")
        s_lcp = sem("logit_columns_ready")
        s_lc = sem("logit_columns_kept")
        s_lgp = sem("logit_rows_ready")
        s_lg = sem("logit_rows_kept")
        s_mp = sem("mask_turned")
        s_mk = [sem(f"mask_kept{n}") for n in range(2)]
        s_mout = sem("mask_stored")
        s_out = sem("logit_rows_stored")
        block = ctx.enter_context(nc.Block())

        mask = src_hot[:].bitcast(BF16)
        W1v = W1.rearrange("(k p) (h c) -> p k h c", p=P, h=H)
        LN = 3 * HG + 7
        LN0 = CG - LN - 8
        LOW_AT = range(CG - 1 - 3 * NT, CG - 3, 3)
        SUM_AT = [j for j in range(CG) if j not in LOW_AT]

        def keep_bank(act, g, b):
            act.wait_ge(s_bank, g * NT + (b + 1 + START))
            act.wait_ge(s_low, g * NT + (b + 1 - NT + START))
            act.activation(packed[:, b, :], psum[:, b, :], ACT.Copy).then_inc(s_bfree, 1)

        def high_digit(act, g, b):
            act.wait_ge(s_bfree, g * NT + (b + 1 + START))
            act.wait_ge(s_add, g * NT + (b + 1 - NT + START))
            act.activation(digits[:, b, HALF:N], packed[:, b, :], ACT.Relu, scale=-1.0 / DIGIT,
                           bias=half_col[:]).then_inc(s_high, 1)

        def low_digit(dve, g, b):
            dve.wait_ge(s_high, g * NT + (b + 1 + START))
            dve.scalar_tensor_tensor(out=digits[:, b, 0:HALF], in0=digits[:, b, HALF:N], scalar=float(DIGIT),
                                     in1=packed[:, b, :], op0=ALU.mult, op1=ALU.add).then_inc(s_low, 1)

        def add_counts(dve, g, b):
            dve.wait_ge(s_low, g * NT + (b + 1 + START))
            dve.wait_ge(s_add, g * NT + (b + 1 - NT + START))
            dve.tensor_tensor(ct[:, b, :], ct[:, b, :], digits[:, b, :], ALU.add).then_inc(s_add, 1)

        def keep_mask(eng, t):
            eng.wait_ge(s_mp, t + 1)
            turned = psum[:, t % 6, :].bitcast(BF16)
            if t % 2 == 0:
                eng.activation(mask[:, t, :], turned, ACT.Copy, scale=-FAR, bias=FAR).then_inc(s_mk[0], 1)
            else:
                eng.tensor_scalar(mask[:, t, :], turned, -FAR, FAR, ALU.mult, ALU.add).then_inc(s_mk[1], 1)

        @block.sync
        def _(sp):
            sp.dma_start(edge_i[:, 0, :], src.rearrange("(p c) -> p c", p=P)).then_inc(s_edges, 16)
            sp.dma_start(edge_i[:, 1, :], dst.rearrange("(p c) -> p c", p=P)).then_inc(s_edges, 16)
            sp.dma_start(xt[:], x.rearrange("(t p) d -> p t d", p=P)).then_inc(s_x, 16)
            sp.dma_start(b1r[:], env["b1"].rearrange("(c p) -> c p", p=P)).then_inc(s_b1, 16)
            for s in (*s_a, *s_w):
                sp.sem_inc(s, START)
            with sp.Fori(0, NG) as g:
                for i in range(HG):
                    h = sp.snap(g * HG + i)
                    sp.wait_ge(s_v, g * (2 * KT * HG) + (2 * KT * (i - HG + 1) + START))
                    sp.sem_inc(s_turn, 1)
                    sp.dma_start(arow[:, i, 0, :], a_s1[bass.ds(h, 1), :].to_broadcast([P, D])).then_inc(s_a[i], 16)
                    sp.dma_start(arow[:, i, 1, :], a_d1[bass.ds(h, 1), :].to_broadcast([P, D])).then_inc(s_a[i], 16)
                    for k in range(KT):
                        sp.wait_ge(s_v, g * (2 * KT * HG) + (2 * KT * (i - 1) + 2 * (k + 1) + START))
                        sp.sem_inc(s_turn, 1)
                        sp.dma_start(wv[:, k, :], W1v[:, k, bass.ds(h, 1), :]).then_inc(s_w[k], 16)
            sp.wait_ge(s_lg, 2)
            sp.dma_start(logit_rows, lg[:]).then_inc(s_out, 16)
            for hf in range(2):
                for n in range(2):
                    sp.wait_ge(s_mk[n], (hf + 1) * (NT // 4))
                tiles = slice(hf * (NT // 2), (hf + 1) * (NT // 2))
                sp.dma_start(mask_dram[hf], mask[:, tiles, :]).then_inc(s_mout, 16)
            sp.wait_ge(s_out, 16)
            sp.wait_ge(s_mout, 32)

        @block.gpsimd
        def _(pool):
            pool.memset(half_col[:], 0.5 - 0.75 / DIGIT).then_inc(s_iota, 1)
            pool.iota(iota[:], pattern=[[1, N]], base=0, channel_multiplier=0,
                      allow_small_or_imprecise_dtypes=True).then_inc(s_iota, 1)
            pool.memset(ct[:], 0).then_inc(s_iota, 1)
            pool.memset(ident[:], 0.0).then_inc(s_ident, 1)
            pool.wait_ge(s_ident, 1)
            pool.affine_select(out=ident[:], in_=ident[:], compare_op=ALU.not_equal, fill=1.0, base=0,
                               pattern=[[-1, P]], channel_multiplier=1).then_inc(s_ident, 1)
            pool.wait_ge(s_ident, 2)
            pool.tensor_copy(ident_b[:], ident[:]).then_inc(s_ident, 1)
            pool.sem_inc(s_xlo, START)
            with pool.Fori(0, NG) as g:
                for i in range(HG):
                    pool.wait_ge(s_xhi, g * HG + (i + 1 + START))
                    tile = bass.ds(g * HG + i, 1)
                    pool.tensor_tensor(xl[:, tile, :], xt[:, tile, :], xh[:, tile, :], ALU.subtract)\
                        .then_inc(s_xlo, 1)

        @block.vector
        def _(dve):
            for b in range(NT):
                dve.memset(psum[:, b, :], 0.0).then_inc(s_bank, 1)
            dve.wait_ge(s_edges, 32)
            dve.tensor_copy(edge_f[:, 0, :], edge_i[:, 0, :]).then_inc(s_prep, 1)
            dve.tensor_scalar(dst_low[:], edge_i[:, 1, :], HALF - 1, None, ALU.bitwise_and).then_inc(s_prep, 1)
            dve.wait_ge(s_prep, 1)
            dve.tensor_scalar(edge_i[:, 0, :], edge_i[:, 1, :], HALF.bit_length() - 1, None,
                              ALU.logical_shift_right).then_inc(s_prep, 1)
            dve.wait_ge(s_prep, 3)
            dve.tensor_copy(edge_f[:, 1, :], dst_low[:]).then_inc(s_prep, 1)
            dve.tensor_scalar(edge_f[:, 2, :], edge_i[:, 0, :], -float(DIGIT + 1), 1.0, ALU.mult,
                              ALU.add).then_inc(s_prep, 1)
            dve.wait_ge(s_iota, 3)
            dve.wait_ge(s_prep, 5)
            for s in (s_hot, s_v, s_vc, s_low, s_add, s_ln, s_bank):
                dve.sem_inc(s, START)
            dve.wait_ge(s_x, 16)

            def w_sum(g, i, q):
                k, sd = q // 2, q % 2
                if q == 0:
                    dve.wait_ge(s_a[i], g * 32 + (32 + START))
                    dve.wait_ge(s_vc, g * HG + (i + START))
                dve.wait_ge(s_w[k], g * (16 * HG) + (16 * (i + 1) + START))
                dve.wait_ge(s_v, g * (2 * KT * HG) + (2 * KT * i + q - 1 + START))
                dve.tensor_tensor_reduce(junk[:, q % 2, :], wv[:, k, :], arow[:, i, sd, :], 1.0, 0.0,
                                         ALU.mult, ALU.add, vsum[:, q:q + 1]).then_inc(s_v, 1)

            def keep_sums(g, i):
                parts = vsum[:].rearrange("p (k s) -> p k s", s=2)
                dve.wait_ge(s_v, g * (2 * KT * HG) + (2 * KT * (i + 1) + START))
                dve.tensor_copy(V[:, :, bass.ds(g * HG + i, 1)], parts[:, :, 0:1])
                dve.tensor_copy(V[:, :, bass.ds(g * HG + (i + H), 1)], parts[:, :, 1:2]).then_inc(s_vc, 1)

            def ln_step(g, n):
                c = [root[:, i, :] for i in range(7)]

                def behind(m):
                    dve.wait_ge(s_ln, g * LN + (m + 1 + START))
                if n < 2 * HG:
                    if n == 0:
                        dve.wait_ge(s_ln, g * LN + START)
                    i, part = n // 2, n % 2
                    ins = dve.bn_stats(stats[:, i, part, :], xt[:, bass.ds(g * HG + i, 1),
                                                                part * (D // 2):(part + 1) * (D // 2)]
                                       .rearrange("p o d -> p (o d)"))
                elif n < 3 * HG:
                    i = n - 2 * HG
                    behind(2 * HG - 1)
                    dve.wait_ge(s_xhi, g * HG + START)
                    dve.sem_inc(s_lnturn, 1)
                    ins = dve.bn_aggr(mv[:, i, :], stats[:, i, :, :].rearrange("p a b -> p (a b)"))
                else:
                    behind(n - 1)
                    m = n - 3 * HG
                    if m == 0:
                        ins = dve.tensor_scalar(c[6], mv[:, :, 0:1].rearrange("p t o -> p (t o)"), -1.0, None,
                                                ALU.mult)
                    elif m == 1:
                        ins = dve.tensor_scalar(c[0], mv[:, :, 1:2].rearrange("p t o -> p (t o)"), EPS_LN, None,
                                                ALU.add)
                    elif m == 2:
                        dve.wait_ge(s_root, g + (1 + START))
                        ins = dve.reciprocal(c[2], c[1])
                    elif m == 3:
                        ins = dve.tensor_tensor(c[3], c[0], c[2], ALU.mult)
                    elif m == 4:
                        ins = dve.tensor_tensor(c[4], c[1], c[3], ALU.add)
                    elif m == 5:
                        ins = dve.tensor_scalar(c[3], c[4], 0.5 / XS, None, ALU.mult)
                    else:
                        ins = dve.reciprocal(c[5], c[3])
                ins.then_inc(s_ln, 1)

            with dve.Fori(0, NG) as g:
                c0 = dve.snap(g * CG)
                for j in range(CG):
                    if j == RING - 1:
                        dve.wait_ge(s_bank, g * NT + (NT + START))
                    else:
                        n = j + 1 - RING if j >= RING else j + 2 - RING
                        dve.wait_ge(s_used, g * (CG - 1) + (n + START))
                    dve.tensor_scalar(src_hot[:, j % RING, :], iota[:], edge_f[:, 0, bass.ds(c0 + j, 1)], None,
                                      ALU.is_equal).then_inc(s_hot, 1)
                    dve.tensor_scalar(dst_hot[:, j % RING, :], iota[:, 0:HALF], edge_f[:, 1, bass.ds(c0 + j, 1)],
                                      edge_f[:, 2, bass.ds(c0 + j, 1)], ALU.is_equal, ALU.mult).then_inc(s_hot, 1)
                    if j in LOW_AT:
                        b = LOW_AT.index(j)
                        low_digit(dve, g, b)
                        if b >= 1:
                            add_counts(dve, g, b - 1)
                    else:
                        i, q = divmod(SUM_AT.index(j), 2 * KT)
                        w_sum(g, i, q)
                        if q == 2 * KT - 1:
                            keep_sums(g, i)
                    if LN0 <= j < LN0 + LN:
                        ln_step(g, j - LN0)
                add_counts(dve, g, NT - 1)
            for b in range(NT):
                low_digit(dve, NG, b)
                if b >= 1:
                    add_counts(dve, NG, b - 1)
                    dve.wait_ge(s_add, NG * NT + b + START)
                    dve.tensor_scalar(near[:, b - 1, :], ct[:, b - 1, :], 1.0, None, ALU.min).then_inc(s_near, 1)
            add_counts(dve, NG, NT - 1)
            dve.wait_ge(s_add, (NG + 1) * NT + START)
            dve.tensor_scalar(near[:, NT - 1, :], ct[:, NT - 1, :], 1.0, None, ALU.min).then_inc(s_near, 1)

            dve.wait_ge(s_lcp, 1)
            dve.tensor_scalar(lc[:].rearrange("p t c -> p (t c)"), psum[:, 6, 0:NT * 2 * H], 1.0 / XS, None,
                              ALU.mult).then_inc(s_lc, 1)
            dve.tensor_copy(b1c[:], psum[:, 6, P:P + H * KT])
            dve.wait_ge(s_lc, 1)
            dve.tensor_scalar(lc02[:].rearrange("p t c -> p (t c)"), lc[:].rearrange("p t c -> p (t c)"),
                              SLOPE, None, ALU.mult).then_inc(s_lc, 1)
            for nh in range(2):
                dve.wait_ge(s_lgp, nh + 1)
                dve.tensor_copy(lg[:, nh * 512:(nh + 1) * 512], psum[0:H, 6 + nh, :]).then_inc(s_lg, 1)
            for t in range(1, NT, 2):
                keep_mask(dve, t)
            dve.wait_ge(s_lc, 2)

        @block.scalar
        def _(act):
            for s in (s_bfree, s_high, s_xhi, s_root, s_xn, s_xr):
                act.sem_inc(s, START)
            act.wait_ge(s_iota, 1)
            with act.Fori(0, NG) as g:
                for b in range(NT):
                    keep_bank(act, g, b)
                for b in range(NT):
                    high_digit(act, g, b)
                act.wait_ge(s_ln, g * LN + (3 * HG + 2 + START))
                act.activation(root[:, 1, :], root[:, 0, :], ACT.Sqrt).then_inc(s_root, 1)
                act.wait_ge(s_ln, g * LN + (LN + START))
                act.sem_inc(s_xturn, 1)
                for i in range(HG):
                    tile = bass.ds(g * HG + i, 1)
                    act.activation(xt[:, tile, :], xt[:, tile, :], ACT.Identity, bias=root[:, 6, i:i + 1])\
                        .then_inc(s_xn, 1)
                for i in range(HG):
                    tile = bass.ds(g * HG + i, 1)
                    act.wait_ge(s_xn, g * HG + (i + 1 + START))
                    act.sem_inc(s_xturn, 1)
                    act.activation(xt[:, tile, :], xt[:, tile, :], ACT.Relu, scale=root[:, 5, i:i + 1])\
                        .then_inc(s_xr, 1)
                for i in range(HG):
                    tile = bass.ds(g * HG + i, 1)
                    act.wait_ge(s_xr, g * HG + (i + 1 + START))
                    act.sem_inc(s_xturn, 1)
                    act.activation(xh[:, tile, :], xt[:, tile, :], ACT.Copy).then_inc(s_xhi, 1)
            keep_bank(act, NG, 0)
            for b in range(NT):
                if b + 1 < NT:
                    keep_bank(act, NG, b + 1)
                high_digit(act, NG, b)
            for i in range(2 * KT):
                k, nh = i // 2, i % 2
                act.wait_ge(s_xTp, i + 1)
                act.activation(xT[:, k, nh * 512:(nh + 1) * 512], psum[:, i % 6, :], ACT.Copy).then_inc(s_xT, 1)
            for t in range(0, NT, 2):
                keep_mask(act, t)

        @block.tensor
        def _(pe):
            pe.sem_inc(s_used, START)
            with pe.Fori(0, NG) as g:
                for j in range(CG):
                    pe.wait_ge(s_hot, g * (2 * CG) + (2 * j + 2 + START))
                    for b in range(NT):
                        if j == 0:
                            pe.wait_ge(s_bfree, g * NT + (b + 1 + START))
                        mm = pe.matmul(psum[:, b, :], src_hot[:, j % RING, b * P:(b + 1) * P],
                                       dst_hot[:, j % RING, :], start=(j == 0), stop=(j == CG - 1))
                        if j == CG - 1:
                            mm.then_inc(s_bank, 1)
                    if j < CG - 1:
                        mm.then_inc(s_used, 1)
            pe.wait_ge(s_ident, 3)
            pe.wait_ge(s_xr, HG * NG + START)
            for i in range(2 * KT):
                k, nh = i // 2, i % 2
                if i >= 6:
                    pe.wait_ge(s_xT, i - 5)
                else:
                    pe.wait_ge(s_bfree, NT * NG + i + 1 + START)
                for q in range(4):
                    mm = pe.transpose(psum[:, i % 6, q * P:(q + 1) * P], xt[:, 4 * nh + q, k * P:(k + 1) * P],
                                      ident[:])
                mm.then_inc(s_xTp, 1)
            pe.wait_ge(s_vc, H + START)
            pe.wait_ge(s_bfree, NT * (NG + 1) + START)
            for t in range(NT):
                for k in range(KT):
                    if t % 4 == 0:
                        pe.wait_ge(s_xT, 2 * k + t // 4 + 1)
                    mm = pe.matmul(psum[:, 6, t * 2 * H:(t + 1) * 2 * H], xT[:, k, t * P:(t + 1) * P], V[:, k, :],
                                   start=(k == 0), stop=(k == KT - 1))
            pe.wait_ge(s_b1, 16)
            pe.transpose(psum[:, 6, P:P + H * KT], b1r[:], ident[0:H * KT, 0:H * KT]).then_inc(s_lcp, 1)
            pe.wait_ge(s_xT, 2 * KT)
            for t in range(NT):
                if t == 4:
                    pe.wait_ge(s_lc, 2)
                    for n in range(NT):
                        mm = pe.transpose(psum[0:H, 6 + n // 4, (n % 4) * P:(n % 4 + 1) * P], lc[:, n, 0:H], ident[:])
                        if n % 4 == 3:
                            mm.then_inc(s_lgp, 1)
                if t >= 6:
                    pe.wait_ge(s_mk[t % 2], (t - 6) // 2 + 1)
                turned = psum[:, t % 6, :].bitcast(BF16)
                for s in range(NT):
                    if t == 0:
                        pe.wait_ge(s_near, s + 1)
                    mm = pe.transpose(turned[:, s * P:(s + 1) * P], near[:, s, t * P:(t + 1) * P], ident_b[:])
                mm.then_inc(s_mp, 1)


def rstd_steps(dve, mv, root, s_ln, done, s_root, roots=1, cols=slice(None)):
    r = [root[:, i, cols] for i in range(6)]
    dve.wait_ge(s_ln, done)
    dve.tensor_scalar(r[0], mv[:, cols, 1:2].rearrange("p t o -> p (t o)"), EPS_LN, None, ALU.add).then_inc(s_ln, 1)
    dve.wait_ge(s_root, roots)
    dve.reciprocal(r[2], r[1]).then_inc(s_ln, 1)
    dve.wait_ge(s_ln, done + 2)
    dve.tensor_tensor(r[3], r[0], r[2], ALU.mult).then_inc(s_ln, 1)
    dve.wait_ge(s_ln, done + 3)
    dve.scalar_tensor_tensor(out=r[4], in0=r[1], scalar=1.0, in1=r[3], op0=ALU.mult, op1=ALU.add).then_inc(s_ln, 1)
    dve.wait_ge(s_ln, done + 4)
    dve.tensor_scalar(r[3], r[4], 0.5, None, ALU.mult).then_inc(s_ln, 1)
    dve.wait_ge(s_ln, done + 5)
    dve.reciprocal(r[5], r[3]).then_inc(s_ln, 1)
    return done + 6


def heads(nc, env):
    W1, W2, b1c = env["W1"], env["W2"], env["b1c"]
    xh, xl, ct, lc, lc02 = (env[k] for k in ("xh", "xl", "ct", "lc", "lc02"))
    logit_rows, mask_dram, ab_dram, h2_dram = (env[k] for k in ("logit_rows", "mask_dram", "ab_dram", "h2_dram"))
    D = W2.shape[1]
    H = W1.shape[1] // D
    N = ct.shape[2]
    NT, KT = N // P, D // P
    HALF = N // 2
    DT = HALF // P
    S = START

    with ExitStack() as ctx:
        def sb(name, shape, dt):
            return ctx.enter_context(nc.sbuf_tensor(name, shape, dt))

        sem = Sems(nc, ctx)
        h2ps = ctx.enter_context(nc.psum_tensor("h2ps", [P, 6, 512], F32))
        bank = [ctx.enter_context(nc.psum_tensor(f"bank{i}", [P, 512], F32)) for i in range(2)]
        ph = [sb(f"p_high{i}", [P, NT, HALF], F16) for i in range(2)]
        pl = [sb(f"p_low{i}", [P, NT, HALF], F16) for i in range(2)]
        zh = sb("z_high", [P, KT, HALF], F32R)
        zl = sb("z_low", [P, KT, HALF], F32R)
        w1r = sb("w1_raw", [P, 2, KT, P], F32)
        w1h = sb("w1_high", [P, 2, KT, P], F32R)
        w1l = sb("w1_low", [P, 2, KT, P], F32R)
        w2r = sb("w2_raw", [P, 2, D], F32)
        w2h = sb("w2_high", [P, 2, D], F32R)
        w2l = sb("w2_low", [P, 2, D], F32R)
        hh = sb("h_high", [P, 3, HALF], F32R)
        hl = sb("h_low", [P, 3, HALF], F32R)
        work = sb("work", [P, 6, HALF], F32)
        zt, ut, et = (work[:, 2 * i:2 * i + 2, :] for i in range(3))
        ab_rows = [sb(f"ab_rows{i}", [P, 2, HALF], F32) for i in range(2)]
        as_row = sb("as_row", [P, N], F32)
        mask = sb("mask_half", [P, DT, N], BF16)
        ta = sb("ta", [P, 2, HALF], F32)
        tb = sb("tb", [P, 2, HALF], F32)
        psums = sb("p_sums", [P, 2, HALF], F32)
        rden = sb("rden", [P, HALF], F32)
        den = sb("den", [P, HALF], F32)
        junk = sb("junk_m", [P, 2, N], BF16)
        top = sb("top", [P, 4, DT], F32)
        ab = [sb(f"ab{i}", [P, 2, DT], F32) for i in range(2)]
        b1u = [sb(f"b1u{i}", [P, KT], F32) for i in range(2)]
        ones = sb("ones", [P, P], F32)

        m_ones = sem("ones_made")
        m_mask = sem("mask_half_loaded")
        m_as = sem("as_row_loaded")
        m_top = sem("maxima_taken")
        m_sp = sem("sp_waits_over")
        m_small = sem("maxima_steps")
        m_turn = sem("maximum_begun")
        m_ab = sem("ab_columns_made")
        m_abs = sem("ab_columns_stored")
        m_abr = [sem(f"ab_rows_loaded{i}") for i in range(2)]
        m_b1 = sem("b1_columns_taken")
        m_terms = sem("exponent_terms_made")
        m_expo = sem("exponents_made")
        m_exp = sem("exponentials_made")
        m_p = sem("weights_made")
        m_ph = sem("weights_high")
        m_pl = sem("weights_low")
        m_sum = sem("weights_summed")
        m_sumturn = sem("weights_sum_begun")
        m_den = sem("denominator_ready")
        m_deneps = sem("denominator_kept")
        m_rden = sem("denominator_inverted")
        m_z = sem("z_ready")
        m_zt = sem("z_scaled")
        m_zh = sem("z_high_done")
        m_zl = sem("z_low_done")
        m_w1 = [sem(f"w1_loaded{i}") for i in range(2)]
        m_w2 = [sem(f"w2_loaded{i}") for i in range(2)]
        m_w1h, m_w1l = sem("w1_high_done"), sem("w1_low_done")
        m_w2h, m_w2l = sem("w2_high_done"), sem("w2_low_done")
        m_h = sem("h_ready")
        m_u = sem("h_biased")
        m_neg = sem("h_negative_part")
        m_eexp = sem("h_exp")
        m_elu = sem("h_elu")
        m_hh = sem("h_high_done")
        m_hl = sem("h_low_done")
        m_o = sem("h2_added")
        m_keep = sem("h2_half_copied")
        m_zero = sem("h2_zeroed")
        m_store = sem("h2_half_stored")
        block = ctx.enter_context(nc.Block())

        W1v = W1.rearrange("(k p) (c j) -> p k c j", p=P, j=P)
        W2v = W2.rearrange("(c p) d -> p c d", p=P)


        def counter(eng, u0):
            cache = {}

            def at(j, per, n):
                if isinstance(u0, int):
                    return (u0 + j) * per + n + S
                if per not in cache:
                    cache[per] = eng.snap(u0 * per)
                return cache[per] + (j * per + n + S)
            return at

        def load_stats(sp, v):
            hv, fv = (sp.snap(n) if not isinstance(v, int) else n for n in (v % H, (v // H) % 2))
            sp.wait_ge(m_top, v * DT + S)
            sp.sem_inc(m_sp, 1)
            sp.dma_start(as_row[:], logit_rows[bass.ds(hv, 1), :].to_broadcast([P, N])).then_inc(m_as, 16)
            sp.dma_start(mask[:], mask_dram[bass.ds(fv, 1), :, :, :]).then_inc(m_mask, 16)

        def spread(sp, v, par):
            sp.wait_ge(m_ab, v + (1 + S))
            sp.sem_inc(m_sp, 1)
            sp.wait_ge(m_terms, v * NT + (S - NT))
            sp.sem_inc(m_sp, 1)
            sp.dma_start(ab_dram[par].rearrange("a (t p) -> p a t", p=P), ab[par][:],
                         allow_slow_non_contiguous=True).then_inc(m_abs, 16)
            sp.wait_ge(m_abs, v * 16 + (16 + S))
            sp.sem_inc(m_sp, 1)
            sp.dma_start(ab_rows[par][:], ab_dram[par].partition_broadcast(P)).then_inc(m_abr[par], 16)

        def maxima(dve, v, par):
            hv, tv = (dve.snap(n) if not isinstance(v, int) else n for n in (v % H, ((v // H) % 2) * DT))
            dve.wait_ge(m_as, v * 16 + (16 + S))
            dve.wait_ge(m_mask, v * 16 + (16 + S))
            dve.wait_ge(m_ab, v + S)
            for t in range(DT):
                dve.wait_ge(m_top, v * DT + (t - 1 + S))
                dve.sem_inc(m_turn, 1)
                dve.tensor_tensor_reduce(junk[:, t % 2, :], mask[:, t, :], as_row[:], 1.0, FAR, ALU.add,
                                         ALU.max, top[:, 0, t:t + 1]).then_inc(m_top, 1)
            ad = lc[:, bass.ds(tv, DT), bass.ds(hv + H, 1)].rearrange("p t o -> p (t o)")
            dve.wait_ge(m_top, v * DT + (DT + S))
            dve.tensor_tensor(top[:, 1, :], top[:, 0, :], ad, ALU.add).then_inc(m_small, 1)
            dve.wait_ge(m_small, v * 2 + (1 + S))
            dve.scalar_tensor_tensor(out=top[:, 2, :], in0=top[:, 1, :], scalar=SLOPE, in1=top[:, 1, :],
                                     op0=ALU.mult, op1=ALU.max).then_inc(m_small, 1)
            dve.wait_ge(m_small, v * 2 + (2 + S))
            dve.wait_ge(m_abs, v * 16 + S)
            dve.tensor_tensor(ab[par][:, 0, :], ad, top[:, 2, :], ALU.subtract)
            dve.scalar_tensor_tensor(out=ab[par][:, 1, :], in0=ad, scalar=SLOPE, in1=top[:, 2, :],
                                     op0=ALU.mult, op1=ALU.subtract).then_inc(m_ab, 1)

        def exponent_terms(dve, at, j, s, par, hv):
            if s == 0:
                dve.wait_ge(m_abr[par], at(j, 8, 8 if par else 16))
            dve.wait_ge(m_p, at(j, NT, s - 1))
            dve.tensor_scalar(ta[:, s % 2, :], ab_rows[par][:, 0, :], lc[:, s, bass.ds(hv, 1)], 0.0, ALU.add,
                              ALU.min)
            dve.wait_ge(m_pl, at(j, NT, s - 1))
            dve.wait_ge(m_sum, at(j, NT, s - 1))
            dve.tensor_scalar(tb[:, s % 2, :], ab_rows[par][:, 1, :], lc02[:, s, bass.ds(hv, 1)], 0.0, ALU.add,
                              ALU.min).then_inc(m_terms, 1)

        def exponent(dve, at, j, s):
            dve.wait_ge(m_terms, at(j, NT, s + 1))
            dve.tensor_tensor(ta[:, s % 2, :], ta[:, s % 2, :], tb[:, s % 2, :], ALU.max).then_inc(m_expo, 1)

        def weights(dve, at, j, s, tv):
            dve.wait_ge(m_exp, at(j, NT, s + 1))
            dve.tensor_tensor(tb[:, s % 2, :], ta[:, s % 2, :], ct[:, s, bass.ds(tv, HALF)],
                              ALU.mult).then_inc(m_p, 1)

        def weights_low(dve, at, j, s, par):
            dve.wait_ge(m_ph, at(j, NT, s + 1))
            dve.tensor_tensor(pl[par][:, s, :], tb[:, s % 2, :], ph[par][:, s, :], ALU.subtract).then_inc(m_pl, 1)

        def z_scaled(dve, at, j, k):
            dve.wait_ge(m_z, at(j, KT, k + 1))
            if k < 2:
                dve.wait_ge(m_zl, at(j, KT, 0))
                dve.wait_ge(m_rden, at(j, 1, 1))
            else:
                dve.wait_ge(m_zl, at(j, KT, k - 1))
            dve.tensor_tensor(zt[:, k % 2, :], bank[(k + 1) % 2][:], rden[:], ALU.mult).then_inc(m_zt, 1)

        def z_low(dve, at, j, k):
            dve.wait_ge(m_zh, at(j, KT, k + 1))
            dve.tensor_tensor(zl[:, k, :], zt[:, k % 2, :], f32(zh[:, k, :]), ALU.subtract).then_inc(m_zl, 1)

        def w1_low(dve, at, j, i):
            dve.wait_ge(m_w1h, at(j, KT, i + 1))
            dve.tensor_tensor(w1l[:, i % 2, :, :], w1r[:, i % 2, :, :], f32(w1h[:, i % 2, :, :]),
                              ALU.subtract).then_inc(m_w1l, 1)

        def w2_low(dve, at, j, i):
            dve.wait_ge(m_w2h, at(j, KT, i + 1))
            dve.tensor_tensor(w2l[:, i % 2, :], w2r[:, i % 2, :], f32(w2h[:, i % 2, :]),
                              ALU.subtract).then_inc(m_w2l, 1)

        def h_negative(dve, at, j, i):
            dve.wait_ge(m_u, at(j, KT, i + 1))
            dve.wait_ge(m_hl, at(j, KT, i - 1))
            dve.tensor_scalar(et[:, i % 2, :], ut[:, i % 2, :], 0.0, None, ALU.min).then_inc(m_neg, 1)

        def h_elu(dve, at, j, i):
            dve.wait_ge(m_eexp, at(j, KT, i + 1))
            dve.scalar_tensor_tensor(out=et[:, i % 2, :], in0=et[:, i % 2, :], scalar=-1.0, in1=ut[:, i % 2, :],
                                     op0=ALU.add, op1=ALU.max).then_inc(m_elu, 1)

        def h_low(dve, at, j, i):
            dve.wait_ge(m_hh, at(j, KT, i + 1))
            dve.tensor_tensor(hl[:, i % 3, :], et[:, i % 2, :], f32(hh[:, i % 3, :]), ALU.subtract).then_inc(m_hl, 1)

        def exponential(act, at, j, s):
            act.wait_ge(m_expo, at(j, NT, s + 1))
            act.activation(ta[:, s % 2, :], ta[:, s % 2, :], ACT.Exp).then_inc(m_exp, 1)

        def weights_high(act, at, j, s, par):
            act.wait_ge(m_p, at(j, NT, s + 1))
            if s == 0:
                act.wait_ge(m_z, at(j, KT, -KT))
            act.activation(ph[par][:, s, :], tb[:, s % 2, :], ACT.Copy).then_inc(m_ph, 1)

        def z_high(act, at, j, k):
            act.wait_ge(m_zt, at(j, KT, k + 1))
            if k == 0:
                act.wait_ge(m_h, at(j, KT, 0))
            act.activation(zh[:, k, :], zt[:, k % 2, :], ACT.Copy).then_inc(m_zh, 1)

        def w1_high(act, at, j, i):
            act.wait_ge(m_w1[i % 2], at(j, 8 * KT, 16 * (i // 2 + 1)))
            act.wait_ge(m_h, at(j, KT, i - 1))
            act.activation(w1h[:, i % 2, :, :], w1r[:, i % 2, :, :], ACT.Copy).then_inc(m_w1h, 1)

        def w2_high(act, at, j, i):
            act.wait_ge(m_w2[i % 2], at(j, 8 * KT, 16 * (i // 2 + 1)))
            act.wait_ge(m_o, at(j, KT, i - 1))
            act.activation(w2h[:, i % 2, :], w2r[:, i % 2, :], ACT.Copy).then_inc(m_w2h, 1)

        def h_biased(act, at, j, i):
            act.wait_ge(m_h, at(j, KT, i + 1))
            if i == 0:
                act.wait_ge(m_b1, at(j, 1, 1))
            act.wait_ge(m_elu, at(j, KT, i - 1))
            act.activation(ut[:, i % 2, :], bank[(i + 1) % 2][:], ACT.Identity, bias=b1u[j][:, i:i + 1]).then_inc(m_u, 1)

        def h_exp(act, at, j, i):
            act.wait_ge(m_neg, at(j, KT, i + 1))
            act.activation(et[:, i % 2, :], et[:, i % 2, :], ACT.Exp).then_inc(m_eexp, 1)

        def h_high(act, at, j, i):
            act.wait_ge(m_elu, at(j, KT, i + 1))
            act.wait_ge(m_o, at(j, KT, i - 2))
            act.activation(hh[:, i % 3, :], et[:, i % 2, :], ACT.Copy).then_inc(m_hh, 1)

        W1_AT = {0: 0, 1: 1, 7: 2, 8: 3, 9: 4, 10: 5}
        W2_AT = {0: 0, 1: 1, 9: 2, 10: 3, 11: 4, 12: 5}
        P_AT = {2: 0, 3: 1, 4: 2, 5: 3, 8: 4, 9: 5, 10: 6, 11: 7}
        MAXIMA_AT = 13
        STEPS = range(14)

        @block.sync
        def _(sp):
            for s in (m_as, m_mask, m_abs, *m_abr, *m_w1, *m_w2, m_store):
                sp.sem_inc(s, S)
            for i in range(2):
                sp.dma_start(w1r[:, i, :, :], W1v[:, :, i, :]).then_inc(m_w1[i], 16)
                sp.dma_start(w2r[:, i, :], W2v[:, i, :]).then_inc(m_w2[i], 16)
            load_stats(sp, 0)
            spread(sp, 0, 0)
            load_stats(sp, 1)
            with sp.Fori(0, 2 * H, H) as half:
                with sp.Fori(0, H, 2) as pair:
                    u0 = sp.snap(half + pair)
                    at = counter(sp, u0)
                    for j in range(2):
                        u = sp.snap(u0 + j)
                        head = sp.snap(u % H)
                        tile0 = sp.snap(head * KT)
                        next0 = sp.snap(((u + 1) % H) * KT)

                        behind = [sp.snap(tile0 + (i + 2) if i < KT - 2 else next0 + (i + 2 - KT))
                                  for i in range(KT)]

                        def tile(i):
                            return bass.ds(behind[i], 1)
                        spread(sp, u + 1, (j + 1) % 2)
                        load_stats(sp, u + 2)
                        for t in STEPS:
                            if t in W1_AT:
                                sp.wait_ge(m_w1l, at(j, KT, W1_AT[t] + 1))
                                sp.sem_inc(m_sp, 1)
                                sp.dma_start(w1r[:, W1_AT[t] % 2, :, :], W1v[:, :, tile(W1_AT[t]), :])\
                                    .then_inc(m_w1[W1_AT[t] % 2], 16)
                            if t in W2_AT:
                                sp.wait_ge(m_w2l, at(j, KT, W2_AT[t] + 1))
                                sp.sem_inc(m_sp, 1)
                                sp.dma_start(w2r[:, W2_AT[t] % 2, :], W2v[:, tile(W2_AT[t]), :])\
                                    .then_inc(m_w2[W2_AT[t] % 2], 16)
                hn = sp.snap(half // H)
                sp.wait_ge(m_keep, hn * 6 + (6 + S))
                sp.sem_inc(m_sp, 1)
                sp.dma_start(h2_dram[bass.ds(hn, 1), :, :, :], work[:]).then_inc(m_store, 16)
            sp.wait_ge(m_store, 32 + S)
            sp.wait_ge(m_abs, 16 * (2 * H + 1) + S)
            sp.wait_ge(m_as, 16 * (2 * H + 2) + S)
            sp.wait_ge(m_mask, 16 * (2 * H + 2) + S)
            sp.wait_ge(m_abr[0], 16 * (H + 1) + S)
            for i in range(2):
                sp.wait_ge(m_w1[i], 16 * (KT * H + 1) + S)
                sp.wait_ge(m_w2[i], 16 * (KT * H + 1) + S)

        @block.gpsimd
        def _(pool):
            pool.memset(ones[:], 1.0).then_inc(m_ones, 1)
            pool.sem_inc(m_sum, S)

            def add(at, j, s, par):
                pool.wait_ge(m_p, at(j, NT, s + 1))
                if s == 0:
                    pool.sem_inc(m_sumturn, 1)
                    pool.wait_ge(m_den, at(j, 1, -1))
                    pool.sem_inc(m_sumturn, 1)
                    pool.tensor_copy(psums[:, par, :], tb[:, 0, :]).then_inc(m_sum, 1)
                else:
                    pool.wait_ge(m_sum, at(j, NT, s))
                    pool.tensor_tensor(psums[:, par, :], psums[:, par, :], tb[:, s % 2, :], ALU.add).then_inc(m_sum, 1)

            at = counter(pool, 0)
            for s in range(NT):
                add(at, 0, s, 0)
            with pool.Fori(0, 2 * H, 2) as u0:
                at = counter(pool, u0)
                for j in range(2):
                    for s in range(NT):
                        add(at, j + 1, s, (j + 1) % 2)

        @block.vector
        def _(dve):
            for s in (m_top, m_small, m_ab, m_terms, m_expo, m_p, m_pl, m_deneps, m_rden, m_zt, m_zl, m_w1l,
                      m_w2l, m_neg, m_elu, m_hl, m_keep, m_zero, m_b1):
                dve.sem_inc(s, S)
            for b in range(6):
                dve.memset(h2ps[:, b, :], 0.0).then_inc(m_zero, 1)
            maxima(dve, 0, 0)
            at = counter(dve, 0)
            for s in range(NT + 1):
                if s < NT:
                    exponent_terms(dve, at, 0, s, 0, 0)
                    exponent(dve, at, 0, s)
                if s >= 1:
                    weights(dve, at, 0, s - 1, 0)
                    weights_low(dve, at, 0, s - 1, 0)
            maxima(dve, 1, 1)
            with dve.Fori(0, 2 * H, H) as half:
                with dve.Fori(0, H, 2) as pair:
                    u0 = dve.snap(half + pair)
                    at = counter(dve, u0)
                    for j in range(2):
                        v = dve.snap(u0 + (j + 1))
                        hv = dve.snap(v % H)
                        tv = dve.snap(((v // H) % 2) * HALF)
                        par = (j + 1) % 2
                        for t in STEPS:
                            k, i, s = t - 1, t - 7, P_AT.get(t)
                            low = P_AT.get(t - 1)
                            if t == 0:
                                dve.wait_ge(m_den, at(j, 1, 1))
                                dve.wait_ge(m_rden, at(j, 1, 0))
                                dve.tensor_scalar(den[:], bank[0][:], EPS_DEN, XS, ALU.add, ALU.mult)\
                                    .then_inc(m_deneps, 1)
                                dve.wait_ge(m_deneps, at(j, 1, 1))
                                dve.wait_ge(m_zt, at(j, KT, 0))
                                dve.reciprocal(rden[:], den[:]).then_inc(m_rden, 1)
                                dve.wait_ge(m_u, at(j, KT, -KT))
                                dve.tensor_copy(b1u[j][:], b1c[:, bass.ds(dve.snap(((u0 + j) % H) * KT), KT)])\
                                    .then_inc(m_b1, 1)
                            if 0 <= k < KT:
                                if k == 0:
                                    dve.wait_ge(m_store, (half // H) * 16 + S)
                                z_scaled(dve, at, j, k)
                            if 0 <= i < KT:
                                h_negative(dve, at, j, i)
                            if low is not None:
                                weights_low(dve, at, j + 1, low, par)
                            if s is not None:
                                exponent_terms(dve, at, j + 1, s, par, hv)
                            if 0 <= i < KT:
                                h_elu(dve, at, j, i)
                            if s is not None:
                                exponent(dve, at, j + 1, s)
                            if 0 <= k < KT:
                                z_low(dve, at, j, k)
                            if 0 <= i < KT:
                                h_low(dve, at, j, i)
                            if t in W1_AT:
                                w1_low(dve, at, j, W1_AT[t])
                            if s is not None:
                                weights(dve, at, j + 1, s, tv)
                            if t in W2_AT:
                                w2_low(dve, at, j, W2_AT[t])
                            if t == MAXIMA_AT:
                                maxima(dve, dve.snap(u0 + (j + 2)), j)
                hn = dve.snap(half // H)
                dve.wait_ge(m_o, half * KT + (H * KT + S))
                dve.wait_ge(m_hl, half * KT + (H * KT + S))
                for b in range(3, 6):
                    dve.tensor_copy(work[:, b, :], h2ps[:, b, :]).then_inc(m_keep, 1)
                dve.wait_ge(m_keep, hn * 6 + (6 + S))
                for b in range(6):
                    dve.memset(h2ps[:, b, :], 0.0).then_inc(m_zero, 1)

        @block.scalar
        def _(act):
            for s in (m_exp, m_ph, m_zh, m_w1h, m_w2h, m_u, m_eexp, m_hh):
                act.sem_inc(s, S)
            at = counter(act, 0)
            for s in range(NT + 1):
                if s < NT:
                    exponential(act, at, 0, s)
                if s >= 1:
                    weights_high(act, at, 0, s - 1, 0)
            with act.Fori(0, 2 * H, H) as half:
                with act.Fori(0, H, 2) as pair:
                    u0 = act.snap(half + pair)
                    at = counter(act, u0)
                    for j in range(2):
                        par = (j + 1) % 2
                        for t in STEPS:
                            k, i, s = t - 1, t - 7, P_AT.get(t)
                            if 0 <= i < KT:
                                h_biased(act, at, j, i)
                            if t in W1_AT:
                                w1_high(act, at, j, W1_AT[t])
                            if 0 <= k < KT:
                                z_high(act, at, j, k)
                            if 0 <= i < KT:
                                h_exp(act, at, j, i)
                            if t in W2_AT:
                                w2_high(act, at, j, W2_AT[t])
                            if 0 <= i < KT:
                                h_high(act, at, j, i)
                            if s is not None:
                                exponential(act, at, j + 1, s)
                            if s is not None:
                                weights_high(act, at, j + 1, s, par)
                act.wait_ge(m_o, half * KT + (H * KT + S))
                act.wait_ge(m_hl, half * KT + (H * KT + S))
                for b in range(3):
                    act.activation(work[:, b, :], h2ps[:, b, :], ACT.Copy).then_inc(m_keep, 1)

        @block.tensor
        def _(pe):
            for s in (m_den, m_z, m_h, m_o):
                pe.sem_inc(s, S)
            pe.wait_ge(m_ones, 1)

            def product(out, terms, **kw):
                for n, (a, b) in enumerate(terms):
                    mm = pe.matmul(out, a, b, start=(n == 0), stop=(n == len(terms) - 1), **kw)
                return mm

            def z_tile(at, j, k):
                if k == 0:
                    pass
                elif k == 1:
                    pe.wait_ge(m_deneps, at(j, 1, 1))
                else:
                    pe.wait_ge(m_zt, at(j, KT, k - 1))
                for s in range(NT):
                    if k == 0:
                        pe.wait_ge(m_pl, at(j, NT, s + 1))
                    kk = slice(k * P, (k + 1) * P)
                    for n, (a, b) in enumerate(((xh, ph), (xh, pl), (xl, ph))):
                        mm = pe.matmul(bank[(k + 1) % 2][:], a[:, s, kk], b[j][:, s, :], start=(s == 0 and n == 0),
                                       stop=(s == NT - 1 and n == 2))
                mm.then_inc(m_z, 1)

            def h_tile(at, j, i):
                pe.wait_ge(m_w1l, at(j, KT, i + 1))
                if i < 2:
                    pe.wait_ge(m_zt, at(j, KT, KT - 1 + i))
                else:
                    pe.wait_ge(m_u, at(j, KT, i - 1))
                for k in range(KT):
                    if i == 0:
                        pe.wait_ge(m_zl, at(j, KT, k + 1))
                    for n, (a, b) in enumerate(((w1h, zh), (w1h, zl), (w1l, zh))):
                        mm = pe.matmul(bank[(i + 1) % 2][:], a[:, i % 2, k, :], b[:, k, :], start=(k == 0 and n == 0),
                                       stop=(k == KT - 1 and n == 2))
                mm.then_inc(m_h, 1)

            def h2_tile(at, j, i, hn):
                pe.wait_ge(m_hl, at(j, KT, i + 1))
                pe.wait_ge(m_w2l, at(j, KT, i + 1))
                if j == 0 and i == 0:
                    pe.wait_ge(m_zero, hn * 6 + (6 + S))
                for a, b in ((hh, w2h), (hh, w2l), (hl, w2h)):
                    for t in range(DT):
                        at0 = t * D
                        while at0 < (t + 1) * D:
                            to = min((t + 1) * D, (at0 // 512 + 1) * 512)
                            mm = pe.matmul(h2ps[:, at0 // 512, at0 % 512:at0 % 512 + to - at0],
                                           a[:, i % 3, t * P:(t + 1) * P], b[:, i % 2, at0 - t * D:to - t * D],
                                           start=False, stop=True, skip_group_check=True)
                            at0 = to
                mm.then_inc(m_o, 1)

            with pe.Fori(0, 2 * H, H) as half:
                hn = pe.snap(half // H)
                with pe.Fori(0, H, 2) as pair:
                    u0 = pe.snap(half + pair)
                    at = counter(pe, u0)
                    for j in range(2):
                        pe.wait_ge(m_sum, at(j, NT, NT))
                        pe.matmul(bank[0][:], ones[:], psums[:, j, :], start=True, stop=True).then_inc(m_den, 1)
                        for k in range(KT):
                            z_tile(at, j, k)
                        h_tile(at, j, 0)
                        h_tile(at, j, 1)
                        for i in range(2, KT):
                            h_tile(at, j, i)
                            h2_tile(at, j, i - 2, hn)
                        h2_tile(at, j, KT - 2, hn)
                        h2_tile(at, j, KT - 1, hn)


def second_logits(nc, env):
    h2_dram, mask_dram, row_dram, row2_dram = (env[k] for k in ("h2_dram", "mask_dram", "row_dram", "row2_dram"))
    a_s2, a_d2 = env["a_s2"], env["a_d2"]
    ct, hh, hl, lc2, ab2, dinv = (env[k] for k in ("ct", "h2h", "h2l", "lc2", "ab2", "dinv"))
    NT, N = ct.shape[1], ct.shape[2]
    D = a_s2.shape[1]
    HT = NT // 2

    with ExitStack() as ctx:
        def sb(name, shape, dt):
            return ctx.enter_context(nc.sbuf_tensor(name, shape, dt))

        sem = Sems(nc, ctx)
        ps = ctx.enter_context(nc.psum_tensor("l2_ps", [P, 4, 512], F32))
        hraw = sb("h2_raw", [P, NT, D], F32)
        arow = sb("a2_rows", [P, 2, D], F32)
        junk = sb("junk2", [P, 2, N], BF16)
        mask = sb("mask2", [P, 2, HT, N], BF16)
        as_row = sb("as2_row", [P, N], F32)
        small = sb("small2", [P, 3, NT], F32)
        rows = sb("rows2", [2 * NT, P], F32)
        rows1 = sb("rows1", [NT, P], F32)
        ident = sb("ident2", [P, P], F32)
        cth = sb("ct_high", [P, 2, N], F16)
        ctl = sb("ct_low", [P, 2, N], F16)
        ones = sb("ones2", [P, 2], F16)
        zeros = sb("zeros2", [P, P], F16)
        deg = sb("deg", [P, 5, NT], F32)

        t_h = [sem(f"h2_loaded{i}") for i in range(2)]
        t_a = sem("a2_rows_loaded")
        t_mask = [sem(f"mask2_loaded{i}") for i in range(2)]
        t_c = sem("constants_made")
        t_sum = sem("a2_sums")
        t_hi = sem("h2_high_done")
        t_lo = sem("h2_low_done")
        t_turn = sem("columns_turned")
        t_rows = sem("rows_kept")
        t_dram = sem("rows_stored")
        t_back = sem("rows_back")
        t_max = sem("maxima2_taken")
        t_small = sem("small2_steps")
        t_cth = sem("ct_high_done")
        t_ctl = sem("ct_low_done")
        t_deg = sem("ct_tile_counted")
        t_root = sem("degree_root")
        t_dg = sem("degree_steps")
        block = ctx.enter_context(nc.Block())

        @block.sync
        def _(sp):
            for hf in range(2):
                sp.dma_start(hraw[:, hf * HT:(hf + 1) * HT, :].rearrange("p t d -> p (t d)"),
                             h2_dram[hf].rearrange("p b c -> p (b c)")).then_inc(t_h[hf], 16)
            sp.dma_start(arow[:, 0, :], a_s2.to_broadcast([P, D])).then_inc(t_a, 16)
            sp.dma_start(arow[:, 1, :], a_d2.to_broadcast([P, D])).then_inc(t_a, 16)
            for hf in range(2):
                sp.dma_start(mask[:, hf, :, :], mask_dram[hf]).then_inc(t_mask[hf], 16)
            sp.wait_ge(t_rows, 1)
            sp.dma_start(row_dram, rows1[:]).then_inc(t_dram, 16)
            sp.wait_ge(t_dram, 16)
            sp.dma_start(as_row[:], row_dram.rearrange("t p -> (t p)").partition_broadcast(P)).then_inc(t_back, 16)
            sp.wait_ge(t_rows, 2)
            sp.dma_start(row2_dram, rows[:]).then_inc(t_dram, 16)
            sp.wait_ge(t_dram, 32)

        @block.gpsimd
        def _(pool):
            pool.memset(ident[:], 0.0).then_inc(t_c, 1)
            pool.wait_ge(t_c, 1)
            pool.affine_select(out=ident[:], in_=ident[:], compare_op=ALU.not_equal, fill=1.0, base=0,
                               pattern=[[-1, P]], channel_multiplier=1).then_inc(t_c, 1)
            pool.memset(ones[:], 1.0).then_inc(t_c, 1)
            pool.memset(zeros[:], 0.0).then_inc(t_c, 1)

        @block.vector
        def _(dve):
            dve.wait_ge(t_a, 32)
            for t in range(NT):
                if t % HT == 0:
                    dve.wait_ge(t_h[t // HT], 16)
                for sd in range(2):
                    n = 2 * t + sd
                    if n >= 2:
                        dve.wait_ge(t_sum, n - 1)
                    dve.tensor_tensor_reduce(junk[:, sd, 0:D], hraw[:, t, :], arow[:, sd, :], 1.0, 0.0, ALU.mult,
                                             ALU.add, lc2[:, sd, t:t + 1]).then_inc(t_sum, 1)
                dve.wait_ge(t_cth, t + 1)
                if t >= 2:
                    dve.wait_ge(t_deg, t - 1)
                dve.tensor_tensor(ctl[:, t % 2, :], ct[:, t, :], cth[:, t % 2, :], ALU.subtract).then_inc(t_ctl, 1)
                dve.wait_ge(t_hi, t + 1)
                dve.tensor_tensor(hl[:, t, 0:D], hraw[:, t, :], f32(hh[:, t, 0:D]), ALU.subtract).then_inc(t_lo, 1)
            dve.wait_ge(t_sum, 2 * NT)
            dve.tensor_scalar(lc2[:, 2, :], lc2[:, 0, :], SLOPE, None, ALU.mult).then_inc(t_small, 1)
            dve.wait_ge(t_turn, 1)
            dve.tensor_copy(rows1[:], ps[0:NT, 0, 0:P]).then_inc(t_rows, 1)
            dve.wait_ge(t_deg, NT)
            dve.tensor_scalar(deg[:, 0, :], ps[:, 3, 0:2 * NT].rearrange("p (t o) -> p t o", o=2)[:, :, 0:1]
                              .rearrange("p t o -> p (t o)"), 1.0, None, ALU.add).then_inc(t_dg, 1)
            dve.wait_ge(t_root, 1)
            dve.reciprocal(deg[:, 2, :], deg[:, 1, :]).then_inc(t_dg, 1)
            dve.wait_ge(t_dg, 2)
            dve.tensor_tensor(deg[:, 3, :], deg[:, 0, :], deg[:, 2, :], ALU.mult).then_inc(t_dg, 1)
            dve.wait_ge(t_dg, 3)
            dve.tensor_tensor(deg[:, 4, :], deg[:, 3, :], deg[:, 1, :], ALU.add).then_inc(t_dg, 1)
            dve.wait_ge(t_dg, 4)
            dve.tensor_scalar(deg[:, 3, :], deg[:, 4, :], 0.5, None, ALU.mult).then_inc(t_dg, 1)
            dve.wait_ge(t_dg, 5)
            dve.reciprocal(dinv[:, 0, :], deg[:, 3, :]).then_inc(t_dg, 1)
            dve.wait_ge(t_dg, 6)
            dve.tensor_scalar(dinv[:, 1, :], dinv[:, 0, :], XS, None, ALU.mult)
            dve.tensor_scalar(dinv[:, 2, :], dinv[:, 0, :], 1.0 / XS, None, ALU.mult).then_inc(t_dg, 1)
            dve.wait_ge(t_back, 16)
            for t in range(NT):
                if t % HT == 0:
                    dve.wait_ge(t_mask[t // HT], 16)
                if t >= 2:
                    dve.wait_ge(t_max, t - 1)
                else:
                    dve.wait_ge(t_sum, 2 * NT)
                dve.tensor_tensor_reduce(junk[:, t % 2, :], mask[:, t // HT, t % HT, :], as_row[:], 1.0, FAR,
                                         ALU.add, ALU.max, small[:, 0, t:t + 1]).then_inc(t_max, 1)
            dve.wait_ge(t_max, NT)
            dve.tensor_tensor(small[:, 1, :], small[:, 0, :], lc2[:, 1, :], ALU.add).then_inc(t_small, 1)
            dve.wait_ge(t_small, 2)
            dve.scalar_tensor_tensor(out=small[:, 2, :], in0=small[:, 1, :], scalar=SLOPE, in1=small[:, 1, :],
                                     op0=ALU.mult, op1=ALU.max).then_inc(t_small, 1)
            dve.wait_ge(t_small, 3)
            dve.tensor_tensor(ab2[:, 0, :], lc2[:, 1, :], small[:, 2, :], ALU.subtract)
            dve.scalar_tensor_tensor(out=ab2[:, 1, :], in0=lc2[:, 1, :], scalar=SLOPE, in1=small[:, 2, :],
                                     op0=ALU.mult, op1=ALU.subtract).then_inc(t_small, 1)
            dve.wait_ge(t_turn, 2)
            dve.tensor_copy(rows[:], ps[0:2 * NT, 1, 0:P]).then_inc(t_rows, 1)

        @block.scalar
        def _(act):
            for t in range(NT):
                if t >= 2:
                    act.wait_ge(t_deg, t - 1)
                act.activation(cth[:, t % 2, :], ct[:, t, :], ACT.Copy).then_inc(t_cth, 1)
                if t % HT == 0:
                    act.wait_ge(t_h[t // HT], 16)
                act.activation(hh[:, t, 0:D], hraw[:, t, :], ACT.Copy).then_inc(t_hi, 1)
            act.wait_ge(t_c, 4)
            act.activation(hh[:, :, D:D + 2], ones[:].unsqueeze(1).to_broadcast([P, NT, 2]), ACT.Copy)
            act.activation(hl[:, :, D:D + 2], zeros[:, 0:2].unsqueeze(1).to_broadcast([P, NT, 2]), ACT.Copy)
            act.wait_ge(t_dg, 1)
            act.activation(deg[:, 1, :], deg[:, 0, :], ACT.Sqrt).then_inc(t_root, 1)

        @block.tensor
        def _(pe):
            pe.wait_ge(t_c, 4)
            pe.matmul(ps[:, 3, 0:2 * NT], zeros[:], zeros[:, 0:2 * NT], start=True, stop=False, skip_group_check=True)
            for s in range(NT):
                pe.wait_ge(t_ctl, s + 1)
                for part in (cth, ctl):
                    for t in range(NT):
                        mm = pe.matmul(ps[:, 3, 2 * t:2 * t + 2], part[:, s % 2, t * P:(t + 1) * P], ones[:],
                                       start=False, stop=True, skip_group_check=True)
                mm.then_inc(t_deg, 1)
            pe.wait_ge(t_sum, 2 * NT)
            pe.transpose(ps[0:NT, 0, 0:P], lc2[:, 0, :], ident[:]).then_inc(t_turn, 1)
            pe.wait_ge(t_small, 4)
            pe.transpose(ps[0:2 * NT, 1, 0:P], ab2[:].rearrange("p a t -> p (a t)"), ident[:]).then_inc(t_turn, 1)


def second_attention(nc, env):
    x, b2, row2_dram = env["x"], env["b2"], env["row2_dram"]
    ct, hh, hl, lc2, dinv, xt, mv = (env[k] for k in ("ct", "h2h", "h2l", "lc2", "dinv", "xt", "mv"))
    NT, N = ct.shape[1], ct.shape[2]
    D = x.shape[1]
    HT, HALF = NT // 2, N // 2

    with ExitStack() as ctx:
        def sb(name, shape, dt):
            return ctx.enter_context(nc.sbuf_tensor(name, shape, dt))

        sem = Sems(nc, ctx)
        ps = ctx.enter_context(nc.psum_tensor("a2_ps", [P, 8, 512], F32))
        ph = [sb(f"p2_high{i}", [P, NT, HALF], F32R) for i in range(2)]
        pl = [sb(f"p2_low{i}", [P, NT, HALF], F32R) for i in range(2)]
        ab_rows = sb("ab2_rows", [P, 2, N], F32)
        b2row = sb("b2_row", [P, D], F32)
        ta = sb("ta2", [P, 2, HALF], F32)
        tb = sb("tb2", [P, 2, HALF], F32)
        rd = sb("rd2", [P, 2, NT], F32)
        stats = sb("stats2", [P, NT, 2, 6], F32)
        root = sb("root2", [P, 6, NT], F32)

        t_ab = sem("ab2_rows_loaded")
        t_x = sem("x_back")
        t_b2 = sem("b2_loaded")
        t_terms = sem("terms2_made")
        t_expo = sem("exponents2_made")
        t_exp = sem("exponentials2_made")
        t_p = sem("weights2_made")
        t_ph = sem("weights2_high")
        t_pl = sem("weights2_low")
        t_xb = sem("x_biased")
        t_o = sem("attention2_tile")
        t_rd = sem("sum2_steps")
        t_x1 = sem("x1_parts")
        t_st = sem("stats2_steps")
        t_root = sem("root2_taken")
        block = ctx.enter_context(nc.Block())

        @block.sync
        def _(sp):
            sp.dma_start(ab_rows[:], row2_dram.rearrange("(a t) p -> a (t p)", a=2).partition_broadcast(P))\
              .then_inc(t_ab, 16)
            sp.dma_start(b2row[:], b2.partition_broadcast(P)).then_inc(t_b2, 16)
            sp.dma_start(xt[:], x.rearrange("(t p) d -> p t d", p=P)).then_inc(t_x, 16)

        @block.gpsimd
        def _(pool):
            pool.wait_ge(t_x, 16)
            pool.wait_ge(t_b2, 16)
            for t in range(NT):
                pool.tensor_tensor(xt[:, t, :], xt[:, t, :], b2row[:], ALU.add).then_inc(t_xb, 1)

        def halves(hf):
            return slice(hf * HALF, (hf + 1) * HALF)

        @block.vector
        def _(dve):
            dve.wait_ge(t_ab, 16)

            def terms(n):
                hf, s = divmod(n, NT)
                if n >= 2:
                    dve.wait_ge(t_pl, n - 1)
                dve.tensor_scalar(ta[:, n % 2, :], ab_rows[:, 0, halves(hf)], lc2[:, 0, s:s + 1], 0.0, ALU.add,
                                  ALU.min)
                dve.tensor_scalar(tb[:, n % 2, :], ab_rows[:, 1, halves(hf)], lc2[:, 2, s:s + 1], 0.0, ALU.add,
                                  ALU.min).then_inc(t_terms, 1)
                dve.wait_ge(t_terms, n + 1)
                dve.tensor_tensor(ta[:, n % 2, :], ta[:, n % 2, :], tb[:, n % 2, :], ALU.max).then_inc(t_expo, 1)

            def rest(n):
                hf, s = divmod(n, NT)
                dve.wait_ge(t_exp, n + 1)
                dve.tensor_tensor(tb[:, n % 2, :], ta[:, n % 2, :], ct[:, s, halves(hf)], ALU.mult).then_inc(t_p, 1)
                dve.wait_ge(t_ph, n + 1)
                dve.tensor_tensor(pl[hf][:, s, :], tb[:, n % 2, :], f32(ph[hf][:, s, :]), ALU.subtract)\
                    .then_inc(t_pl, 1)

            def tile_out(t):
                a, b = ps[:, 2 * (t % 4), :], ps[:, 2 * (t % 4) + 1, :]
                dve.wait_ge(t_o, t + 1)
                dve.tensor_scalar(rd[:, 0, t:t + 1], b[:, D - 384:D - 383], EPS_DEN, None, ALU.add).then_inc(t_rd, 1)
                dve.wait_ge(t_rd, 2 * t + 1)
                dve.reciprocal(rd[:, 1, t:t + 1], rd[:, 0, t:t + 1]).then_inc(t_rd, 1)
                dve.wait_ge(t_rd, 2 * t + 2)
                dve.wait_ge(t_xb, t + 1)
                for c, bankc in enumerate((a, b)):
                    part = xt[:, t, c * 384:(c + 1) * 384]
                    dve.scalar_tensor_tensor(out=part, in0=bankc[:, 0:384], scalar=rd[:, 1, t:t + 1], in1=part,
                                             op0=ALU.mult, op1=ALU.add).then_inc(t_x1, 1)
                for c in range(2):
                    dve.wait_ge(t_x1, 2 * t + c + 1)
                    dve.bn_stats(stats[:, t, c, :], xt[:, t, c * 384:(c + 1) * 384]).then_inc(t_st, 1)
                dve.wait_ge(t_st, 3 * t + 2)
                dve.bn_aggr(mv[:, t, :], stats[:, t, :, :].rearrange("p a b -> p (a b)")).then_inc(t_st, 1)

            for n in range(2 * NT + 1):
                if n < 2 * NT:
                    terms(n)
                if n >= 1:
                    rest(n - 1)
            for t in range(NT):
                tile_out(t)
            done = rstd_steps(dve, mv, root, t_st, 3 * NT, t_root)
            dve.wait_ge(t_st, done)
            dve.tensor_copy(dinv[:, 3, :], root[:, 5, :])

        @block.scalar
        def _(act):
            for n in range(2 * NT):
                hf, s = divmod(n, NT)
                act.wait_ge(t_expo, n + 1)
                act.activation(ta[:, n % 2, :], ta[:, n % 2, :], ACT.Exp).then_inc(t_exp, 1)
                act.wait_ge(t_p, n + 1)
                act.activation(ph[hf][:, s, :], tb[:, n % 2, :], ACT.Copy).then_inc(t_ph, 1)
            act.wait_ge(t_st, 3 * NT + 1)
            act.activation(root[:, 1, :], root[:, 0, :], ACT.Sqrt).then_inc(t_root, 1)

        @block.tensor
        def _(pe):
            for t in range(NT):
                hf, tt = divmod(t, HT)
                if t >= 4:
                    pe.wait_ge(t_x1, 2 * (t - 3))
                for s in range(NT):
                    if tt == 0:
                        pe.wait_ge(t_pl, hf * NT + s + 1)
                    dd = slice(tt * P, (tt + 1) * P)
                    for n, (a, b) in enumerate(((ph, hh), (ph, hl), (pl, hh))):
                        for c, (lo, hi) in enumerate(((0, 384), (384, D + 2))):
                            mm = pe.matmul(ps[:, 2 * (t % 4) + c, 0:hi - lo], a[hf][:, s, dd], b[:, s, lo:hi],
                                           start=(s == 0 and n == 0), stop=(s == NT - 1 and n == 2))
                mm.then_inc(t_o, 1)


def convolution(nc, env):
    Wg, bg, out = env["Wg"], env["bg"], env["out"]
    ct, dinv, xt, mv = (env[k] for k in ("ct", "dinv", "xt", "mv"))
    NT, N = ct.shape[1], ct.shape[2]
    D = Wg.shape[1]
    KT = D // P
    HALF = N // 2
    HT = NT // 2

    with ExitStack() as ctx:
        def sb(name, shape, dt):
            return ctx.enter_context(nc.sbuf_tensor(name, shape, dt))

        sem = Sems(nc, ctx)
        ps = ctx.enter_context(nc.psum_tensor("g_ps", [P, 8, 512], F32))
        xh = sb("x2_high", [P, NT, D], F16)
        xl = sb("x2_low", [P, NT, D], F16)
        xs = sb("x2_scaled", [P, 2, D], F32)
        cf = sb("count_f", [P, 2, N], F32)
        chi = sb("count_high", [P, NT, N], F16)
        clo = sb("count_low", [P, NT, N], F16)
        ident = sb("ident3", [P, P], F32)
        wr = sb("wg_raw", [P, 2, D], F32)
        wh = sb("wg_high", [P, KT, D], F32R)
        wl = sb("wg_low", [P, KT, D], F32R)
        zt = sb("z3", [P, 2, HALF], F32)
        zh = sb("z3_high", [P, KT, N], F32R)
        zl = sb("z3_low", [P, KT, N], F32R)
        bgrow = sb("bg_row", [P, D], F32)

        g_w = [sem(f"wg_loaded{i}") for i in range(2)]
        g_b = sem("bg_loaded")
        g_c = sem("ident3_made")
        g_xs = sem("x2_scaled_steps")
        g_xh = sem("x2_high_done")
        g_xl = sem("x2_low_done")
        g_cf = sem("counts_float")
        g_ci = sem("loops_added")
        g_ch = sem("counts_high")
        g_cl = sem("counts_low")
        g_wh = sem("wg_high_done")
        g_wl = sem("wg_low_done")
        g_xb = sem("x1_biased")
        g_z = sem("z3_ready")
        g_zt = sem("z3_copied")
        g_zh = sem("z3_high_done")
        g_zl = sem("z3_low_done")
        g_o = sem("convolution_tile")
        g_y = sem("output_parts")
        g_out = sem("output_stored")
        block = ctx.enter_context(nc.Block())

        @block.sync
        def _(sp):
            sp.dma_start(bgrow[:], bg.partition_broadcast(P)).then_inc(g_b, 16)
            for k in range(KT):
                if k >= 2:
                    sp.wait_ge(g_wl, k - 1)
                sp.dma_start(wr[:, k % 2, :], Wg[k * P:(k + 1) * P, :]).then_inc(g_w[k % 2], 16)
            for t in range(NT):
                sp.wait_ge(g_y, 2 * t + 2)
                sp.dma_start(out[t * P:(t + 1) * P, :], xt[:, t, :]).then_inc(g_out, 16)
            sp.wait_ge(g_out, 16 * NT)

        @block.gpsimd
        def _(pool):
            pool.memset(ident[:], 0.0).then_inc(g_c, 1)
            pool.wait_ge(g_c, 1)
            pool.affine_select(out=ident[:], in_=ident[:], compare_op=ALU.not_equal, fill=1.0, base=0,
                               pattern=[[-1, P]], channel_multiplier=1).then_inc(g_c, 1)
            pool.wait_ge(g_b, 16)
            for t in range(NT):
                pool.wait_ge(g_xs, 2 * t + 1)
                pool.tensor_tensor(xt[:, t, :], xt[:, t, :], bgrow[:], ALU.add).then_inc(g_xb, 1)

        @block.vector
        def _(dve):
            dve.wait_ge(g_c, 2)

            def tile_in(s):
                if s >= 2:
                    dve.wait_ge(g_xl, s - 1)
                dve.tensor_scalar(xs[:, s % 2, :], xt[:, s, :], mv[:, s, 0:1], dinv[:, 3, s:s + 1], ALU.subtract,
                                  ALU.mult).then_inc(g_xs, 1)
                dve.wait_ge(g_cf, s + 1)
                diag = cf[:, s % 2, s * P:(s + 1) * P]
                dve.tensor_tensor(diag, diag, ident[:], ALU.add).then_inc(g_ci, 1)
                dve.wait_ge(g_xs, 2 * s + 1)
                dve.tensor_scalar(xs[:, s % 2, :], xs[:, s % 2, :], 0.0, dinv[:, 1, s:s + 1], ALU.max,
                                  ALU.mult).then_inc(g_xs, 1)
                dve.wait_ge(g_ch, s + 1)
                dve.tensor_tensor(clo[:, s, :], cf[:, s % 2, :], chi[:, s, :], ALU.subtract).then_inc(g_cl, 1)
                dve.wait_ge(g_xh, s + 1)
                dve.tensor_tensor(xl[:, s, :], xs[:, s % 2, :], xh[:, s, :], ALU.subtract).then_inc(g_xl, 1)

            def w_low(k):
                dve.wait_ge(g_wh, k + 1)
                dve.tensor_tensor(wl[:, k, :], wr[:, k % 2, :], f32(wh[:, k, :]), ALU.subtract).then_inc(g_wl, 1)

            for s in range(NT):
                tile_in(s)
            for n in range(2 * KT):
                hf, k = divmod(n, KT)
                dve.wait_ge(g_z, n + 1)
                if n >= 2:
                    dve.wait_ge(g_zl, n - 1)
                dve.tensor_copy(zt[:, n % 2, :], ps[:, n % 2, :]).then_inc(g_zt, 1)
                if n < KT:
                    w_low(n)
                dve.wait_ge(g_zh, n + 1)
                dve.tensor_tensor(zl[:, k, hf * HALF:(hf + 1) * HALF], zt[:, n % 2, :],
                                  f32(zh[:, k, hf * HALF:(hf + 1) * HALF]), ALU.subtract).then_inc(g_zl, 1)
            for t in range(NT):
                dve.wait_ge(g_o, t + 1)
                dve.wait_ge(g_xb, t + 1)
                for c in range(2):
                    part = xt[:, t, c * 384:(c + 1) * 384]
                    dve.scalar_tensor_tensor(out=part, in0=ps[:, 2 + 2 * (t % 3) + c, 0:384],
                                             scalar=dinv[:, 2, t:t + 1], in1=part, op0=ALU.mult,
                                             op1=ALU.add).then_inc(g_y, 1)

        @block.scalar
        def _(act):
            for s in range(NT):
                if s >= 2:
                    act.wait_ge(g_cl, s - 1)
                act.activation(cf[:, s % 2, :], ct[:, s, :], ACT.Copy).then_inc(g_cf, 1)
                act.wait_ge(g_ci, s + 1)
                act.activation(chi[:, s, :], cf[:, s % 2, :], ACT.Copy).then_inc(g_ch, 1)
                act.wait_ge(g_xs, 2 * s + 2)
                act.activation(xh[:, s, :], xs[:, s % 2, :], ACT.Copy).then_inc(g_xh, 1)
            for n in range(2 * KT):
                hf, k = divmod(n, KT)
                if n < KT:
                    act.wait_ge(g_w[n % 2], 16 * (n // 2 + 1))
                    act.activation(wh[:, n, :], wr[:, n % 2, :], ACT.Copy).then_inc(g_wh, 1)
                act.wait_ge(g_zt, n + 1)
                act.activation(zh[:, k, hf * HALF:(hf + 1) * HALF], zt[:, n % 2, :], ACT.Copy).then_inc(g_zh, 1)

        @block.tensor
        def _(pe):
            for n in range(2 * KT):
                hf, k = divmod(n, KT)
                if n >= 2:
                    pe.wait_ge(g_zt, n - 1)
                for s in range(NT):
                    if n == 0:
                        pe.wait_ge(g_xl, s + 1)
                        pe.wait_ge(g_cl, s + 1)
                    for i, (a, b) in enumerate(((xh, chi), (xh, clo), (xl, chi))):
                        mm = pe.matmul(ps[:, n % 2, :], a[:, s, k * P:(k + 1) * P],
                                       b[:, s, hf * HALF:(hf + 1) * HALF], start=(s == 0 and i == 0),
                                       stop=(s == NT - 1 and i == 2))
                mm.then_inc(g_z, 1)
            pe.wait_ge(g_wl, KT)
            for t in range(NT):
                if t >= 3:
                    pe.wait_ge(g_y, 2 * (t - 2))
                for k in range(KT):
                    if t in (0, HT):
                        pe.wait_ge(g_zl, (t // HT) * KT + k + 1)
                    for i, (a, b) in enumerate(((zh, wh), (zh, wl), (zl, wh))):
                        for c in range(2):
                            mm = pe.matmul(ps[:, 2 + 2 * (t % 3) + c, 0:384], a[:, k, t * P:(t + 1) * P],
                                           b[:, k, c * 384:(c + 1) * 384], start=(k == 0 and i == 0),
                                           stop=(k == KT - 1 and i == 2))
                mm.then_inc(g_o, 1)


def build(nc, x, src, dst, W1, a_s1, a_d1, b1, W2, a_s2, a_d2, b2, Wg, bg, out):
    N, D = x.shape
    H = a_s1.shape[0]
    NT, KT, HALF = N // P, D // P, N // 2
    env = dict(x=x, src=src, dst=dst, W1=W1, a_s1=a_s1, a_d1=a_d1, b1=b1, W2=W2, a_s2=a_s2, a_d2=a_d2,
               b2=b2, Wg=Wg, bg=bg, out=out)
    for name, shape, dt in (("logit_rows", (H, N), F32), ("mask_dram", (2, P, NT // 2, N), BF16),
                            ("ab_dram", (2, 2, HALF), F32), ("h2_dram", (2, P, 6, 512), F32),
                            ("row_dram", (NT, P), F32), ("row2_dram", (2 * NT, P), F32)):
        env[name] = nc.dram_tensor(name, shape, dt).ap()
    with ExitStack() as whole:
        env["ct"] = whole.enter_context(nc.sbuf_tensor("ct", [P, NT, N], U16))
        with ExitStack() as first:
            for name, shape, dt in (("xh", [P, NT, D], F16), ("xl", [P, NT, D], F16), ("lc", [P, NT, 2 * H], F32),
                                    ("lc02", [P, NT, 2 * H], F32), ("b1c", [P, H * KT], F32)):
                env[name] = first.enter_context(nc.sbuf_tensor(name, shape, dt))
            startup(nc, env)
            heads(nc, env)
        for name, shape, dt in (("lc2", [P, 3, NT], F32), ("ab2", [P, 2, NT], F32), ("dinv", [P, 4, NT], F32),
                                ("mv2", [P, NT, 2], F32), ("xt2", [P, NT, D], F32)):
            env[name] = whole.enter_context(nc.sbuf_tensor(name, shape, dt))
        env["xt"], env["mv"] = env["xt2"], env["mv2"]
        with ExitStack() as second:
            env["h2h"] = second.enter_context(nc.sbuf_tensor("h2h", [P, NT, D + 2], F32R))
            env["h2l"] = second.enter_context(nc.sbuf_tensor("h2l", [P, NT, D + 2], F32R))
            second_logits(nc, env)
            second_attention(nc, env)
        convolution(nc, env)


_INS = ['x', 'src', 'dst', 'L0_gnn_W1', 'L0_gnn_a_src1', 'L0_gnn_a_dst1', 'L0_gnn_b1', 'L0_gnn_W2',
        'L0_gnn_a_src2', 'L0_gnn_a_dst2', 'L0_gnn_b2', 'L1_gnn_W', 'L1_gnn_b']


def kernel(**inputs):
    import numpy as _np
    import concourse.bacc as _bacc
    from concourse import mybir as _mybir
    from concourse.bass_utils import run_bass_kernel_spmd as _run

    nc = _bacc.Bacc("TRN2", target_bir_lowering=False, num_devices=1)
    arrays, args = {}, []
    for name in _INS:
        a = _np.ascontiguousarray(inputs[name])
        arrays[f"in_{name}_dram"] = a
        args.append(nc.dram_tensor(f"in_{name}_dram", a.shape, _mybir.dt.from_np(a.dtype), kind="ExternalInput").ap())
    out = nc.dram_tensor("out_0_dram", arrays["in_x_dram"].shape, F32, kind="ExternalOutput").ap()
    build(nc, *args, out)
    r = _run(nc, [arrays], core_ids=[0])
    return r.results[0]["out_0_dram"]
```

```python
from contextlib import ExitStack

import concourse.bass as bass
from concourse import mybir

P = 128
F32 = mybir.dt.float32
F32R = mybir.dt.float32r
F16 = mybir.dt.float16
BF16 = mybir.dt.bfloat16
I32 = mybir.dt.int32
U16 = mybir.dt.uint16
ALU = mybir.AluOpType
ACT = mybir.ActivationFunctionType

SLOPE = 0.2
EPS_DEN = 1e-16
EPS_LN = 1e-5
FAR = -1e38
XS = 1024.0
DIGIT = 4096
START = 16


def f32(ap):
    return ap.bitcast(F32)


class Sems:

    def __init__(self, nc, ctx):
        self.nc, self.ctx = nc, ctx

    def __call__(self, name):
        return self.ctx.enter_context(self.nc.semaphore(name))


def startup(nc, env):
    x, src, dst, W1, a_s1, a_d1 = (env[k] for k in ("x", "src", "dst", "W1", "a_s1", "a_d1"))
    N, D = x.shape
    E = src.shape[0]
    H = a_s1.shape[0]
    NT, KT = N // P, D // P
    HALF = N // 2
    CH = E // P
    CG = DIGIT // P
    NG = CH // CG
    HG = H // NG
    RING = 8
    assert CG * P <= DIGIT and CH == CG * NG and H == NT == HG * NG and CG == NT + 2 * KT * HG
    xh, xl, ct, lc, lc02, b1c, ident = (env[k] for k in ("xh", "xl", "ct", "lc", "lc02", "b1c", "ident"))
    mask_dram = env["mask_dram"]

    with ExitStack() as ctx:
        def sb(name, shape, dt):
            return ctx.enter_context(nc.sbuf_tensor(name, shape, dt))

        sem = Sems(nc, ctx)
        psum = ctx.enter_context(nc.psum_tensor("count_ps", [P, 8, 512], F32))
        edge_i = sb("edge_i", [P, 2, CH], I32)
        dst_low = sb("dst_low", [P, CH], I32)
        edge_f = sb("edge_f", [P, 3, CH], F32)
        iota = sb("iota", [P, N], F16)
        src_hot = sb("src_hot", [P, RING, N], F16)
        dst_hot = sb("dst_hot", [P, RING, HALF], F16)
        xt = sb("xt", [P, NT, D], F32)
        stats = sb("stats", [P, HG, 2, 6], F32)
        mv = sb("mv", [P, HG, 2], F32)
        root = sb("root", [P, 7, HG], F32)
        xT = sb("xT", [P, KT, N], F32)
        wv = sb("wv", [P, KT, D], F32)
        arow = sb("arow", [P, HG, 2, D], F32)
        junk = sb("junk", [P, 2, D], BF16)
        vsum = sb("vsum", [P, 2 * KT], F32)
        V = sb("V", [P, KT, 2 * H], F32)
        packed = sb("packed", [P, NT, 512], F32)
        digits = sb("digits", [P, NT, N], U16)
        ident_b = sb("ident_b", [P, P], BF16)
        prod = xT[:, 0:2, 0:D]
        half_col = sb("half_col", [P, 1], F32)
        b1r = sb("b1_rows", [H * KT, P], F32)

        s_edges = sem("edges_loaded")
        s_x = sem("x_loaded")
        s_b1 = sem("b1_loaded")
        s_w = [sem(f"w_tile_loaded{k}") for k in range(KT)]
        s_a = [sem(f"a_rows_loaded{i}") for i in range(HG)]
        s_turn = sem("loads_begun")
        s_iota = sem("iota_made")
        s_ct = sem("counts_zeroed")
        s_ident = sem("ident_made")
        s_prep = sem("edge_prep")
        s_ln = sem("ln_steps")
        s_root = sem("root_taken")
        s_hot = sem("one_hots_made")
        s_used = sem("one_hots_used")
        s_bank = sem("bank_filled")
        s_bfree = sem("bank_read")
        s_xturn = sem("x_turn_begun")
        s_lnturn = sem("averages_begun")
        s_xn = sem("x_centred")
        s_xr = sem("x_normed")
        s_xhi = sem("x_high")
        s_v = sem("w_a_summed")
        s_vp = sem("w_a_multiplied")
        s_va = sem("w_a_products_summed")
        s_vc = sem("w_a_kept")
        s_high = sem("high_digits")
        s_low = sem("low_digits")
        s_add = sem("counts_added")
        s_near = sem("near_made")
        s_xTp = sem("x_turned")
        s_xT = sem("xT_kept")
        s_lcp = sem("logit_columns_ready")
        s_lc = sem("logit_columns_kept")
        s_mp = sem("mask_turned")
        s_mk = [sem(f"mask_kept{n}") for n in range(2)]
        s_mout = sem("mask_stored")
        block = ctx.enter_context(nc.Block())

        masks = [env["mask0"], src_hot[:, 0:NT // 2, :].bitcast(BF16)]
        near = digits[:].bitcast(BF16)
        W1v = W1.rearrange("(k p) (h c) -> p k h c", p=P, h=H)
        SV = 2 * (KT - 1)
        LN = 3 * HG + 7
        LN0 = CG - LN - 8
        LOW_AT = range(CG - 1 - 3 * NT, CG - 3, 3)
        SUM_AT = [j for j in range(CG) if j not in LOW_AT]

        def keep_bank(act, g, b):
            act.wait_ge(s_bank, g * NT + (b + 1 + START))
            act.wait_ge(s_low, g * NT + (b + 1 - NT + START))
            act.activation(packed[:, b, :], psum[:, b, :], ACT.Copy).then_inc(s_bfree, 1)

        def high_digit(act, g, b):
            act.wait_ge(s_bfree, g * NT + (b + 1 + START))
            act.wait_ge(s_add, g * NT + (b + 1 - NT + START))
            act.activation(digits[:, b, HALF:N], packed[:, b, :], ACT.Relu, scale=-1.0 / DIGIT,
                           bias=half_col[:]).then_inc(s_high, 1)

        def low_digit(dve, g, b):
            dve.wait_ge(s_high, g * NT + (b + 1 + START))
            dve.scalar_tensor_tensor(out=digits[:, b, 0:HALF], in0=digits[:, b, HALF:N], scalar=float(DIGIT),
                                     in1=packed[:, b, :], op0=ALU.mult, op1=ALU.add).then_inc(s_low, 1)

        def add_counts(dve, g, b):
            dve.wait_ge(s_low, g * NT + (b + 1 + START))
            dve.wait_ge(s_add, g * NT + (b + 1 - NT + START))
            if b == 0:
                dve.wait_ge(s_ct, 1)
            dve.tensor_tensor(ct[:, b, :], ct[:, b, :], digits[:, b, :], ALU.add).then_inc(s_add, 1)

        def keep_mask(eng, t):
            eng.wait_ge(s_mp, t + 1)
            turned = psum[:, t % 6, :].bitcast(BF16)
            mask = masks[t // (NT // 2)][:, t % (NT // 2), :]
            if t % 2 == 0:
                eng.activation(mask, turned, ACT.Copy, scale=-FAR, bias=FAR).then_inc(s_mk[0], 1)
            else:
                eng.tensor_scalar(mask, turned, -FAR, FAR, ALU.mult, ALU.add).then_inc(s_mk[1], 1)

        @block.sync
        def _(sp):
            sp.dma_start(edge_i[:, 0, :], src.rearrange("(p c) -> p c", p=P)).then_inc(s_edges, 16)
            sp.dma_start(edge_i[:, 1, :], dst.rearrange("(p c) -> p c", p=P)).then_inc(s_edges, 16)
            sp.dma_start(b1r[:], env["b1"].rearrange("(c p) -> c p", p=P)).then_inc(s_b1, 16)
            for s in (*s_a, *s_w):
                sp.sem_inc(s, START)
            with sp.Fori(0, NG) as g:
                for i in range(HG):
                    h = sp.snap(g * HG + i)
                    sp.wait_ge(s_v, g * (SV * HG) + (SV * (i - HG + 1) + START))
                    sp.sem_inc(s_turn, 1)
                    sp.wait_ge(s_vp, g * (2 * HG) + (2 * (i - HG + 1) + START))
                    sp.sem_inc(s_turn, 1)
                    sp.dma_start(arow[:, i, 0, :], a_s1[bass.ds(h, 1), :].to_broadcast([P, D])).then_inc(s_a[i], 16)
                    sp.dma_start(arow[:, i, 1, :], a_d1[bass.ds(h, 1), :].to_broadcast([P, D])).then_inc(s_a[i], 16)
                    for k in range(KT):
                        if k < KT - 1:
                            sp.wait_ge(s_v, g * (SV * HG) + (SV * (i - 1) + 2 * (k + 1) + START))
                        else:
                            sp.wait_ge(s_vp, g * (2 * HG) + (2 * i + START))
                        sp.sem_inc(s_turn, 1)
                        sp.dma_start(wv[:, k, :], W1v[:, k, bass.ds(h, 1), :]).then_inc(s_w[k], 16)
            for hf in range(2):
                for n in range(2):
                    sp.wait_ge(s_mk[n], (hf + 1) * (NT // 4))
                sp.dma_start(mask_dram[hf], masks[hf]).then_inc(s_mout, 16)
            sp.wait_ge(s_mout, 32)

        @block.gpsimd
        def _(pool):
            pool.sem_inc(s_vp, START)
            pool.memset(half_col[:], 0.5 - 0.75 / DIGIT).then_inc(s_iota, 1)
            pool.iota(iota[:], pattern=[[1, N]], base=0, channel_multiplier=0,
                      allow_small_or_imprecise_dtypes=True).then_inc(s_iota, 1)
            pool.memset(ct[:], 0).then_inc(s_ct, 1)
            pool.memset(ident[:], 0.0).then_inc(s_ident, 1)
            pool.wait_ge(s_ident, 1)
            pool.affine_select(out=ident[:], in_=ident[:], compare_op=ALU.not_equal, fill=1.0, base=0,
                               pattern=[[-1, P]], channel_multiplier=1).then_inc(s_ident, 1)
            pool.wait_ge(s_ident, 2)
            pool.tensor_copy(ident_b[:], ident[:]).then_inc(s_ident, 1)
            with pool.Fori(0, NG) as g:
                for i in range(HG):
                    for sd in range(2):
                        if sd == 0:
                            pool.wait_ge(s_a[i], g * 32 + (32 + START))
                            pool.wait_ge(s_w[KT - 1], g * (16 * HG) + (16 * (i + 1) + START))
                        pool.wait_ge(s_va, g * (2 * HG) + (2 * i + sd - 1 + START))
                        pool.tensor_tensor(prod[:, sd, :], wv[:, KT - 1, :], arow[:, i, sd, :], ALU.mult)\
                            .then_inc(s_vp, 1)
                for i in range(HG):
                    pool.wait_ge(s_xhi, g * HG + (i + 1 + START))
                    tile = bass.ds(g * HG + i, 1)
                    pool.tensor_tensor(xl[:, tile, :], xt[:, tile, :], xh[:, tile, :], ALU.subtract)

        @block.vector
        def _(dve):
            for s in (s_hot, s_v, s_vc, s_low, s_add, s_ln, s_bank):
                dve.sem_inc(s, START)
            for b in range(NT):
                dve.memset(psum[:, b, :], 0.0).then_inc(s_bank, 1)
            dve.wait_ge(s_edges, 32)
            dve.tensor_copy(edge_f[:, 0, :], edge_i[:, 0, :]).then_inc(s_prep, 1)
            dve.tensor_scalar(dst_low[:], edge_i[:, 1, :], HALF - 1, None, ALU.bitwise_and).then_inc(s_prep, 1)
            dve.wait_ge(s_prep, 1)
            dve.tensor_scalar(edge_i[:, 0, :], edge_i[:, 1, :], HALF.bit_length() - 1, None,
                              ALU.logical_shift_right).then_inc(s_prep, 1)
            dve.wait_ge(s_prep, 3)
            dve.tensor_copy(edge_f[:, 1, :], dst_low[:]).then_inc(s_prep, 1)
            dve.tensor_scalar(edge_f[:, 2, :], edge_i[:, 0, :], -float(DIGIT + 1), 1.0, ALU.mult,
                              ALU.add).then_inc(s_prep, 1)
            dve.wait_ge(s_iota, 2)
            dve.wait_ge(s_prep, 5)

            def w_sum(g, i, q):
                k, sd = q // 2, q % 2
                if q == 0:
                    dve.wait_ge(s_a[i], g * 32 + (32 + START))
                    dve.wait_ge(s_vc, g * HG + (i + START))
                dve.wait_ge(s_w[k], g * (16 * HG) + (16 * (i + 1) + START))
                dve.wait_ge(s_v, g * (SV * HG) + (SV * i + q - 1 + START))
                dve.tensor_tensor_reduce(junk[:, q % 2, :], wv[:, k, :], arow[:, i, sd, :], 1.0, 0.0,
                                         ALU.mult, ALU.add, vsum[:, q:q + 1]).then_inc(s_v, 1)

            def keep_sums(g, i):
                parts = vsum[:].rearrange("p (k s) -> p k s", s=2)
                dve.wait_ge(s_v, g * (SV * HG) + (SV * (i + 1) + START))
                dve.wait_ge(s_va, g * (2 * HG) + (2 * (i + 1) + START))
                dve.tensor_copy(V[:, :, bass.ds(g * HG + i, 1)], parts[:, :, 0:1])
                dve.tensor_copy(V[:, :, bass.ds(g * HG + (i + H), 1)], parts[:, :, 1:2]).then_inc(s_vc, 1)

            def ln_step(g, n):
                c = [root[:, i, :] for i in range(7)]

                def behind(m):
                    dve.wait_ge(s_ln, g * LN + (m + 1 + START))
                if n < 2 * HG:
                    if n == 0:
                        dve.wait_ge(s_x, 16)
                        dve.wait_ge(s_ln, g * LN + START)
                    i, part = n // 2, n % 2
                    ins = dve.bn_stats(stats[:, i, part, :], xt[:, bass.ds(g * HG + i, 1),
                                                                part * (D // 2):(part + 1) * (D // 2)]
                                       .rearrange("p o d -> p (o d)"))
                elif n < 3 * HG:
                    i = n - 2 * HG
                    behind(2 * HG - 1)
                    dve.wait_ge(s_xhi, g * HG + START)
                    dve.sem_inc(s_lnturn, 1)
                    ins = dve.bn_aggr(mv[:, i, :], stats[:, i, :, :].rearrange("p a b -> p (a b)"))
                else:
                    behind(n - 1)
                    m = n - 3 * HG
                    if m == 0:
                        ins = dve.tensor_scalar(c[6], mv[:, :, 0:1].rearrange("p t o -> p (t o)"), -1.0, None,
                                                ALU.mult)
                    elif m == 1:
                        ins = dve.tensor_scalar(c[0], mv[:, :, 1:2].rearrange("p t o -> p (t o)"), EPS_LN, None,
                                                ALU.add)
                    elif m == 2:
                        dve.wait_ge(s_root, g + (1 + START))
                        ins = dve.reciprocal(c[2], c[1])
                    elif m == 3:
                        ins = dve.tensor_tensor(c[3], c[0], c[2], ALU.mult)
                    elif m == 4:
                        ins = dve.tensor_tensor(c[4], c[1], c[3], ALU.add)
                    elif m == 5:
                        ins = dve.tensor_scalar(c[3], c[4], 0.5 / XS, None, ALU.mult)
                    else:
                        ins = dve.reciprocal(c[5], c[3])
                ins.then_inc(s_ln, 1)

            with dve.Fori(0, NG) as g:
                c0 = dve.snap(g * CG)
                for j in range(CG):
                    if j == RING - 1:
                        dve.wait_ge(s_bank, g * NT + (NT + START))
                    else:
                        n = j + 1 - RING if j >= RING else j + 2 - RING
                        dve.wait_ge(s_used, g * (CG - 1) + (n + START))
                    dve.tensor_scalar(src_hot[:, j % RING, :], iota[:], edge_f[:, 0, bass.ds(c0 + j, 1)], None,
                                      ALU.is_equal).then_inc(s_hot, 1)
                    dve.tensor_scalar(dst_hot[:, j % RING, :], iota[:, 0:HALF], edge_f[:, 1, bass.ds(c0 + j, 1)],
                                      edge_f[:, 2, bass.ds(c0 + j, 1)], ALU.is_equal, ALU.mult).then_inc(s_hot, 1)
                    if j in LOW_AT:
                        b = LOW_AT.index(j)
                        low_digit(dve, g, b)
                        if b >= 1:
                            add_counts(dve, g, b - 1)
                    else:
                        i, q = divmod(SUM_AT.index(j), 2 * KT)
                        if q >= 2 * KT - SV:
                            w_sum(g, i, q - (2 * KT - SV))
                        if q == 2 * KT - 1:
                            keep_sums(g, i)
                    if LN0 <= j < LN0 + LN:
                        ln_step(g, j - LN0)
                add_counts(dve, g, NT - 1)
            for b in range(NT):
                low_digit(dve, NG, b)
                if b >= 1:
                    add_counts(dve, NG, b - 1)
                    dve.wait_ge(s_add, NG * NT + b + START)
                    dve.tensor_scalar(near[:, b - 1, :], ct[:, b - 1, :], 1.0, None, ALU.min).then_inc(s_near, 1)
            add_counts(dve, NG, NT - 1)
            dve.wait_ge(s_add, (NG + 1) * NT + START)
            dve.tensor_scalar(near[:, NT - 1, :], ct[:, NT - 1, :], 1.0, None, ALU.min).then_inc(s_near, 1)

            for t in range(1, NT, 2):
                keep_mask(dve, t)
            dve.wait_ge(s_lcp, 1)
            dve.tensor_scalar(lc[:].rearrange("p t c -> p (t c)"), psum[:, 6, 0:NT * 2 * H], 1.0 / XS, None,
                              ALU.mult).then_inc(s_lc, 1)
            dve.tensor_copy(b1c[:], psum[:, 6, P:P + H * KT])
            dve.wait_ge(s_lc, 1)
            dve.tensor_scalar(lc02[:].rearrange("p t c -> p (t c)"), lc[:].rearrange("p t c -> p (t c)"),
                              SLOPE, None, ALU.mult).then_inc(s_lc, 1)
            dve.wait_ge(s_lc, 2)

        @block.scalar
        def _(act):
            for s in (s_bfree, s_high, s_xhi, s_root, s_xn, s_xr, s_va):
                act.sem_inc(s, START)
            act.wait_ge(s_iota, 1)

            def products_summed(g, i):
                for sd in range(2):
                    act.wait_ge(s_vp, g * (2 * HG) + (2 * i + sd + 1 + START))
                    if sd == 0:
                        act.wait_ge(s_vc, g * HG + (i + START))
                    act.activation(prod[:, sd, :], prod[:, sd, :], ACT.Copy,
                                   accum_out=vsum[:, SV + sd:SV + sd + 1]).then_inc(s_va, 1)

            act.wait_ge(s_bank, NT + START)
            act.dma_start(xt[:], x.rearrange("(t p) d -> p t d", p=P)).then_inc(s_x, 16)
            with act.Fori(0, NG) as g:
                for b in range(NT):
                    keep_bank(act, g, b)
                for b in range(NT):
                    high_digit(act, g, b)
                products_summed(g, 0)
                act.wait_ge(s_ln, g * LN + (3 * HG + 2 + START))
                act.activation(root[:, 1, :], root[:, 0, :], ACT.Sqrt).then_inc(s_root, 1)
                act.wait_ge(s_ln, g * LN + (LN + START))
                act.sem_inc(s_xturn, 1)
                for i in range(HG):
                    tile = bass.ds(g * HG + i, 1)
                    act.activation(xt[:, tile, :], xt[:, tile, :], ACT.Identity, bias=root[:, 6, i:i + 1])\
                        .then_inc(s_xn, 1)
                for i in range(HG):
                    tile = bass.ds(g * HG + i, 1)
                    act.wait_ge(s_xn, g * HG + (i + 1 + START))
                    act.sem_inc(s_xturn, 1)
                    act.activation(xt[:, tile, :], xt[:, tile, :], ACT.Relu, scale=root[:, 5, i:i + 1])\
                        .then_inc(s_xr, 1)
                for i in range(HG):
                    tile = bass.ds(g * HG + i, 1)
                    act.wait_ge(s_xr, g * HG + (i + 1 + START))
                    act.sem_inc(s_xturn, 1)
                    act.activation(xh[:, tile, :], xt[:, tile, :], ACT.Copy).then_inc(s_xhi, 1)
                for i in range(1, HG):
                    products_summed(g, i)
            keep_bank(act, NG, 0)
            for b in range(NT):
                if b + 1 < NT:
                    keep_bank(act, NG, b + 1)
                high_digit(act, NG, b)
            for i in range(2 * KT):
                k, nh = i // 2, i % 2
                act.wait_ge(s_xTp, i + 1)
                act.activation(xT[:, k, nh * 512:(nh + 1) * 512], psum[:, i % 6, :], ACT.Copy).then_inc(s_xT, 1)
            for t in range(0, NT, 2):
                keep_mask(act, t)

        @block.tensor
        def _(pe):
            pe.sem_inc(s_used, START)
            steps = [(0, 1), *((j,) for j in range(2, CG - 2)), (CG - 2, CG - 1)]
            with pe.Fori(0, NG) as g:
                for step in steps:
                    pe.wait_ge(s_hot, g * (2 * CG) + (2 * step[-1] + 2 + START))
                    for b in range(NT):
                        if step[0] == 0:
                            pe.wait_ge(s_bfree, g * NT + (b + 1 + START))
                        for j in step:
                            mm = pe.matmul(psum[:, b, :], src_hot[:, j % RING, b * P:(b + 1) * P],
                                           dst_hot[:, j % RING, :], start=(j == 0), stop=(j == CG - 1))
                            if j == CG - 1:
                                mm.then_inc(s_bank, 1)
                            elif b == NT - 1:
                                mm.then_inc(s_used, 1)

            pe.wait_ge(s_ident, 3)
            pe.wait_ge(s_xr, HG * NG + START)
            for i in range(2 * KT):
                k, nh = i // 2, i % 2
                if i >= 6:
                    pe.wait_ge(s_xT, i - 5)
                else:
                    pe.wait_ge(s_bfree, NT * NG + i + 1 + START)
                for q in range(4):
                    mm = pe.transpose(psum[:, i % 6, q * P:(q + 1) * P], xt[:, 4 * nh + q, k * P:(k + 1) * P],
                                      ident[:])
                mm.then_inc(s_xTp, 1)
            for t in range(NT):
                if t < 6:
                    pe.wait_ge(s_xT, t + 7)
                else:
                    pe.wait_ge(s_mk[t % 2], (t - 6) // 2 + 1)
                turned = psum[:, t % 6, :].bitcast(BF16)
                for s in range(NT):
                    if t == 0:
                        pe.wait_ge(s_near, s + 1)
                    mm = pe.transpose(turned[:, s * P:(s + 1) * P], near[:, s, t * P:(t + 1) * P], ident_b[:])
                mm.then_inc(s_mp, 1)
            pe.wait_ge(s_vc, H + START)
            pe.wait_ge(s_bfree, NT * (NG + 1) + START)
            for t in range(NT):
                for k in range(KT):
                    if t % 4 == 0:
                        pe.wait_ge(s_xT, 2 * k + t // 4 + 1)
                    mm = pe.matmul(psum[:, 6, t * 2 * H:(t + 1) * 2 * H], xT[:, k, t * P:(t + 1) * P], V[:, k, :],
                                   start=(k == 0), stop=(k == KT - 1))
            pe.wait_ge(s_b1, 16)
            pe.transpose(psum[:, 6, P:P + H * KT], b1r[:], ident[0:H * KT, 0:H * KT]).then_inc(s_lcp, 1)


def heads(nc, env):
    W1, W2, b1c = env["W1"], env["W2"], env["b1c"]
    xh, xl, ct, lc, lc02 = (env[k] for k in ("xh", "xl", "ct", "lc", "lc02"))
    logit_rows, mask_dram, ab_dram, h2_dram = (env[k] for k in ("logit_rows", "mask_dram", "ab_dram", "h2_dram"))
    D = W2.shape[1]
    H = W1.shape[1] // D
    N = ct.shape[2]
    NT, KT = N // P, D // P
    HALF = N // 2
    DT = HALF // P
    S = START

    with ExitStack() as ctx:
        def sb(name, shape, dt):
            return ctx.enter_context(nc.sbuf_tensor(name, shape, dt))

        sem = Sems(nc, ctx)
        h2ps = ctx.enter_context(nc.psum_tensor("h2ps", [P, 6, 512], F32))
        bank = [ctx.enter_context(nc.psum_tensor(f"bank{i}", [P, 512], F32)) for i in range(2)]
        ph = [sb(f"p_high{i}", [P, NT, HALF], F16) for i in range(2)]
        pl = [sb(f"p_low{i}", [P, NT, HALF], F16) for i in range(2)]
        zh = sb("z_high", [P, KT, HALF], F32R)
        zl = sb("z_low", [P, KT, HALF], F32R)
        w1r = sb("w1_raw", [P, 2, KT, P], F32)
        w1h = sb("w1_high", [P, 2, KT, P], F32R)
        w1l = sb("w1_low", [P, 2, KT, P], F32R)
        w2r = sb("w2_raw", [P, 2, D], F32)
        w2h = sb("w2_high", [P, 2, D], F32R)
        w2l = sb("w2_low", [P, 2, D], F32R)
        hh = sb("h_high", [P, 3, HALF], F32R)
        hl = sb("h_low", [P, 3, HALF], F32R)
        work = env["work"]
        zt, ut, et = (work[:, 2 * i:2 * i + 2, :] for i in range(3))
        ab_rows = [sb(f"ab_rows{i}", [P, 2, HALF], F32) for i in range(2)]
        as_row = sb("as_row", [P, N], F32)
        mask = sb("mask_half", [P, DT, N], BF16)
        ta = sb("ta", [P, 2, HALF], F32)
        tb = sb("tb", [P, 2, HALF], F32)
        psums = sb("p_sums", [P, 2, HALF], F32)
        rden = sb("rden", [P, HALF], F32)
        junk = sb("junk_m", [P, 2, N], BF16)
        top = sb("top", [P, 4, DT], F32)
        ab = [sb(f"ab{i}", [P, 2, DT], F32) for i in range(2)]
        b1u = [sb(f"b1u{i}", [P, KT], F32) for i in range(2)]
        psum_high = sb("p_sums_high", [P, HALF], F32R)
        psum_low = sb("p_sums_low", [P, HALF], F32R)
        ones_raw = sb("ones_raw", [P, P], F32)
        ones = sb("ones", [P, P], F32R)
        ident = env["ident"]
        mask0, as_row0 = env["mask0"], work[:, 4:6, :]
        lg = ab_rows[1][0:H, :, :]

        m_ones = sem("ones_made")
        m_first = sem("first_rows_ready")
        m_fkept = sem("first_rows_kept")
        m_rows = sem("logit_rows_stored")
        m_mask = sem("mask_half_loaded")
        m_a2 = sem("a2_rows_loaded")
        m_as = sem("as_row_loaded")
        m_top = sem("maxima_taken")
        m_sp = sem("sp_waits_over")
        m_small = sem("maxima_steps")
        m_turn = sem("maximum_begun")
        m_ab = sem("ab_columns_made")
        m_abs = sem("ab_columns_stored")
        m_abr = [sem(f"ab_rows_loaded{i}") for i in range(2)]
        m_b1 = sem("b1_columns_taken")
        m_terms = sem("exponent_terms_made")
        m_expo = sem("exponents_made")
        m_exp = sem("exponentials_made")
        m_p = sem("weights_made")
        m_ph = sem("weights_high")
        m_pl = sem("weights_low")
        m_sum = sem("weights_summed")
        m_sumturn = sem("weights_sum_begun")
        m_sumhigh = sem("weights_sum_high")
        m_sumlow = sem("weights_sum_low")
        m_den = sem("denominator_ready")
        m_deneps = sem("denominator_kept")
        m_rden = sem("denominator_inverted")
        m_z = sem("z_ready")
        m_zt = sem("z_scaled")
        m_zh = sem("z_high_done")
        m_zl = sem("z_low_done")
        m_w1 = [sem(f"w1_loaded{i}") for i in range(2)]
        m_w2 = [sem(f"w2_loaded{i}") for i in range(2)]
        m_w1h, m_w1l = sem("w1_high_done"), sem("w1_low_done")
        m_w2h, m_w2l = sem("w2_high_done"), sem("w2_low_done")
        m_h = sem("h_ready")
        m_u = sem("h_biased")
        m_neg = sem("h_negative_part")
        m_eexp = sem("h_exp")
        m_elu = sem("h_elu")
        m_hh = sem("h_high_done")
        m_hl = sem("h_low_done")
        m_o = sem("h2_added")
        m_keep = sem("h2_half_copied")
        m_zero = sem("h2_zeroed")
        m_store = sem("h2_half_stored")
        block = ctx.enter_context(nc.Block())

        W1v = W1.rearrange("(k p) (c j) -> p k c j", p=P, j=P)
        W2v = W2.rearrange("(c p) d -> p c d", p=P)


        def counter(eng, u0):
            cache = {}

            def at(j, per, n):
                if isinstance(u0, int):
                    return (u0 + j) * per + n + S
                if per not in cache:
                    cache[per] = eng.snap(u0 * per)
                return cache[per] + (j * per + n + S)
            return at

        def load_stats(sp, v):
            hv, fv = (sp.snap(n) if not isinstance(v, int) else n for n in (v % H, (v // H) % 2))
            sp.wait_ge(m_top, v * DT + S)
            sp.sem_inc(m_sp, 1)
            sp.dma_start(as_row[:], logit_rows[bass.ds(hv, 1), :].to_broadcast([P, N])).then_inc(m_as, 16)
            sp.dma_start(mask[:], mask_dram[bass.ds(fv, 1), :, :, :]).then_inc(m_mask, 16)

        def spread(sp, v, par):
            sp.wait_ge(m_ab, v + (1 + S))
            sp.sem_inc(m_sp, 1)
            sp.wait_ge(m_terms, v * NT + (S - NT))
            sp.sem_inc(m_sp, 1)
            sp.dma_start(ab_dram[par].rearrange("a (t p) -> p a t", p=P), ab[par][:],
                         allow_slow_non_contiguous=True).then_inc(m_abs, 16)
            sp.wait_ge(m_abs, v * 16 + (16 + S))
            sp.sem_inc(m_sp, 1)
            sp.dma_start(ab_rows[par][:], ab_dram[par].partition_broadcast(P)).then_inc(m_abr[par], 16)

        def maxima(dve, v, par, mask=mask, as_row=as_row[:]):
            hv, tv = (dve.snap(n) if not isinstance(v, int) else n for n in (v % H, ((v // H) % 2) * DT))
            if isinstance(v, int) and v == 0:
                dve.wait_ge(m_fkept, 2)
            else:
                dve.wait_ge(m_as, v * 16 + (16 + S))
                dve.wait_ge(m_mask, v * 16 + (16 + S))
                dve.wait_ge(m_ab, v + S)
            for t in range(DT):
                dve.wait_ge(m_top, v * DT + (t - 1 + S))
                dve.sem_inc(m_turn, 1)
                dve.tensor_tensor_reduce(junk[:, t % 2, :], mask[:, t, :], as_row, 1.0, FAR, ALU.add,
                                         ALU.max, top[:, 0, t:t + 1]).then_inc(m_top, 1)
            ad = lc[:, bass.ds(tv, DT), bass.ds(hv + H, 1)].rearrange("p t o -> p (t o)")
            dve.wait_ge(m_top, v * DT + (DT + S))
            dve.tensor_tensor(top[:, 1, :], top[:, 0, :], ad, ALU.add).then_inc(m_small, 1)
            dve.wait_ge(m_small, v * 2 + (1 + S))
            dve.scalar_tensor_tensor(out=top[:, 2, :], in0=top[:, 1, :], scalar=SLOPE, in1=top[:, 1, :],
                                     op0=ALU.mult, op1=ALU.max).then_inc(m_small, 1)
            dve.wait_ge(m_small, v * 2 + (2 + S))
            dve.wait_ge(m_abs, v * 16 + S)
            dve.tensor_tensor(ab[par][:, 0, :], ad, top[:, 2, :], ALU.subtract)
            dve.scalar_tensor_tensor(out=ab[par][:, 1, :], in0=ad, scalar=SLOPE, in1=top[:, 2, :],
                                     op0=ALU.mult, op1=ALU.subtract).then_inc(m_ab, 1)

        def slot(x, s, first):
            if first and s % 3 == 2:
                return work[:, 0 if x is ta else 1, :]
            return x[:, s % (3 if first else 2), :]

        def exponent_terms(dve, at, j, s, par, hv, first=False):
            if first:
                dve.wait_ge(m_fkept, 6)
            elif s == 0:
                dve.wait_ge(m_abr[par], at(j, 8, 8 if par else 16))
            ring = 3 if first else 2
            if s >= ring or not first:
                dve.wait_ge(m_p, at(j, NT, s + 1 - ring))
            dve.tensor_scalar(slot(ta, s, first), ab_rows[par][:, 0, :], lc[:, s, bass.ds(hv, 1)], 0.0, ALU.add,
                              ALU.min)
            if s >= ring or not first:
                dve.wait_ge(m_pl, at(j, NT, s + 1 - ring))
                dve.wait_ge(m_sum, at(j, NT, s + 1 - ring))
            dve.tensor_scalar(slot(tb, s, first), ab_rows[par][:, 1, :], lc02[:, s, bass.ds(hv, 1)], 0.0, ALU.add,
                              ALU.min).then_inc(m_terms, 1)

        def exponent(dve, at, j, s, first=False):
            a, b = slot(ta, s, first), slot(tb, s, first)
            dve.wait_ge(m_terms, at(j, NT, s + 1))
            dve.tensor_tensor(a, a, b, ALU.max).then_inc(m_expo, 1)

        def weights(dve, at, j, s, tv, first=False):
            dve.wait_ge(m_exp, at(j, NT, s + 1))
            dve.tensor_tensor(slot(tb, s, first), slot(ta, s, first), ct[:, s, bass.ds(tv, HALF)],
                              ALU.mult).then_inc(m_p, 1)

        def weights_low(dve, at, j, s, par, first=False):
            dve.wait_ge(m_ph, at(j, NT, s + 1))
            dve.tensor_tensor(pl[par][:, s, :], slot(tb, s, first), ph[par][:, s, :], ALU.subtract)\
                .then_inc(m_pl, 1)

        def z_scaled(dve, at, j, k):
            dve.wait_ge(m_z, at(j, KT, k + 1))
            if k < 2:
                dve.wait_ge(m_zl, at(j, KT, 0))
                dve.wait_ge(m_rden, at(j, 1, 1))
            else:
                dve.wait_ge(m_zl, at(j, KT, k - 1))
            dve.tensor_tensor(zt[:, k % 2, :], bank[(k + 1) % 2][:], rden[:], ALU.mult).then_inc(m_zt, 1)

        def z_low(dve, at, j, k):
            dve.wait_ge(m_zh, at(j, KT, k + 1))
            dve.tensor_tensor(zl[:, k, :], zt[:, k % 2, :], f32(zh[:, k, :]), ALU.subtract).then_inc(m_zl, 1)

        def w1_low(dve, at, j, i):
            dve.wait_ge(m_w1h, at(j, KT, i + 1))
            dve.tensor_tensor(w1l[:, i % 2, :, :], w1r[:, i % 2, :, :], f32(w1h[:, i % 2, :, :]),
                              ALU.subtract).then_inc(m_w1l, 1)

        def w2_low(dve, at, j, i):
            dve.wait_ge(m_w2h, at(j, KT, i + 1))
            dve.tensor_tensor(w2l[:, i % 2, :], w2r[:, i % 2, :], f32(w2h[:, i % 2, :]),
                              ALU.subtract).then_inc(m_w2l, 1)

        def h_negative(dve, at, j, i):
            dve.wait_ge(m_u, at(j, KT, i + 1))
            dve.wait_ge(m_hl, at(j, KT, i - 1))
            dve.tensor_scalar(et[:, i % 2, :], ut[:, i % 2, :], 0.0, None, ALU.min).then_inc(m_neg, 1)

        def h_elu(dve, at, j, i):
            dve.wait_ge(m_eexp, at(j, KT, i + 1))
            dve.scalar_tensor_tensor(out=et[:, i % 2, :], in0=et[:, i % 2, :], scalar=-1.0, in1=ut[:, i % 2, :],
                                     op0=ALU.add, op1=ALU.max).then_inc(m_elu, 1)

        def h_low(dve, at, j, i):
            dve.wait_ge(m_hh, at(j, KT, i + 1))
            dve.tensor_tensor(hl[:, i % 3, :], et[:, i % 2, :], f32(hh[:, i % 3, :]), ALU.subtract).then_inc(m_hl, 1)

        def exponential(act, at, j, s, first=False):
            act.wait_ge(m_expo, at(j, NT, s + 1))
            act.activation(slot(ta, s, first), slot(ta, s, first), ACT.Exp).then_inc(m_exp, 1)

        def weights_high(act, at, j, s, par, first=False):
            act.wait_ge(m_p, at(j, NT, s + 1))
            if s == 0:
                act.wait_ge(m_z, at(j, KT, -KT))
            act.activation(ph[par][:, s, :], slot(tb, s, first), ACT.Copy).then_inc(m_ph, 1)

        def sum_high(act, at, j, par):
            act.wait_ge(m_sum, at(j, NT, NT))
            act.wait_ge(m_den, at(j, 1, 0))
            act.activation(psum_high[:], psums[:, par, :], ACT.Copy).then_inc(m_sumhigh, 1)

        def z_high(act, at, j, k):
            act.wait_ge(m_zt, at(j, KT, k + 1))
            if k == 0:
                act.wait_ge(m_h, at(j, KT, 0))
            act.activation(zh[:, k, :], zt[:, k % 2, :], ACT.Copy).then_inc(m_zh, 1)

        def w1_high(act, at, j, i):
            act.wait_ge(m_w1[i % 2], at(j, 8 * KT, 16 * (i // 2 + 1)))
            act.wait_ge(m_h, at(j, KT, i - 1))
            act.activation(w1h[:, i % 2, :, :], w1r[:, i % 2, :, :], ACT.Copy).then_inc(m_w1h, 1)

        def w2_high(act, at, j, i):
            act.wait_ge(m_w2[i % 2], at(j, 8 * KT, 16 * (i // 2 + 1)))
            act.wait_ge(m_o, at(j, KT, i - 1))
            act.activation(w2h[:, i % 2, :], w2r[:, i % 2, :], ACT.Copy).then_inc(m_w2h, 1)

        def h_biased(act, at, j, i):
            act.wait_ge(m_h, at(j, KT, i + 1))
            if i == 0:
                act.wait_ge(m_b1, at(j, 1, 1))
            act.wait_ge(m_elu, at(j, KT, i - 1))
            act.activation(ut[:, i % 2, :], bank[(i + 1) % 2][:], ACT.Identity, bias=b1u[j][:, i:i + 1])\
                .then_inc(m_u, 1)

        def h_exp(act, at, j, i):
            act.wait_ge(m_neg, at(j, KT, i + 1))
            act.activation(et[:, i % 2, :], et[:, i % 2, :], ACT.Exp).then_inc(m_eexp, 1)

        def h_high(act, at, j, i):
            act.wait_ge(m_elu, at(j, KT, i + 1))
            act.wait_ge(m_o, at(j, KT, i - 2))
            act.activation(hh[:, i % 3, :], et[:, i % 2, :], ACT.Copy).then_inc(m_hh, 1)

        W1_AT = {0: 0, 1: 1, 7: 2, 8: 3, 9: 4, 10: 5}
        W2_AT = {0: 0, 1: 1, 9: 2, 10: 3, 11: 4, 12: 5}
        P_AT = {2: 0, 3: 1, 4: 2, 5: 3, 8: 4, 9: 5, 10: 6, 11: 7}
        MAXIMA_AT, SUM_AT = 13, 12
        STEPS = range(14)

        @block.sync
        def _(sp):
            for s in (m_abr[1], *m_w1, *m_w2, m_store):
                sp.sem_inc(s, S)
            for s in (m_as, m_mask, m_abs, m_abr[0]):
                sp.sem_inc(s, 16 + S)
            for i in range(2):
                sp.dma_start(w1r[:, i, :, :], W1v[:, :, i, :]).then_inc(m_w1[i], 16)
                sp.dma_start(w2r[:, i, :], W2v[:, i, :]).then_inc(m_w2[i], 16)
            sp.wait_ge(m_fkept, 4)
            sp.dma_start(logit_rows, lg.rearrange("h a b -> h (a b)")).then_inc(m_rows, 16)
            sp.dma_start(env["a2_rows"][:, 0, :], env["a_s2"].to_broadcast([P, D])).then_inc(m_a2, 16)
            sp.dma_start(env["a2_rows"][:, 1, :], env["a_d2"].to_broadcast([P, D])).then_inc(m_a2, 16)
            sp.wait_ge(m_rows, 16)
            load_stats(sp, 1)
            for half in (0, H):
                with sp.Fori(0, H, 2) as pair:
                    u0 = sp.snap(half + pair)
                    at = counter(sp, u0)
                    for j in range(2):
                        u = sp.snap(u0 + j)
                        head = sp.snap(u % H)
                        tile0 = sp.snap(head * KT)
                        next0 = sp.snap(((u + 1) % H) * KT)

                        behind = [sp.snap(tile0 + (i + 2) if i < KT - 2 else next0 + (i + 2 - KT))
                                  for i in range(KT)]

                        def tile(i):
                            return bass.ds(behind[i], 1)
                        spread(sp, u + 1, (j + 1) % 2)
                        load_stats(sp, u + 2)
                        for t in STEPS:
                            if t in W1_AT:
                                sp.wait_ge(m_w1l, at(j, KT, W1_AT[t] + 1))
                                sp.sem_inc(m_sp, 1)
                                sp.dma_start(w1r[:, W1_AT[t] % 2, :, :], W1v[:, :, tile(W1_AT[t]), :])\
                                    .then_inc(m_w1[W1_AT[t] % 2], 16)
                            if t in W2_AT:
                                sp.wait_ge(m_w2l, at(j, KT, W2_AT[t] + 1))
                                sp.sem_inc(m_sp, 1)
                                sp.dma_start(w2r[:, W2_AT[t] % 2, :], W2v[:, tile(W2_AT[t]), :])\
                                    .then_inc(m_w2[W2_AT[t] % 2], 16)
                if half == 0:
                    sp.wait_ge(m_keep, 6 + S)
                    sp.sem_inc(m_sp, 1)
                    sp.dma_start(h2_dram, work[:]).then_inc(m_store, 16)
            sp.wait_ge(m_store, 16 + S)
            sp.wait_ge(m_a2, 32)
            sp.wait_ge(m_abs, 16 * (2 * H + 1) + S)
            sp.wait_ge(m_as, 16 * (2 * H + 2) + S)
            sp.wait_ge(m_mask, 16 * (2 * H + 2) + S)
            sp.wait_ge(m_abr[0], 16 * (H + 1) + S)
            for i in range(2):
                sp.wait_ge(m_w1[i], 16 * (KT * H + 1) + S)
                sp.wait_ge(m_w2[i], 16 * (KT * H + 1) + S)

        @block.gpsimd
        def _(pool):
            pool.memset(ones_raw[:], 1.0).then_inc(m_ones, 1)
            pool.sem_inc(m_sum, S)
            pool.sem_inc(m_sumlow, S)

            def add(at, j, s, par, first=False):
                pool.wait_ge(m_p, at(j, NT, s + 1))
                if s == 0:
                    pool.sem_inc(m_sumturn, 1)
                    pool.wait_ge(m_sumlow, at(j, 1, -1))
                    pool.sem_inc(m_sumturn, 1)
                    pool.tensor_copy(psums[:, par, :], slot(tb, s, first)).then_inc(m_sum, 1)
                else:
                    pool.wait_ge(m_sum, at(j, NT, s))
                    pool.tensor_tensor(psums[:, par, :], psums[:, par, :], slot(tb, s, first), ALU.add)\
                        .then_inc(m_sum, 1)

            def sum_low(at, j, par):
                pool.wait_ge(m_sumhigh, at(j, 1, 1))
                pool.wait_ge(m_den, at(j, 1, 0))
                pool.tensor_tensor(psum_low[:], psums[:, par, :], f32(psum_high[:]), ALU.subtract)\
                    .then_inc(m_sumlow, 1)

            at = counter(pool, 0)
            for s in range(NT):
                add(at, 0, s, 0, first=True)
            sum_low(at, 0, 0)
            with pool.Fori(0, 2 * H, 2) as u0:
                at = counter(pool, u0)
                for j in range(2):
                    for s in range(NT):
                        add(at, j + 1, s, (j + 1) % 2)
                    sum_low(at, j + 1, (j + 1) % 2)

        @block.vector
        def _(dve):
            for s in (m_top, m_small, m_ab, m_terms, m_expo, m_p, m_pl, m_deneps, m_rden, m_zt, m_zl, m_w1l,
                      m_w2l, m_neg, m_elu, m_hl, m_keep, m_zero, m_b1):
                dve.sem_inc(s, S)
            maxima(dve, 0, 0, mask0, as_row0.rearrange("p a b -> p (a b)"))
            at = counter(dve, 0)
            for s in range(NT + 2):
                if s < NT:
                    exponent_terms(dve, at, 0, s, 0, 0, first=True)
                    exponent(dve, at, 0, s, first=True)
                if 1 <= s <= NT:
                    weights(dve, at, 0, s - 1, 0, first=True)
                if s >= 2:
                    weights_low(dve, at, 0, s - 2, 0, first=True)
            maxima(dve, 1, 1)
            with dve.Fori(0, 2 * H, H) as half:
                hn = dve.snap(half // H)
                dve.wait_ge(m_keep, hn * 6 + S)
                dve.sem_inc(m_turn, 1)
                for b in range(6):
                    dve.memset(h2ps[:, b, :], 0.0).then_inc(m_zero, 1)
                with dve.Fori(0, H, 2) as pair:
                    u0 = dve.snap(half + pair)
                    at = counter(dve, u0)
                    for j in range(2):
                        v = dve.snap(u0 + (j + 1))
                        hv = dve.snap(v % H)
                        tv = dve.snap(((v // H) % 2) * HALF)
                        par = (j + 1) % 2
                        for t in STEPS:
                            k, i, s = t - 1, t - 7, P_AT.get(t)
                            low = P_AT.get(t - 1)
                            if t == 0:
                                dve.wait_ge(m_den, at(j, 1, 1))
                                dve.wait_ge(m_zt, at(j, KT, 0))
                                dve.tensor_scalar(rden[:], bank[0][:], EPS_DEN, XS, ALU.add, ALU.mult)\
                                    .then_inc(m_deneps, 1)
                                dve.wait_ge(m_deneps, at(j, 1, 1))
                                dve.reciprocal(rden[:], rden[:]).then_inc(m_rden, 1)
                                dve.wait_ge(m_u, at(j, KT, -KT))
                                dve.tensor_copy(b1u[j][:], b1c[:, bass.ds(dve.snap(((u0 + j) % H) * KT), KT)])\
                                    .then_inc(m_b1, 1)
                            if 0 <= k < KT:
                                if k == 0:
                                    dve.wait_ge(m_store, (half // H) * 16 + S)
                                z_scaled(dve, at, j, k)
                            if 0 <= i < KT:
                                h_negative(dve, at, j, i)
                            if t in W1_AT and s is None:
                                w1_low(dve, at, j, W1_AT[t])
                            if low is not None:
                                weights_low(dve, at, j + 1, low, par)
                            if s is not None:
                                exponent_terms(dve, at, j + 1, s, par, hv)
                            if 0 <= i < KT:
                                h_elu(dve, at, j, i)
                            if s is not None:
                                exponent(dve, at, j + 1, s)
                            if 0 <= k < KT:
                                z_low(dve, at, j, k)
                            if 0 <= i < KT:
                                h_low(dve, at, j, i)
                            if t in W1_AT and s is not None:
                                w1_low(dve, at, j, W1_AT[t])
                            if s is not None:
                                weights(dve, at, j + 1, s, tv)
                            if t in W2_AT:
                                w2_low(dve, at, j, W2_AT[t])
                            if t == MAXIMA_AT:
                                maxima(dve, dve.snap(u0 + (j + 2)), j)
                dve.wait_ge(m_o, half * KT + (H * KT + S))
                dve.wait_ge(m_hl, half * KT + (H * KT + S))
                for b in range(3, 6):
                    dve.tensor_copy(work[:, b, :], h2ps[:, b, :]).then_inc(m_keep, 1)

        @block.scalar
        def _(act):
            for s in (m_exp, m_ph, m_zh, m_w1h, m_w2h, m_u, m_eexp, m_hh, m_sumhigh):
                act.sem_inc(s, S)
            act.wait_ge(m_ones, 1)
            act.activation(ones[:], ones_raw[:], ACT.Copy).then_inc(m_ones, 1)
            for n, out in enumerate((as_row0[:, 0, :], as_row0[:, 1, :], lg[:, 0, :], lg[:, 1, :],
                                     ab_rows[0][:, 0, :], ab_rows[0][:, 1, :])):
                act.wait_ge(m_first, n + 1)
                act.activation(out, bank[n % 2][0:H if n in (2, 3) else P, :], ACT.Copy).then_inc(m_fkept, 1)
            at = counter(act, 0)
            for s in range(NT + 1):
                if s < NT:
                    exponential(act, at, 0, s, first=True)
                if s >= 1:
                    weights_high(act, at, 0, s - 1, 0, first=True)
            sum_high(act, at, 0, 0)
            with act.Fori(0, 2 * H, H) as half:
                with act.Fori(0, H, 2) as pair:
                    u0 = act.snap(half + pair)
                    at = counter(act, u0)
                    for j in range(2):
                        par = (j + 1) % 2
                        for t in STEPS:
                            k, i, s = t - 1, t - 7, P_AT.get(t)
                            if 0 <= i < KT:
                                h_biased(act, at, j, i)
                            if t in W1_AT:
                                w1_high(act, at, j, W1_AT[t])
                            if 0 <= k < KT:
                                z_high(act, at, j, k)
                            if 0 <= i < KT:
                                h_exp(act, at, j, i)
                            if t in W2_AT:
                                w2_high(act, at, j, W2_AT[t])
                            if 0 <= i < KT:
                                h_high(act, at, j, i)
                            if s is not None:
                                exponential(act, at, j + 1, s)
                            if s is not None:
                                weights_high(act, at, j + 1, s, par)
                            if t == SUM_AT:
                                sum_high(act, at, j + 1, par)
                act.wait_ge(m_o, half * KT + (H * KT + S))
                act.wait_ge(m_hl, half * KT + (H * KT + S))
                for b in range(3):
                    act.activation(work[:, b, :], h2ps[:, b, :], ACT.Copy).then_inc(m_keep, 1)

        @block.tensor
        def _(pe):
            for s in (m_den, m_z, m_h, m_o):
                pe.sem_inc(s, S)
            pe.wait_ge(m_ones, 2)
            for n in range(6):
                what, half = divmod(n, 2)
                if n >= 2:
                    pe.wait_ge(m_fkept, n - 1)
                if n == 4:
                    pe.wait_ge(m_ab, 1 + S)
                for t in range(DT):
                    to = slice(t * P, (t + 1) * P)
                    if what == 1:
                        mm = pe.transpose(bank[half][0:H, to], lc[:, half * DT + t, 0:H], ident[:])
                    else:
                        column = lc[:, half * DT + t, 0:1] if what == 0 else ab[0][:, half, t:t + 1]
                        mm = pe.matmul(bank[half][:, to], column.to_broadcast([P, P]), ident[:], start=True,
                                       stop=True)
                mm.then_inc(m_first, 1)

            def product(out, terms, **kw):
                for n, (a, b) in enumerate(terms):
                    mm = pe.matmul(out, a, b, start=(n == 0), stop=(n == len(terms) - 1), **kw)
                return mm

            def z_tile(at, j, k):
                if k == 0:
                    pass
                elif k == 1:
                    pe.wait_ge(m_deneps, at(j, 1, 1))
                else:
                    pe.wait_ge(m_zt, at(j, KT, k - 1))
                for s in range(NT):
                    if k == 0:
                        pe.wait_ge(m_pl, at(j, NT, s + 1))
                    kk = slice(k * P, (k + 1) * P)
                    for n, (a, b) in enumerate(((xh, ph), (xh, pl), (xl, ph))):
                        mm = pe.matmul(bank[(k + 1) % 2][:], a[:, s, kk], b[j][:, s, :], start=(s == 0 and n == 0),
                                       stop=(s == NT - 1 and n == 2))
                mm.then_inc(m_z, 1)

            def h_tile(at, j, i):
                pe.wait_ge(m_w1l, at(j, KT, i + 1))
                if i < 2:
                    pe.wait_ge(m_zt, at(j, KT, KT - 1 + i))
                else:
                    pe.wait_ge(m_u, at(j, KT, i - 1))
                for k in range(KT):
                    if i == 0:
                        pe.wait_ge(m_zl, at(j, KT, k + 1))
                    for n, (a, b) in enumerate(((w1h, zh), (w1h, zl), (w1l, zh))):
                        mm = pe.matmul(bank[(i + 1) % 2][:], a[:, i % 2, k, :], b[:, k, :], start=(k == 0 and n == 0),
                                       stop=(k == KT - 1 and n == 2))
                mm.then_inc(m_h, 1)

            def h2_tile(at, j, i, hn):
                pe.wait_ge(m_hl, at(j, KT, i + 1))
                pe.wait_ge(m_w2l, at(j, KT, i + 1))
                if j == 0 and i == 0:
                    pe.wait_ge(m_zero, hn * 6 + (6 + S))
                for a, b in ((hh, w2h), (hh, w2l), (hl, w2h)):
                    for t in range(DT):
                        at0 = t * D
                        while at0 < (t + 1) * D:
                            to = min((t + 1) * D, (at0 // 512 + 1) * 512)
                            mm = pe.matmul(h2ps[:, at0 // 512, at0 % 512:at0 % 512 + to - at0],
                                           a[:, i % 3, t * P:(t + 1) * P], b[:, i % 2, at0 - t * D:to - t * D],
                                           start=False, stop=True, skip_group_check=True)
                            at0 = to
                mm.then_inc(m_o, 1)

            with pe.Fori(0, 2 * H, H) as half:
                hn = pe.snap(half // H)
                with pe.Fori(0, H, 2) as pair:
                    u0 = pe.snap(half + pair)
                    at = counter(pe, u0)
                    for j in range(2):
                        pe.wait_ge(m_sumlow, at(j, 1, 1))
                        pe.matmul(bank[0][:], ones[:], psum_high[:], start=True, stop=False)
                        pe.matmul(bank[0][:], ones[:], psum_low[:], start=False, stop=True).then_inc(m_den, 1)
                        for k in range(KT):
                            z_tile(at, j, k)
                        h_tile(at, j, 0)
                        h_tile(at, j, 1)
                        for i in range(2, KT):
                            h_tile(at, j, i)
                            h2_tile(at, j, i - 2, hn)
                        h2_tile(at, j, KT - 2, hn)
                        h2_tile(at, j, KT - 1, hn)


def largest_neighbour(dve, env, t):
    small, mask, junk, as_row = (env[k] for k in ("small2", "mask2", "junk2", "as_row2"))
    return dve.tensor_tensor_reduce(junk[:, t % 2, :], mask[:, t % mask.shape[1], :], as_row, 1.0, FAR, ALU.add,
                                    ALU.max, small[:, 0, t:t + 1])


def score_maxima(dve, env, hf, steps, done):
    small, lc2, ab2 = env["small2"], env["lc2"], env["ab2"]
    HT = ab2.shape[2] // 2
    c = slice(hf * HT, (hf + 1) * HT)
    dve.tensor_tensor(small[:, 1, c], small[:, 0, c], lc2[:, 1, c], ALU.add).then_inc(steps, 1)
    dve.wait_ge(steps, done + 1)
    dve.scalar_tensor_tensor(out=small[:, 2, c], in0=small[:, 1, c], scalar=SLOPE, in1=small[:, 1, c],
                             op0=ALU.mult, op1=ALU.max).then_inc(steps, 1)
    dve.wait_ge(steps, done + 2)
    dve.tensor_tensor(ab2[:, 0, c], lc2[:, 1, c], small[:, 2, c], ALU.subtract).then_inc(steps, 1)
    dve.scalar_tensor_tensor(out=ab2[:, 1, c], in0=lc2[:, 1, c], scalar=SLOPE, in1=small[:, 2, c],
                             op0=ALU.mult, op1=ALU.subtract).then_inc(steps, 1)


def second_logits(nc, env):
    h2_dram, mask_dram, arow = (env[k] for k in ("h2_dram", "mask_dram", "a2_rows"))
    hh, hl, lc2, ab_rows, xt, work = (env[k] for k in ("h2h", "h2l", "lc2", "ab_rows2", "xt2", "work"))
    ab2, mask, junk, as_row, b2row = (env[k] for k in ("ab2", "mask2", "junk2", "as_row2", "b2_row"))
    ident, ones, zeros = (env[k] for k in ("ident2", "ones2", "zeros2"))
    NT, N = ab_rows.shape[2] // P, ab_rows.shape[2]
    D = xt.shape[2]
    HT, HALF = NT // 2, N // 2

    with ExitStack() as ctx:
        def sb(name, shape, dt):
            return ctx.enter_context(nc.sbuf_tensor(name, shape, dt))

        sem = Sems(nc, ctx)
        ps = ctx.enter_context(nc.psum_tensor("l2_ps", [P, 4, 512], F32))
        hraw = sb("h2_first_half", [P, HT, D], F32)

        t_h = sem("h2_loaded")
        t_b2 = sem("b2_loaded")
        t_x = sem("x_back")
        t_mask = sem("mask2_loaded")
        t_c = sem("constants_made")
        t_sum = sem("a2_sums")
        t_hi = sem("h2_high_done")
        t_row = sem("as2_row_ready")
        t_back = sem("as2_row_kept")
        t_max = sem("maxima2_taken")
        t_small = sem("small2_steps")
        t_abp = sem("ab2_rows_ready")
        block = ctx.enter_context(nc.Block())

        TILES = [*range(HT, NT), *range(HT)]

        def raw(t):
            half = hraw[:].rearrange("p t d -> p (t d)") if t < HT else work[:].rearrange("p b c -> p (b c)")
            return half[:, t % HT * D:(t % HT + 1) * D]

        @block.sync
        def _(sp):
            sp.dma_start(hraw[:].rearrange("p t d -> p (t d)"), h2_dram.rearrange("p b c -> p (b c)"))\
                .then_inc(t_h, 16)
            sp.dma_start(b2row[:], env["b2"].partition_broadcast(P)).then_inc(t_b2, 16)
            sp.dma_start(mask[:], mask_dram[0]).then_inc(t_mask, 16)
            sp.dma_start(xt[:], env["x"].rearrange("(t p) d -> p t d", p=P)).then_inc(t_x, 16)

        @block.gpsimd
        def _(pool):
            pool.memset(ident[:], 0.0).then_inc(t_c, 1)
            pool.wait_ge(t_c, 1)
            pool.affine_select(out=ident[:], in_=ident[:], compare_op=ALU.not_equal, fill=1.0, base=0,
                               pattern=[[-1, P]], channel_multiplier=1).then_inc(t_c, 1)
            pool.memset(ones[:], 1.0).then_inc(t_c, 1)
            pool.memset(zeros[:], 0.0).then_inc(t_c, 1)
            for n, t in enumerate(TILES):
                pool.wait_ge(t_hi, n + 1)
                pool.tensor_tensor(hl[:, t, 0:D], raw(t), f32(hh[:, t, 0:D]), ALU.subtract)
            pool.wait_ge(t_b2, 16)
            pool.wait_ge(t_x, 16)
            for t in range(HT):
                pool.tensor_tensor(xt[:, t, :], xt[:, t, :], b2row[:], ALU.add)

        @block.vector
        def _(dve):
            for n, t in enumerate(TILES):
                if t == 0:
                    dve.wait_ge(t_h, 16)
                for sd in range(2):
                    if n >= 1:
                        dve.wait_ge(t_sum, 2 * n + sd - 1)
                    dve.tensor_tensor_reduce(junk[:, sd, 0:D], raw(t), arow[:, sd, :], 1.0, 0.0, ALU.mult,
                                             ALU.add, lc2[:, sd, t:t + 1]).then_inc(t_sum, 1)
            dve.wait_ge(t_sum, 2 * NT)
            dve.tensor_scalar(lc2[:, 2, :], lc2[:, 0, :], SLOPE, None, ALU.mult).then_inc(t_small, 1)
            dve.wait_ge(t_back, 2)
            dve.wait_ge(t_mask, 16)
            for t in range(HT):
                if t >= 2:
                    dve.wait_ge(t_max, t - 1)
                largest_neighbour(dve, env, t).then_inc(t_max, 1)
            dve.wait_ge(t_max, HT)
            score_maxima(dve, env, 0, t_small, 1)

        @block.scalar
        def _(act):
            for n, t in enumerate(TILES):
                if t == 0:
                    act.wait_ge(t_h, 16)
                act.activation(hh[:, t, 0:D], raw(t), ACT.Copy).then_inc(t_hi, 1)
            act.wait_ge(t_c, 4)
            act.activation(hh[:, :, D:D + 2], ones[:].unsqueeze(1).to_broadcast([P, NT, 2]), ACT.Copy)
            act.activation(hl[:, :, D:D + 2], zeros[:, 0:2].unsqueeze(1).to_broadcast([P, NT, 2]), ACT.Copy)
            for hf in range(2):
                act.wait_ge(t_row, hf + 1)
                act.activation(as_row[:, hf * HALF:(hf + 1) * HALF], ps[:, hf, :], ACT.Copy).then_inc(t_back, 1)
            for a in range(2):
                act.wait_ge(t_abp, a + 1)
                act.activation(ab_rows[:, a, 0:HALF], ps[:, 2 + a, :], ACT.Copy)

        @block.tensor
        def _(pe):
            def to_rows(out, columns):
                for t in range(HT):
                    mm = pe.matmul(out[:, t * P:(t + 1) * P], columns[:, t:t + 1].to_broadcast([P, P]), ident[:],
                                   start=True, stop=True)
                return mm

            pe.wait_ge(t_c, 2)
            pe.wait_ge(t_sum, 2 * NT)
            for hf in range(2):
                to_rows(ps[:, hf, :], lc2[:, 0, hf * HT:(hf + 1) * HT]).then_inc(t_row, 1)
            pe.wait_ge(t_small, 5)
            for a in range(2):
                to_rows(ps[:, 2 + a, :], ab2[:, a, 0:HT]).then_inc(t_abp, 1)


def second_attention(nc, env):
    ct, chi, clo, hh, hl, lc2, ab_rows = (env[k] for k in ("ct", "chi", "clo", "h2h", "h2l", "lc2", "ab_rows2"))
    xt, mv, root, dinv, work = (env[k] for k in ("xt2", "mv2", "root2", "dinv", "work"))
    ab2, mask, b2row, ab_dram, mask_dram = (env[k] for k in ("ab2", "mask2", "b2_row", "ab_dram", "mask_dram"))
    ident, ones, zeros = (env[k] for k in ("ident2", "ones2", "zeros2"))
    NT, N = ct.shape[1], ct.shape[2]
    D = xt.shape[2]
    HT, HALF = NT // 2, N // 2

    with ExitStack() as ctx:
        def sb(name, shape, dt):
            return ctx.enter_context(nc.sbuf_tensor(name, shape, dt))

        sem = Sems(nc, ctx)
        ps = ctx.enter_context(nc.psum_tensor("a2_ps", [P, 8, 512], F32))
        ph = [sb(f"p2_high{i}", [P, NT, HALF], F32R) for i in range(2)]
        pl = [sb(f"p2_low{i}", [P, NT, HALF], F32R) for i in range(2)]
        cf = env["count_f"]
        ta, tb = work[:, 0:3, :], work[:, 3:6, :]
        rd = sb("rd2", [P, 2, NT], F32)
        stats = sb("stats2", [P, NT, 2, 6], F32)

        t_mask = sem("mask2_second_half_loaded")
        t_max = sem("maxima2_taken")
        t_small = sem("small2_steps")
        t_abs = sem("ab2_columns_stored")
        t_abr = sem("ab2_rows_loaded")
        t_xb = sem("x_biased")
        t_terms = sem("terms2_made")
        t_expo = sem("exponents2_made")
        t_exp = sem("exponentials2_made")
        t_p = sem("weights2_made")
        t_ph = sem("weights2_high")
        t_pl = sem("weights2_low")
        t_cf = sem("counts_float")
        t_loop = sem("loops_added")
        t_ch = sem("counts_high")
        t_cl = sem("counts_low")
        t_deg = sem("degrees_summed")
        t_dk = sem("degrees_kept")
        t_o = sem("attention2_tile")
        t_rd = sem("sum2_steps")
        t_x1 = sem("x1_parts")
        t_st = sem("stats2_steps")
        t_root = sem("root2_taken")
        block = ctx.enter_context(nc.Block())

        def halves(hf):
            return slice(hf * HALF, (hf + 1) * HALF)

        @block.sync
        def _(sp):
            sp.dma_start(mask[:], mask_dram[1]).then_inc(t_mask, 16)
            sp.wait_ge(t_small, 4)
            for a in range(2):
                sp.dma_start(ab_dram[0, a].rearrange("(t p) -> p t", p=P), ab2[:, a, HT:NT],
                             allow_slow_non_contiguous=True).then_inc(t_abs, 16)
            sp.wait_ge(t_abs, 32)
            sp.dma_start(ab_rows[:, :, HALF:N], ab_dram[0].partition_broadcast(P)).then_inc(t_abr, 16)

        @block.gpsimd
        def _(pool):
            for n in range(2 * NT):
                hf, s = divmod(n, NT)
                pool.wait_ge(t_ph, n + 1)
                pool.tensor_tensor(pl[hf][:, s, :], tb[:, n % 3, :], f32(ph[hf][:, s, :]), ALU.subtract)\
                    .then_inc(t_pl, 1)
            for s in range(NT):
                pool.wait_ge(t_cf, s + 1)
                diag = cf[:, s % 2, s * P:(s + 1) * P]
                pool.tensor_tensor(diag, diag, ident[:], ALU.add).then_inc(t_loop, 1)

        @block.vector
        def _(dve):
            def terms(n):
                hf, s = divmod(n, NT)
                if n == NT:
                    dve.wait_ge(t_abr, 16)
                if n >= 3:
                    dve.wait_ge(t_p, n - 2)
                    dve.wait_ge(t_pl, n - 2)
                dve.tensor_scalar(ta[:, n % 3, :], ab_rows[:, 0, halves(hf)], lc2[:, 0, s:s + 1], 0.0, ALU.add,
                                  ALU.min)
                dve.tensor_scalar(tb[:, n % 3, :], ab_rows[:, 1, halves(hf)], lc2[:, 2, s:s + 1], 0.0, ALU.add,
                                  ALU.min).then_inc(t_terms, 1)
                dve.wait_ge(t_terms, n + 1)
                dve.tensor_tensor(ta[:, n % 3, :], ta[:, n % 3, :], tb[:, n % 3, :], ALU.max).then_inc(t_expo, 1)

            def weights(n):
                hf, s = divmod(n, NT)
                dve.wait_ge(t_exp, n + 1)
                dve.tensor_tensor(tb[:, n % 3, :], ta[:, n % 3, :], ct[:, s, halves(hf)], ALU.mult).then_inc(t_p, 1)

            def tile_out(t):
                a, b = ps[:, 2 * (t % 4), :], ps[:, 2 * (t % 4) + 1, :]
                dve.wait_ge(t_o, t + 1)
                dve.tensor_scalar(rd[:, 0, t:t + 1], b[:, D - 384:D - 383], EPS_DEN, None, ALU.add).then_inc(t_rd, 1)
                dve.wait_ge(t_rd, 2 * t + 1)
                dve.reciprocal(rd[:, 1, t:t + 1], rd[:, 0, t:t + 1]).then_inc(t_rd, 1)
                dve.wait_ge(t_rd, 2 * t + 2)
                if t >= HT:
                    dve.wait_ge(t_xb, t - HT + 1)
                for c, bankc in enumerate((a, b)):
                    part = xt[:, t, c * 384:(c + 1) * 384]
                    dve.scalar_tensor_tensor(out=part, in0=bankc[:, 0:384], scalar=rd[:, 1, t:t + 1], in1=part,
                                             op0=ALU.mult, op1=ALU.add).then_inc(t_x1, 1)
                for c in range(2):
                    dve.wait_ge(t_x1, 2 * t + c + 1)
                    dve.bn_stats(stats[:, t, c, :], xt[:, t, c * 384:(c + 1) * 384]).then_inc(t_st, 1)
                dve.wait_ge(t_st, 3 * t + 2)
                dve.bn_aggr(mv[:, t, :], stats[:, t, :, :].rearrange("p a b -> p (a b)")).then_inc(t_st, 1)

            def counts_low(s):
                dve.wait_ge(t_ch, s + 1)
                dve.wait_ge(t_p, NT + s + 1)
                dve.tensor_tensor(clo[:, s, :], cf[:, s % 2, :], chi[:, s, :], ALU.subtract).then_inc(t_cl, 1)

            def x_biased(t):
                dve.tensor_tensor(xt[:, t, :], xt[:, t, :], b2row[:], ALU.add).then_inc(t_xb, 1)

            for n in range(2 * NT + 1):
                if n == 2 * NT - 1:
                    tile_out(0)
                if n < 2 * NT:
                    terms(n)
                if n >= 1:
                    weights(n - 1)
                if 1 <= n <= HT:
                    if n == 1:
                        dve.wait_ge(t_mask, 16)
                    if n >= 3:
                        dve.wait_ge(t_max, n - 2)
                    largest_neighbour(dve, env, HT + n - 1).then_inc(t_max, 1)
                if n == HT:
                    dve.wait_ge(t_max, HT)
                    score_maxima(dve, env, 1, t_small, 0)
            for t in range(NT):
                if t == 2:
                    x_biased(HT)
                if t == NT - 1:
                    dve.wait_ge(t_deg, 1)
                    dve.tensor_copy(root[:, 0, NT:2 * NT], ps[:, 0, 0:2 * NT].rearrange("p (t o) -> p t o", o=2)
                                    [:, :, 0:1].rearrange("p t o -> p (t o)")).then_inc(t_dk, 1)
                if t > 0:
                    tile_out(t)
                if 1 <= t <= HT:
                    counts_low(2 * t - 2)
                    counts_low(2 * t - 1)
                    if t < HT:
                        x_biased(HT + t)
            done = 3 * NT
            dve.wait_ge(t_dk, 1)
            dve.wait_ge(t_st, done)
            dve.tensor_scalar(root[:, 0, 0:NT], mv[:, :, 1:2].rearrange("p t o -> p (t o)"), EPS_LN, None,
                              ALU.add).then_inc(t_st, 1)
            dve.wait_ge(t_root, 2)
            dve.reciprocal(root[:, 2, :], root[:, 1, :]).then_inc(t_st, 1)
            dve.wait_ge(t_st, done + 2)
            dve.tensor_tensor(root[:, 3, :], root[:, 0, :], root[:, 2, :], ALU.mult).then_inc(t_st, 1)
            dve.wait_ge(t_st, done + 3)
            dve.tensor_tensor(root[:, 4, :], root[:, 1, :], root[:, 3, :], ALU.add).then_inc(t_st, 1)
            dve.wait_ge(t_st, done + 4)
            dve.tensor_scalar(root[:, 3, :], root[:, 4, :], 0.5, None, ALU.mult).then_inc(t_st, 1)
            dve.wait_ge(t_st, done + 5)
            dve.reciprocal(root[:, 5, :], root[:, 3, :]).then_inc(t_st, 1)
            dve.wait_ge(t_st, done + 6)
            dve.tensor_scalar(dinv[:, 0, :], root[:, 5, NT:2 * NT], XS, None, ALU.mult)
            dve.tensor_scalar(dinv[:, 1, :], root[:, 5, NT:2 * NT], 1.0 / XS, None, ALU.mult)

        @block.scalar
        def _(act):
            def counts_float(s):
                if s >= 2:
                    act.wait_ge(t_cl, s - 1)
                act.activation(cf[:, s % 2, :], ct[:, s, :], ACT.Copy).then_inc(t_cf, 1)

            def counts_high(s):
                act.wait_ge(t_loop, s + 1)
                act.activation(chi[:, s, :], cf[:, s % 2, :], ACT.Copy).then_inc(t_ch, 1)

            for n in range(2 * NT + 1):
                if n < 2 * NT:
                    act.wait_ge(t_expo, n + 1)
                    act.activation(ta[:, n % 3, :], ta[:, n % 3, :], ACT.Exp).then_inc(t_exp, 1)
                if n >= 1:
                    hf, s = divmod(n - 1, NT)
                    act.wait_ge(t_p, n)
                    act.activation(ph[hf][:, s, :], tb[:, (n - 1) % 3, :], ACT.Copy).then_inc(t_ph, 1)
            for s in range(NT):
                counts_float(s)
                counts_high(s)
            act.wait_ge(t_dk, 1)
            act.activation(root[:, 1, NT:2 * NT], root[:, 0, NT:2 * NT], ACT.Sqrt).then_inc(t_root, 1)
            act.wait_ge(t_st, 3 * NT + 1)
            act.activation(root[:, 1, 0:NT], root[:, 0, 0:NT], ACT.Sqrt).then_inc(t_root, 1)

        @block.tensor
        def _(pe):
            def products(t, s, parts=(0, 1, 2)):
                dd = slice(t % HT * P, (t % HT + 1) * P)
                for n in parts:
                    a, b = ((ph, hh), (ph, hl), (pl, hh))[n]
                    for c, (lo, hi) in enumerate(((0, 384), (384, D + 2))):
                        mm = pe.matmul(ps[:, 2 * (t % 4) + c, 0:hi - lo], a[t // HT][:, s, dd], b[:, s, lo:hi],
                                       start=(s == 0 and n == 0), stop=(s == NT - 1 and n == 2))
                if s == NT - 1 and 2 in parts:
                    mm.then_inc(t_o, 1)

            for s in range(NT):
                pe.wait_ge(t_ph, s + 1)
                for t in range(HT):
                    products(t, s, (0, 1))
                pe.wait_ge(t_pl, s + 1)
                for t in range(HT):
                    products(t, s, (2,))
            for t in range(HT, NT):
                pe.wait_ge(t_x1, 2 * (t - 3))
                if t == NT - 1:
                    pe.wait_ge(t_x1, 2 * (HT + 1))
                    pe.matmul(ps[:, 0, 0:2 * NT], zeros[:], zeros[:, 0:2 * NT], start=True, stop=False,
                              skip_group_check=True)
                    for s in range(NT):
                        pe.wait_ge(t_cl, s + 1)
                        for part in (chi, clo):
                            for d in range(NT):
                                mm = pe.matmul(ps[:, 0, 2 * d:2 * d + 2], part[:, s, d * P:(d + 1) * P], ones[:],
                                               start=False, stop=True, skip_group_check=True)
                    mm.then_inc(t_deg, 1)
                for s in range(NT):
                    if t == HT:
                        pe.wait_ge(t_pl, NT + s + 1)
                    products(t, s)


def convolution(nc, env):
    Wg, bg, out = env["Wg"], env["bg"], env["out"]
    chi, clo, xt, mv, root, dinv, work = (env[k] for k in ("chi", "clo", "xt2", "mv2", "root2", "dinv", "work"))
    NT, N = chi.shape[1], chi.shape[2]
    D = Wg.shape[1]
    KT = D // P
    HALF = N // 2
    HT = NT // 2

    with ExitStack() as ctx:
        def sb(name, shape, dt):
            return ctx.enter_context(nc.sbuf_tensor(name, shape, dt))

        sem = Sems(nc, ctx)
        ps = ctx.enter_context(nc.psum_tensor("g_ps", [P, 8, 512], F32))
        xh = sb("x2_high", [P, NT, D], F16)
        xl = sb("x2_low", [P, NT, D], F16)
        xs = sb("x2_scaled", [P, 2, D], F32)
        wr = sb("wg_raw", [P, 2, D], F32)
        wh = sb("wg_high", [P, KT, D], F32R)
        wl = sb("wg_low", [P, KT, D], F32R)
        zt = work[:, 0:2, :]
        zh = sb("z3_high", [P, KT, N], F32R)
        zl = sb("z3_low", [P, KT, N], F32R)
        bgrow = sb("bg_row", [P, D], F32)

        g_w = [sem(f"wg_loaded{i}") for i in range(2)]
        g_b = sem("bg_loaded")
        g_xc = sem("x2_normed")
        g_xs = sem("x2_scaled_done")
        g_xh = sem("x2_high_done")
        g_xl = sem("x2_low_done")
        g_wh = sem("wg_high_done")
        g_wl = sem("wg_low_done")
        g_xb = sem("x1_biased")
        g_z = sem("z3_ready")
        g_zt = sem("z3_copied")
        g_zh = sem("z3_high_done")
        g_zl = sem("z3_low_done")
        g_o = sem("convolution_tile")
        g_y = sem("output_parts")
        g_out = sem("output_stored")
        block = ctx.enter_context(nc.Block())

        @block.sync
        def _(sp):
            for k in range(2):
                sp.dma_start(wr[:, k, :], Wg[k * P:(k + 1) * P, :]).then_inc(g_w[k], 16)
            sp.dma_start(bgrow[:], bg.partition_broadcast(P)).then_inc(g_b, 16)
            for k in range(2, KT):
                sp.wait_ge(g_wl, k - 1)
                sp.dma_start(wr[:, k % 2, :], Wg[k * P:(k + 1) * P, :]).then_inc(g_w[k % 2], 16)
            for t in range(NT):
                sp.wait_ge(g_y, 2 * t + 2)
                sp.dma_start(out[t * P:(t + 1) * P, :], xt[:, t, :]).then_inc(g_out, 16)
            sp.wait_ge(g_out, 16 * NT)

        @block.gpsimd
        def _(pool):
            pool.wait_ge(g_b, 16)
            for t in range(NT):
                pool.wait_ge(g_xc, t + 1)
                pool.tensor_tensor(xt[:, t, :], xt[:, t, :], bgrow[:], ALU.add).then_inc(g_xb, 1)

        @block.vector
        def _(dve):
            def x_scaled(s):
                if s >= 2:
                    dve.wait_ge(g_xl, s - 1)
                dve.tensor_scalar(xs[:, s % 2, :], xt[:, s, :], mv[:, s, 0:1], root[:, 5, s:s + 1], ALU.subtract,
                                  ALU.mult).then_inc(g_xc, 1)
                dve.wait_ge(g_xc, s + 1)
                dve.tensor_scalar(xs[:, s % 2, :], xs[:, s % 2, :], 0.0, dinv[:, 0, s:s + 1], ALU.max,
                                  ALU.mult).then_inc(g_xs, 1)

            def x_low(s):
                dve.wait_ge(g_xh, s + 1)
                dve.tensor_tensor(xl[:, s, :], xs[:, s % 2, :], xh[:, s, :], ALU.subtract).then_inc(g_xl, 1)

            def z_low(n):
                hf, k = divmod(n, KT)
                dve.wait_ge(g_zh, n + 1)
                dve.tensor_tensor(zl[:, k, hf * HALF:(hf + 1) * HALF], zt[:, n % 2, :],
                                  f32(zh[:, k, hf * HALF:(hf + 1) * HALF]), ALU.subtract).then_inc(g_zl, 1)

            for s in range(NT + 1):
                if s < NT:
                    x_scaled(s)
                if s >= 1:
                    x_low(s - 1)
            for k in range(KT):
                dve.wait_ge(g_wh, k + 1)
                dve.tensor_tensor(wl[:, k, :], wr[:, k % 2, :], f32(wh[:, k, :]), ALU.subtract).then_inc(g_wl, 1)
            for n in range(2 * KT):
                dve.wait_ge(g_z, n + 1)
                if n >= 2:
                    dve.wait_ge(g_zl, n - 1)
                dve.tensor_copy(zt[:, n % 2, :], ps[:, n if n < KT else 6 + n % 2, :]).then_inc(g_zt, 1)
                if n >= 1:
                    z_low(n - 1)
            z_low(2 * KT - 1)
            for t in range(NT):
                dve.wait_ge(g_o, t + 1)
                dve.wait_ge(g_xb, t + 1)
                for c in range(2):
                    part = xt[:, t, c * 384:(c + 1) * 384]
                    dve.scalar_tensor_tensor(out=part, in0=ps[:, 2 * (t % 3) + c, 0:384],
                                             scalar=dinv[:, 1, t:t + 1], in1=part, op0=ALU.mult,
                                             op1=ALU.add).then_inc(g_y, 1)

        @block.scalar
        def _(act):
            for s in range(NT):
                act.wait_ge(g_xs, s + 1)
                act.activation(xh[:, s, :], xs[:, s % 2, :], ACT.Copy).then_inc(g_xh, 1)
            for k in range(KT):
                act.wait_ge(g_w[k % 2], 16 * (k // 2 + 1))
                act.activation(wh[:, k, :], wr[:, k % 2, :], ACT.Copy).then_inc(g_wh, 1)
            for n in range(2 * KT):
                hf, k = divmod(n, KT)
                act.wait_ge(g_zt, n + 1)
                act.activation(zh[:, k, hf * HALF:(hf + 1) * HALF], zt[:, n % 2, :], ACT.Copy).then_inc(g_zh, 1)

        @block.tensor
        def _(pe):
            def products(hf, k, s, bank, parts=(0, 1, 2)):
                for i in parts:
                    a, b = ((xh, chi), (xh, clo), (xl, chi))[i]
                    mm = pe.matmul(ps[:, bank, :], a[:, s, k * P:(k + 1) * P], b[:, s, hf * HALF:(hf + 1) * HALF],
                                   start=(s == 0 and i == 0), stop=(s == NT - 1 and i == 2))
                if s == NT - 1 and 2 in parts:
                    mm.then_inc(g_z, 1)

            for s in range(NT):
                pe.wait_ge(g_xh, s + 1)
                for k in range(KT):
                    products(0, k, s, k, (0, 1))
                pe.wait_ge(g_xl, s + 1)
                for k in range(KT):
                    products(0, k, s, k, (2,))
            for k in range(KT):
                if k >= 2:
                    pe.wait_ge(g_zt, KT + k - 1)
                for s in range(NT):
                    products(1, k, s, 6 + (KT + k) % 2)
            pe.wait_ge(g_wl, KT)
            pe.wait_ge(g_zt, KT)
            for t in range(NT):
                if t >= 3:
                    pe.wait_ge(g_y, 2 * (t - 2))
                for k in range(KT):
                    if t in (0, HT):
                        pe.wait_ge(g_zl, (t // HT) * KT + k + 1)
                    for i, (a, b) in enumerate(((zh, wh), (zh, wl), (zl, wh))):
                        for c in range(2):
                            mm = pe.matmul(ps[:, 2 * (t % 3) + c, 0:384], a[:, k, t * P:(t + 1) * P],
                                           b[:, k, c * 384:(c + 1) * 384], start=(k == 0 and i == 0),
                                           stop=(k == KT - 1 and i == 2))
                mm.then_inc(g_o, 1)


def build(nc, x, src, dst, W1, a_s1, a_d1, b1, W2, a_s2, a_d2, b2, Wg, bg, out):
    N, D = x.shape
    H = a_s1.shape[0]
    NT, KT, HALF = N // P, D // P, N // 2
    env = dict(x=x, src=src, dst=dst, W1=W1, a_s1=a_s1, a_d1=a_d1, b1=b1, W2=W2, a_s2=a_s2, a_d2=a_d2,
               b2=b2, Wg=Wg, bg=bg, out=out)
    for name, shape, dt in (("logit_rows", (H, N), F32), ("mask_dram", (2, P, NT // 2, N), BF16),
                            ("ab_dram", (2, 2, HALF), F32), ("h2_dram", (P, 6, 512), F32)):
        env[name] = nc.dram_tensor(name, shape, dt).ap()

    def buffers(ctx, *wanted):
        for name, shape, dt in wanted:
            env[name] = ctx.enter_context(nc.sbuf_tensor(name, shape, dt))

    with ExitStack() as whole:
        buffers(whole, ("ct", [P, NT, N], U16), ("work", [P, 6, HALF], F32),
                ("a2_rows", [P, 2, D], F32))
        with ExitStack() as first:
            buffers(first, ("xh", [P, NT, D], F16), ("xl", [P, NT, D], F16), ("lc", [P, NT, 2 * H], F32),
                    ("lc02", [P, NT, 2 * H], F32), ("b1c", [P, H * KT], F32), ("ident", [P, P], F32))
            env["mask0"] = env["work"][:, 0:4, :].rearrange("p a b -> p (a b)").bitcast(BF16)\
                .rearrange("p (t n) -> p t n", n=N)
            startup(nc, env)
            heads(nc, env)
        buffers(whole, ("dinv", [P, 2, NT], F32), ("mv2", [P, NT, 2], F32), ("root2", [P, 6, 2 * NT], F32),
                ("xt2", [P, NT, D], F32), ("chi", [P, NT, N], F16))
        env["clo"] = env["ct"][:].bitcast(F16)
        with ExitStack() as second:
            buffers(second, ("ab2", [P, 2, NT], F32), ("small2", [P, 3, NT], F32), ("b2_row", [P, D], F32),
                    ("count_f", [P, 2, N], F32), ("lc2", [P, 3, NT], F32), ("ab_rows2", [P, 2, N], F32),
                    ("h2h", [P, NT, D + 2], F32R),
                    ("h2l", [P, NT, D + 2], F32R), ("ident2", [P, P], F32), ("ones2", [P, 2], F16),
                    ("zeros2", [P, P], F16))
            env["mask2"] = env["count_f"][:].rearrange("p a n -> p (a n)").bitcast(BF16)\
                .rearrange("p (t n) -> p t n", n=N)
            env["junk2"] = env["chi"][:, 0:2, :].bitcast(BF16)
            env["as_row2"] = env["a2_rows"][:].rearrange("p a d -> p (a d)")[:, 0:N]
            second_logits(nc, env)
            second_attention(nc, env)
        convolution(nc, env)


_INS = ['x', 'src', 'dst', 'L0_gnn_W1', 'L0_gnn_a_src1', 'L0_gnn_a_dst1', 'L0_gnn_b1', 'L0_gnn_W2',
        'L0_gnn_a_src2', 'L0_gnn_a_dst2', 'L0_gnn_b2', 'L1_gnn_W', 'L1_gnn_b']


def kernel(**inputs):
    import numpy as _np
    import concourse.bacc as _bacc
    from concourse import mybir as _mybir
    from concourse.bass_utils import run_bass_kernel_spmd as _run

    nc = _bacc.Bacc("TRN2", target_bir_lowering=False, num_devices=1)
    arrays, args = {}, []
    for name in _INS:
        a = _np.ascontiguousarray(inputs[name])
        arrays[f"in_{name}_dram"] = a
        args.append(nc.dram_tensor(f"in_{name}_dram", a.shape, _mybir.dt.from_np(a.dtype), kind="ExternalInput").ap())
    out = nc.dram_tensor("out_0_dram", arrays["in_x_dram"].shape, F32, kind="ExternalOutput").ap()
    build(nc, *args, out)
    r = _run(nc, [arrays], core_ids=[0])
    return r.results[0]["out_0_dram"]
```
